# Optimizing a Trainium2 kernel written in Bass

```python
import numpy as np
import jax
import jax.numpy as jnp

def _softmax(x, axis=-1):
    return jax.nn.softmax(x, axis=axis)

def _gelu(x):
    return jax.nn.gelu(x, approximate=True)

def _silu(x):
    return jax.nn.silu(x)

def _sigmoid(x):
    return jax.nn.sigmoid(x)

def _layernorm(x, axis=-1, eps=1e-05):
    m = jnp.mean(x, axis=axis, keepdims=True)
    v = jnp.var(x, axis=axis, keepdims=True)
    return (x - m) / jnp.sqrt(v + eps)

def _scatter_add(tgt, idx, src, axis=0):
    return tgt.at[idx].add(src)

def _segment_sum(src, seg, n):
    return jax.ops.segment_sum(src, seg, n)
kernel_name = 'mk_xattn_ffn_d2_seqx_r8_6976c0'

def setup_inputs(seed: int=0):
    np.random.seed(seed)
    _w = jnp.asarray

    def _rec_inputs():
        import jax
        import jax.numpy as jnp
        _rk = jax.random.key(seed)
        x = -9.806e-05 + 1 * jax.random.normal(jax.random.fold_in(_rk, 1), (32, 128, 128), jnp.float32)
        _lenS = 128 - jax.random.randint(jax.random.fold_in(_rk, 7), (32,), 0, max(1, 128 // 4) + 1, jnp.int32)
        _lenS2 = 120 - jax.random.randint(jax.random.fold_in(_rk, 8), (32,), 0, max(1, 120 // 4) + 1, jnp.int32)
        _ctx_1024P = jax.random.normal(jax.random.fold_in(_rk, 11), (32, 16, 128), jnp.float32)
        _ctx_1024c = jax.random.dirichlet(jax.random.fold_in(_rk, 511), 0.3 * jnp.ones((16,), jnp.float32), (32, 120))
        _ctx_1024t = jnp.einsum('bsk,bkd->bsd', _ctx_1024c, _ctx_1024P)
        _ctx_1024t = _ctx_1024t * jax.lax.rsqrt(jnp.mean(jnp.square(_ctx_1024t)) + 1e-12) * 0.953939
        ctx_1024 = -1.52775e-05 + 0.999936 * (_ctx_1024t + 0.3 * jax.random.normal(jax.random.fold_in(_rk, 611), (32, 120, 128), jnp.float32))
        _validS = jnp.arange(128)[None, :] < _lenS[:, None]
        _validS2 = jnp.arange(120)[None, :] < _lenS2[:, None]
        _causal = jnp.tril(jnp.ones((128, 128), dtype=bool))
        mask_Bx1xSxS2_ik0 = jnp.where(jnp.broadcast_to(_validS2[:, None, None, :], (32, 1, 128, 120)), 0, 1).astype(jnp.int32)
        return (x, ctx_1024, mask_Bx1xSxS2_ik0)
    x, ctx_1024, mask_Bx1xSxS2_ik0 = _rec_inputs()

    def _L0_xattn_setup():
        import jax, jax.numpy as jnp
        import numpy as np
        D = 128
        NUM_ITERS = 3
        EPS = 1e-06
        SCALE = D ** (-0.5)

        def rmsnorm(x, w, eps=EPS):
            return x * jax.lax.rsqrt(jnp.mean(x * x, axis=-1, keepdims=True) + eps) * w

        def gru_cell(x, h, wih, whh, bih, bhh):
            gx = x @ wih.T + bih
            gh = h @ whh.T + bhh
            xr, xz, xn = jnp.split(gx, 3, axis=-1)
            hr, hz, hn = jnp.split(gh, 3, axis=-1)
            r = jax.nn.sigmoid(xr + hr)
            z = jax.nn.sigmoid(xz + hz)
            n = jnp.tanh(xn + r * hn)
            return (1.0 - z) * n + z * h
        key = jax.random.key(seed)
        ks = jax.random.split(key, 8)
        B, K, M, d = (8, 64, 512, D)
        w_std = d ** (-0.5)
        return {'slots': jax.random.normal(ks[0], (B, K, d), jnp.float32), 'P': jax.random.normal(ks[1], (B, M, d), jnp.float32), 'Wq': jax.random.normal(ks[2], (d, d), jnp.float32) * w_std, 'Wk': jax.random.normal(ks[3], (d, d), jnp.float32) * w_std, 'Wv': jax.random.normal(ks[4], (d, d), jnp.float32) * w_std, 'gru_wih': jax.random.normal(ks[5], (3 * d, d), jnp.float32) * w_std, 'gru_whh': jax.random.normal(ks[6], (3 * d, d), jnp.float32) * w_std, 'gru_bih': jnp.zeros((3 * d,), jnp.float32), 'gru_bhh': jnp.zeros((3 * d,), jnp.float32), 'slot_norm_w': jnp.ones((d,), jnp.float32), 'input_norm_w': jnp.ones((d,), jnp.float32)}
    _L0_xattn_all = _L0_xattn_setup()
    _L0_xattn_in = {k: v for k, v in _L0_xattn_all.items() if k in ('Wq', 'Wk', 'Wv', 'gru_wih', 'gru_whh', 'gru_bih', 'gru_bhh', 'slot_norm_w', 'input_norm_w')}
    del _L0_xattn_all

    def _L0_ffn_setup():
        import jax, jax.numpy as jnp
        import numpy as np
        import math
        B, S, H, I, E = (4, 256, 128, 512, 8)
        TOP_K = 2
        CAPACITY_FACTOR = 1.25
        key = jax.random.key(seed)
        k1, k2, k3, k4, k5 = jax.random.split(key, 5)
        x = jax.random.normal(k1, (B, S, H), dtype=jnp.float32)
        W_router = jax.random.normal(k2, (E, H), dtype=jnp.float32) * (1.0 / math.sqrt(H))
        b_router = jnp.zeros((E,), dtype=jnp.float32)
        experts_inter = jax.random.normal(k3, (E, H, I), dtype=jnp.float32) * 0.02
        experts_out = jax.random.normal(k4, (E, I, H), dtype=jnp.float32) * 0.02
        return {'x': x, 'W_router': W_router, 'b_router': b_router, 'experts_inter': experts_inter, 'experts_out': experts_out}
    _L0_ffn_all = _L0_ffn_setup()
    _L0_ffn_in = {k: v for k, v in _L0_ffn_all.items() if k in ('W_router', 'b_router', 'experts_inter', 'experts_out')}
    del _L0_ffn_all

    def _L1_xattn_setup():
        import jax, jax.numpy as jnp
        import numpy as np
        B, S, D, H = (4, 256, 128, 16)
        DK = D // H

        def _split_heads(x):
            b, s, _ = x.shape
            return x.reshape(b, s, H, DK).transpose(0, 2, 1, 3)
        key = jax.random.key(seed)
        ks = jax.random.split(key, 8)
        Q = jax.random.normal(ks[0], (B, S, D), dtype=jnp.float32)
        K = jax.random.normal(ks[1], (B, S, D), dtype=jnp.float32)
        V = jax.random.normal(ks[2], (B, S, D), dtype=jnp.float32)
        mask = jnp.broadcast_to(jnp.tril(jnp.ones((S, S), dtype=jnp.int32))[None, None], (B, 1, S, S))
        scale = 1.0 / np.sqrt(D)
        W_Q = jax.random.normal(ks[3], (D, D), dtype=jnp.float32) * scale
        W_K = jax.random.normal(ks[4], (D, D), dtype=jnp.float32) * scale
        W_V = jax.random.normal(ks[5], (D, D), dtype=jnp.float32) * scale
        W_O = jax.random.normal(ks[6], (D, D), dtype=jnp.float32) * scale
        return {'Q': Q, 'K': K, 'V': V, 'mask': mask, 'W_Q': W_Q, 'W_K': W_K, 'W_V': W_V, 'W_O': W_O}
    _L1_xattn_all = _L1_xattn_setup()
    _L1_xattn_in = {k: v for k, v in _L1_xattn_all.items() if k in ('W_Q', 'W_K', 'W_V', 'W_O')}
    del _L1_xattn_all

    def _L1_ffn_setup():
        import jax, jax.numpy as jnp
        import numpy as np
        E = 8
        K = 2
        CAPACITY_FACTOR = 1.25
        key = jax.random.key(seed)
        ks = jax.random.split(key, 4)
        B, T, C, H = (8, 256, 128, 512)
        x = jax.random.normal(ks[0], (B, T, C), jnp.float32)
        Wr = jax.random.normal(ks[1], (C, E), jnp.float32) * 0.02
        br = jnp.zeros((E,), jnp.float32)
        W1 = jax.random.normal(ks[2], (E, C, H), jnp.float32) * 0.02
        b1 = jnp.zeros((E, H), jnp.float32)
        W2 = jax.random.normal(ks[3], (E, H, C), jnp.float32) * 0.02
        b2 = jnp.zeros((E, C), jnp.float32)
        return {'x': x, 'Wr': Wr, 'br': br, 'W1': W1, 'b1': b1, 'W2': W2, 'b2': b2}
    _L1_ffn_all = _L1_ffn_setup()
    _L1_ffn_in = {k: v for k, v in _L1_ffn_all.items() if k in ('Wr', 'br', 'W1', 'b1', 'W2', 'b2')}
    del _L1_ffn_all
    return {'x': x, 'ctx_1024': ctx_1024, 'mask_Bx1xSxS2_ik0': mask_Bx1xSxS2_ik0, 'L0_xattn_Wq': _L0_xattn_in['Wq'], 'L0_xattn_Wk': _L0_xattn_in['Wk'], 'L0_xattn_Wv': _L0_xattn_in['Wv'], 'L0_xattn_gru_wih': _L0_xattn_in['gru_wih'], 'L0_xattn_gru_whh': _L0_xattn_in['gru_whh'], 'L0_xattn_gru_bih': _L0_xattn_in['gru_bih'], 'L0_xattn_gru_bhh': _L0_xattn_in['gru_bhh'], 'L0_xattn_slot_norm_w': _L0_xattn_in['slot_norm_w'], 'L0_xattn_input_norm_w': _L0_xattn_in['input_norm_w'], 'L0_ffn_W_router': _L0_ffn_in['W_router'], 'L0_ffn_b_router': _L0_ffn_in['b_router'], 'L0_ffn_experts_inter': _L0_ffn_in['experts_inter'], 'L0_ffn_experts_out': _L0_ffn_in['experts_out'], 'L1_xattn_W_Q': _L1_xattn_in['W_Q'], 'L1_xattn_W_K': _L1_xattn_in['W_K'], 'L1_xattn_W_V': _L1_xattn_in['W_V'], 'L1_xattn_W_O': _L1_xattn_in['W_O'], 'L1_ffn_Wr': _L1_ffn_in['Wr'], 'L1_ffn_br': _L1_ffn_in['br'], 'L1_ffn_W1': _L1_ffn_in['W1'], 'L1_ffn_b1': _L1_ffn_in['b1'], 'L1_ffn_W2': _L1_ffn_in['W2'], 'L1_ffn_b2': _L1_ffn_in['b2']}

def reference(x, ctx_1024, mask_Bx1xSxS2_ik0, L0_xattn_Wq, L0_xattn_Wk, L0_xattn_Wv, L0_xattn_gru_wih, L0_xattn_gru_whh, L0_xattn_gru_bih, L0_xattn_gru_bhh, L0_xattn_slot_norm_w, L0_xattn_input_norm_w, L0_ffn_W_router, L0_ffn_b_router, L0_ffn_experts_inter, L0_ffn_experts_out, L1_xattn_W_Q, L1_xattn_W_K, L1_xattn_W_V, L1_xattn_W_O, L1_ffn_Wr, L1_ffn_br, L1_ffn_W1, L1_ffn_b1, L1_ffn_W2, L1_ffn_b2):
    import jax
    import jax.numpy as jnp

    def _L0_xattn_ref(slots, P, Wq, Wk, Wv, gru_wih, gru_whh, gru_bih, gru_bhh, slot_norm_w, input_norm_w):
        import jax, jax.numpy as jnp
        import numpy as np
        D = 128
        NUM_ITERS = 3
        EPS = 1e-06
        SCALE = D ** (-0.5)

        def rmsnorm(x, w, eps=EPS):
            return x * jax.lax.rsqrt(jnp.mean(x * x, axis=-1, keepdims=True) + eps) * w

        def gru_cell(x, h, wih, whh, bih, bhh):
            gx = x @ wih.T + bih
            gh = h @ whh.T + bhh
            xr, xz, xn = jnp.split(gx, 3, axis=-1)
            hr, hz, hn = jnp.split(gh, 3, axis=-1)
            r = jax.nn.sigmoid(xr + hr)
            z = jax.nn.sigmoid(xz + hz)
            n = jnp.tanh(xn + r * hn)
            return (1.0 - z) * n + z * h
        Pn = rmsnorm(P, input_norm_w)
        k_proj = Pn @ Wk.T
        v_proj = Pn @ Wv.T
        for _ in range(NUM_ITERS):
            sn = rmsnorm(slots, slot_norm_w)
            q_proj = sn @ Wq.T
            scores = jnp.einsum('bkd,bmd->bkm', q_proj, k_proj) * SCALE
            attn = jax.nn.softmax(scores, axis=-2)
            attn = attn / (jnp.sum(attn, axis=-1, keepdims=True) + EPS)
            updates = jnp.einsum('bkm,bmd->bkd', attn, v_proj)
            slots = gru_cell(updates, slots, gru_wih, gru_whh, gru_bih, gru_bhh)
        return slots

    def _L0_ffn_ref(x, W_router, b_router, experts_inter, experts_out):
        import jax, jax.numpy as jnp
        import numpy as np
        import math
        B, S, H, I, E = (4, 256, 128, 512, 8)
        TOP_K = 2
        CAPACITY_FACTOR = 1.25
        b, s, h = x.shape
        e = experts_inter.shape[0]
        T = b * s
        capacity = math.ceil(T / e * CAPACITY_FACTOR)
        x_flat = x.reshape(T, h)
        logits = x_flat @ W_router.T + b_router
        weights_flat = jax.nn.softmax(logits, axis=-1)
        top_vals, top_idx = jax.lax.top_k(weights_flat, TOP_K)
        topk_flat = jnp.zeros_like(weights_flat).at[jnp.arange(T)[:, None], top_idx].set(top_vals)
        routing_mask = (topk_flat > 0).astype(jnp.int32)
        order = jnp.argsort(-routing_mask, axis=0, stable=True)
        sorted_mask = jnp.take_along_axis(routing_mask, order, axis=0)
        sorted_mask = sorted_mask[:capacity]
        sorted_idx = order[:capacity]
        used_tokens = (sorted_idx * sorted_mask).reshape(-1)
        mask_flat = sorted_mask.reshape(-1).astype(x.dtype)
        inputs_tokens = x_flat[used_tokens] * mask_flat[:, None]
        inputs_tokens = inputs_tokens.reshape(capacity, e, h)
        inputs_weights = jnp.take_along_axis(topk_flat, sorted_idx, axis=0)
        hmid = jnp.einsum('ceh,ehi->cei', inputs_tokens, experts_inter)
        hmid = jax.nn.relu(hmid)
        out = jnp.einsum('cei,eih->ceh', hmid, experts_out)
        out = out * inputs_weights[:, :, None]
        combined = jnp.zeros((T, h), dtype=x.dtype).at[used_tokens].add(out.reshape(-1, h))
        return combined.reshape(b, s, h)

    def _L1_xattn_ref(Q, K, V, mask, W_Q, W_K, W_V, W_O):
        import jax, jax.numpy as jnp
        import numpy as np
        B, S, D, H = (4, 256, 128, 16)
        DK = D // H

        def _split_heads(x):
            b, s, _ = x.shape
            return x.reshape(b, s, H, DK).transpose(0, 2, 1, 3)
        q = _split_heads(Q @ W_Q.T)
        k = _split_heads(K @ W_K.T)
        v = _split_heads(V @ W_V.T)
        scores = jnp.einsum('bhqd,bhkd->bhqk', q, k) / jnp.sqrt(jnp.float32(DK))
        scores = jnp.where(mask == 0, -jnp.inf, scores)
        weights = jax.nn.softmax(scores, axis=-1)
        weights = jnp.nan_to_num(weights, nan=0.0)
        attn = jnp.einsum('bhqk,bhkd->bhqd', weights, v)
        attn = attn.transpose(0, 2, 1, 3).reshape(Q.shape[0], Q.shape[1], D)
        return attn @ W_O.T

    def _L1_ffn_ref(x, Wr, br, W1, b1, W2, b2):
        import jax, jax.numpy as jnp
        import numpy as np
        E = 8
        K = 2
        CAPACITY_FACTOR = 1.25
        B, T, C = x.shape
        cap = max(1, int(T / E * CAPACITY_FACTOR))
        probs = jax.nn.softmax(x @ Wr + br, axis=-1)
        topk_p, topk_e = jax.lax.top_k(probs, K)
        e_flat = topk_e.reshape(B, T * K)
        p_flat = topk_p.reshape(B, T * K)
        oh = jax.nn.one_hot(e_flat, E, dtype=jnp.int32)
        pos_all = jnp.cumsum(oh, axis=1) - oh
        pos = jnp.take_along_axis(pos_all, e_flat[:, :, None], axis=2)[:, :, 0]
        keep = pos < cap
        b_idx = jnp.arange(B)[:, None]
        flat_idx = (e_flat * B + b_idx) * cap + jnp.minimum(pos, cap - 1)
        x_rep = jnp.broadcast_to(x[:, :, None, :], (B, T, K, C)).reshape(B, T * K, C)
        buf = jnp.zeros((E * B * cap, C), x.dtype).at[flat_idx.reshape(-1)].add((x_rep * keep[:, :, None].astype(x.dtype)).reshape(-1, C))
        buf = buf.reshape(E, B * cap, C)
        h = jax.nn.relu(jnp.einsum('enc,ech->enh', buf, W1) + b1[:, None, :])
        y = jnp.einsum('enh,ehc->enc', h, W2) + b2[:, None, :]
        y_tok = y.reshape(E * B * cap, C)[flat_idx.reshape(-1)].reshape(B, T * K, C)
        y_tok = y_tok * (p_flat * keep.astype(x.dtype))[:, :, None]
        return y_tok.reshape(B, T, K, C).sum(axis=2)
    x = x + _L0_xattn_ref(_layernorm(x, axis=-1), ctx_1024, L0_xattn_Wq, L0_xattn_Wk, L0_xattn_Wv, L0_xattn_gru_wih, L0_xattn_gru_whh, L0_xattn_gru_bih, L0_xattn_gru_bhh, L0_xattn_slot_norm_w, L0_xattn_input_norm_w)
    x = x + _L0_ffn_ref(_layernorm(x, axis=-1), L0_ffn_W_router, L0_ffn_b_router, L0_ffn_experts_inter, L0_ffn_experts_out)
    x = x + _L1_xattn_ref(_layernorm(x, axis=-1), ctx_1024, ctx_1024, mask_Bx1xSxS2_ik0, L1_xattn_W_Q, L1_xattn_W_K, L1_xattn_W_V, L1_xattn_W_O)
    x = x + _L1_ffn_ref(_layernorm(x, axis=-1), L1_ffn_Wr, L1_ffn_br, L1_ffn_W1, L1_ffn_b1, L1_ffn_W2, L1_ffn_b2)
    return x

_drawn_inputs = setup_inputs


def setup_inputs(seed=0):
    import zlib

    import numpy as np

    out = dict(_drawn_inputs(seed))
    spreads = {'L0_xattn_gru_bih': (0.0, 0.1),
     'L0_xattn_gru_bhh': (0.0, 0.1),
     'L0_xattn_slot_norm_w': (1.0, 0.6),
     'L0_xattn_input_norm_w': (1.0, 0.2),
     'L0_ffn_b_router': (0.0, 0.8),
     'L1_ffn_br': (0.0, 0.694),
     'L1_ffn_b1': (0.0, 0.8),
     'L1_ffn_b2': (0.0, 0.669)}
    factors = {'L0_ffn_W_router': 3.361,
     'L0_ffn_experts_inter': 3.635,
     'L0_ffn_experts_out': 3.056,
     'L1_ffn_Wr': 4.164,
     'L1_ffn_W1': 7.956,
     'L1_ffn_W2': 6.175}
    for name, (base, spread) in spreads.items():
        noise = np.random.default_rng([zlib.crc32(name.encode()), seed]).standard_normal(out[name].shape)
        drawn = base * np.exp(spread * noise) if base else spread * noise
        out[name] = jnp.asarray(drawn.astype(out[name].dtype))
    for name, factor in factors.items():
        out[name] = (out[name] * factor).astype(out[name].dtype)
    return out
```

```python
from contextlib import ExitStack

import concourse.bass as bass
from concourse import mybir

F32 = mybir.dt.float32
BF16 = mybir.dt.bfloat16
I32 = mybir.dt.int32
ALU = mybir.AluOpType
ACT = mybir.ActivationFunctionType
AX = mybir.AxisListType.X

B, S, D = 32, 128, 128
M = 120
G = 4
SLOTS = 2
NG = B // G // SLOTS
ITERS = 3
E, HID = 8, 512
HC = HID // 128
CAP0 = 640
CAP1 = 20
ROWS = E * CAP0
CT = CAP0 // 128
H, DK = 16, 8
HG = 4
BIG = 1.0e30
EPS_LN, EPS_RMS = 1e-5, 1e-6
STOP = 9


def build(nc, t, out):
    ctx = ExitStack()
    with ctx:
        def sb(name, shape, dt=F32, of=ctx):
            return of.enter_context(nc.sbuf_tensor(name, shape, dt))

        def sem(name):
            return ctx.enter_context(nc.semaphore(name))

        def sems(names):
            return {n: sem("s_" + n) for n in names.split()}

        rows_d = [nc.dram_tensor(f"rows{l}", [ROWS, D], F32, kind="Internal").ap() for l in range(2)]
        res_d = [nc.dram_tensor(f"res{l}", [ROWS, D], F32, kind="Internal").ap() for l in range(2)]

        bank = [ctx.enter_context(nc.psum_tensor(f"bank{i}", [128, 512], F32)) for i in range(8)]
        bank4 = None

        ident = sb("ident", [128, 128])
        ident_bf = sb("ident_bf", [128, 128], BF16)
        ones_bf = sb("ones_bf", [128, 128], BF16)
        before = sb("before", [128, 128], BF16)
        ones_row = sb("ones_row", [1, 128])
        head_sel = sb("head_sel", [48, H, M], BF16)
        band = sb("band", [128, HG])
        iota_e = sb("iota_e", [128, E])
        minus_half = sb("minus_half", [128, G])
        eps_ln = sb("eps_ln", [128, G])
        eps_rms = sb("eps_rms", [128, G])
        raw = sb("raw", [128, 11, D])
        wqk = sb("wqk", [128, 2, D])
        small = sb("small", [E, D])
        b1raw = sb("b1raw", [32, 128])
        wT = sb("wT", [128, 11, D])
        mT = sb("mT", [128, D])
        wr = [sb(f"wr{l}", [128, E]) for l in range(2)]
        br = [sb(f"br{l}", [128, E]) for l in range(2)]
        b1T = sb("b1T", [128, E * HC])
        b2r = sb("b2r", [1, E * D])
        win = sb("win", [128, 1])
        wslot = sb("wslot", [128, 1])
        gbi = sb("gbi", [128, 3])
        gbh = sb("gbh", [128, 3])
        gb2 = sb("gb2", [128, 2])

        xs = sb("xs", [128, B, D])
        hs = sb("hs", [128, B, D])
        yk = sb("yk", [128, B * 2, D])
        lg = sb("lg", [128, B, E])
        gate = sb("gate", [128, 2, B])
        slot_i = sb("slot_i", [128, 2, B], I32)

        def per(name, shape, dt=F32, of=ctx):
            return [sb(f"{name}{s}", shape, dt, of) for s in range(SLOTS)]

        gt = sb("gt", [128, B, E])
        ge = sb("ge", [128, B, E])
        gw = sb("gw", [128, B, E])
        gm = [sb(f"gm{k}", [128, E, B]) for k in range(2)]
        gmb = sb("gmb", [128, E, B], BF16)
        gv = sb("gv", [128, E, B])
        gp = sb("gp", [128, E, B])
        gx = sb("gx", [128, B])
        g1 = sb("g1", [128, B])
        eight = sb("eight", [128, B, E])
        chain = sb("chain", [128, E, B])
        base = [sb(f"base{l}", [128, E, B]) for l in range(2)]
        base_i = sb("base_i", [128, E, B], I32)
        sl = [sb(f"sl{k}", [128, B]) for k in range(2)]

        xe = per("xe", [128, CT, D])
        xeT = per("xeT", [128, CAP0])
        w1 = per("w1", [128, HID])
        w2 = per("w2", [128, HC, D])
        hT = per("hT", [128, HC, CAP0])

        va = per("va", [M, H, DK + 1])
        early = ExitStack()
        x_s = per("x_s", [128, G, D], of=early)
        c_s = per("c_s", [M, G, D], of=early)
        cT = per("cT", [128, G, M], of=early)
        g_s = per("g_s", [128, G, M], of=early)
        v_s = per("v_s", [M, G, D + 1], of=early)
        vr_s = per("vr_s", [M, G, D + 1], of=early)
        st = per("st", [128, G * 6], of=early)
        mv = per("mv", [128, G, 2], of=early)
        pw = per("pw", [128, G], of=early)
        rs = per("rs", [128, G], of=early)
        pwc = per("pwc", [128, G], of=early)
        rc = per("rc", [128, G], of=early)
        mx = per("mx", [M, G], of=early)
        nb = per("nb", [M, G], of=early)
        sm = per("sm", [M, G], of=early)
        rm = per("rm", [M, G], of=early)
        cs = per("cs", [128, G], of=early)
        ci = per("ci", [128, G], of=early)
        sT = per("sT", [128, G * S], of=early)
        tok = per("tok", [128, G, D], of=early)
        snT = per("snT", [128, G * S], of=early)
        ex = per("ex", [M, G, S], of=early)
        upT = per("upT", [128, G * S], of=early)
        tr = per("tr", [128, G * S], of=early)
        tz = per("tz", [128, G * S], of=early)
        qn = per("qn", [128, G * S], of=early)
        nn = per("nn", [128, G * S], of=early)
        uu = per("uu", [128, G * S], of=early)

        early.close()

        ca = per("ca", [M, D])
        mk = per("mk", [128, M], I32)
        mb = per("mb", [128, M], BF16)
        mbT = per("mbT", [M, S], BF16)
        caT = per("caT", [128, M])
        kb = per("kb", [128, HG, M])
        xa = per("xa", [128, D])
        sta = per("sta", [128, 6])
        mva = per("mva", [128, 2])
        pwa = per("pwa", [128, 1])
        rsa = per("rsa", [128, 1])
        ha = per("ha", [128, D])
        haT = per("haT", [128, S])
        qT = per("qT", [128, S])
        mxa = per("mxa", [128, H])
        nm = per("nm", [128, H])
        nr = per("nr", [128, H])
        nmp = per("nmp", [128, 3, H], BF16)
        nmT = per("nmT", [3 * H, S], BF16)
        pT = per("pT", [M, H * S])
        den = per("den", [128, H])
        rden = per("rden", [128, H])
        oa = per("oa", [128, D])
        oT = per("oT", [128, S])

        w_in = sem("w_in")
        k_pool = sem("k_pool")
        setup_T = sem("setup_T")
        setup_ev = sem("setup_ev")
        setup_m = sem("setup_m")
        setup_done = sem("setup_done")
        zeroed = sem("zeroed")
        stored = sem("stored")
        F = {k: sem(f"f_{k}") for k in
             ("d dd ex pos posr tot slot scat w0 w1 in0 in1 T Tev h hevD hevA y yevD yevA out gath").split()}
        route_steps = [0]
        C = {k: sem("c_" + k) for k in
             ("in0 in1 x1 x2 st mv pw rr ln T Tev q qev cT cTev k kev v vev mb mbT mbTev s mx nm hi r1 mid lo "
              "nT nTev p ex pv den rd o oT oTev w x3 st2 mv2 pw2 rr2 ln2 keep T2 T2ev lg lgev").split()}
        Z = {k: sem("z_" + k) for k in "a b".split()}
        A = sems("ctx_in0 x_in0 ctx_in1 x_in1 ctx_ms ctx_rr ctx_T ctx_Tev ctx_G ctx_Gev ctx_V ctx_Vev "
                 "x_st x_mv x_rr x_ln x_T x_Tev "
                 "i_tok i_ms i_pw i_rr i_sn i_snT i_snTev i_sc i_mx i_nb i_ex i_rm i_vr i_u i_cs i_ci i_ut "
                 "i_uT i_uTev i_hn i_r i_z i_xn i_tr i_tz i_r2 i_q i_q2 i_n i_z2 i_d i_v i_s "
                 "f_T f_x f_st f_mv f_pw f_rr f_ln f_T2 f_T2ev f_lg f_lgev f_keep x_pw ctx_pw")

        K_POOL = 31
        block = ctx.enter_context(nc.Block())
        W_V, W_IH, W_HH, W_QQ, W_KK, W_VV, W_OO = 0, 1, 4, 7, 8, 9, 10
        x_v = t["x"].rearrange("(g b) s d -> g s b d", b=G)
        c_v = t["ctx_1024"].rearrange("(g b) m d -> g m b d", b=G)
        out_v = out.rearrange("b s d -> s b d")
        base_v = [r.rearrange("(p r) d -> p (r d)", p=128) for r in rows_d]
        res_v = [r.rearrange("(e c p) d -> e p c d", e=E, p=128) for r in res_d]
        rows_v = [r.rearrange("(e c p) d -> e p c d", e=E, p=128) for r in rows_d]
        w1_v = (t["L0_ffn_experts_inter"], t["L1_ffn_W1"])
        w2_v = [w.rearrange("e (c p) d -> e p c d", p=128) for w in (t["L0_ffn_experts_out"], t["L1_ffn_W2"])]
        ye = yk[:, 0:E * CT, :]
        mask_v = t["mask_Bx1xSxS2_ik0"].rearrange("b a s m -> (b a) s m")
        NWD = 19

        def occ(i, it, s, per_turn=ITERS):
            return i * (per_turn * SLOTS) + it * SLOTS + s + 1

        def occ1(i, s):
            return i * SLOTS + s + 1

        @block.sync
        def _(sp):
            for k, name in enumerate(("L0_xattn_Wv", "L1_xattn_W_Q", "L1_xattn_W_K", "L1_xattn_W_V", "L1_xattn_W_O")):
                at = (W_V, W_QQ, W_KK, W_VV, W_OO)[k]
                sp.dma_start(raw[:, at, :], t[name]).then_inc(w_in, 16)
            sp.dma_start(raw[:, W_IH:W_IH + 3, :], t["L0_xattn_gru_wih"].rearrange("(c p) d -> p c d", p=128)).then_inc(w_in, 16)
            sp.dma_start(raw[:, W_HH:W_HH + 3, :], t["L0_xattn_gru_whh"].rearrange("(c p) d -> p c d", p=128)).then_inc(w_in, 16)
            sp.dma_start(wqk[:, 0, :], t["L0_xattn_Wq"]).then_inc(w_in, 16)
            sp.dma_start(wqk[:, 1, :], t["L0_xattn_Wk"]).then_inc(w_in, 16)
            sp.dma_start(small[:, :], t["L0_ffn_W_router"]).then_inc(w_in, 16)
            sp.dma_start(wr[1][:, :], t["L1_ffn_Wr"]).then_inc(w_in, 16)
            sp.dma_start(br[0][:, :], t["L0_ffn_b_router"].partition_broadcast(128)).then_inc(w_in, 16)
            sp.dma_start(br[1][:, :], t["L1_ffn_br"].partition_broadcast(128)).then_inc(w_in, 16)
            sp.dma_start(b1raw[:, :], t["L1_ffn_b1"].rearrange("e (c p) -> (e c) p", p=128)).then_inc(w_in, 16)
            sp.dma_start(b2r[:, :], t["L1_ffn_b2"].rearrange("(a e) d -> a (e d)", a=1)).then_inc(w_in, 16)
            with nc.allow_non_contiguous_dma(reason="columns of 128 and 384 floats"):
                sp.dma_start(win[:, :], t["L0_xattn_input_norm_w"].rearrange("(p a) -> p a", a=1)).then_inc(w_in, 16)
                sp.dma_start(wslot[:, :], t["L0_xattn_slot_norm_w"].rearrange("(p a) -> p a", a=1)).then_inc(w_in, 16)
                sp.dma_start(gbi[:, :], t["L0_xattn_gru_bih"].rearrange("(c p) -> p c", p=128)).then_inc(w_in, 16)
                sp.dma_start(gbh[:, :], t["L0_xattn_gru_bhh"].rearrange("(c p) -> p c", p=128)).then_inc(w_in, 16)
            for s in range(SLOTS):
                sp.dma_start(c_s[s][:, :, :], c_v[s]).then_inc(A[f"ctx_in{s}"], 16)
                sp.dma_start(x_s[s][:, :, :], x_v[s]).then_inc(A[f"x_in{s}"], 16)
            with sp.Fori(1, NG) as i:
                for s in range(SLOTS):
                    sp.wait_ge(A["f_lgev"], occ1(i - 1, s))
                    sp.wait_ge(A["f_keep"], occ1(i - 1, s))
                    sp.dma_start(c_s[s][:, :, :], c_v[bass.ds(i * SLOTS + s, 1)].rearrange("a m b d -> m (a b) d")).then_inc(A[f"ctx_in{s}"], 16)
                    sp.dma_start(x_s[s][:, :, :], x_v[bass.ds(i * SLOTS + s, 1)].rearrange("a m b d -> m (a b) d")).then_inc(A[f"x_in{s}"], 16)

            def experts_sp(l):
                f = F

                def weights(i, s):
                    sp.dma_start(w1[s][:, :], w1_v[l][bass.ds(i * SLOTS + s, 1)].rearrange("a p n -> p (a n)")).then_inc(f[f"w{s}"], 16)
                    sp.dma_start(w2[s][:, :, :], w2_v[l][bass.ds(i * SLOTS + s, 1)].rearrange("a p c d -> p (a c) d")).then_inc(f[f"w{s}"], 16)

                def rows(i, s):
                    sp.dma_start(xe[s][:, :, :], rows_v[l][bass.ds(i * SLOTS + s, 1)].rearrange("a p c d -> p (a c) d")).then_inc(f[f"in{s}"], 16)

                def store(i, s):
                    sp.wait_ge(f["yevA"], occ1(i, s) + l * E)
                    sp.wait_ge(f["yevD"], occ1(i, s) + l * E)
                    sp.dma_start(res_v[l][bass.ds(i * SLOTS + s, 1)].rearrange("a p c d -> p (a c) d"),
                                 ye[:, bass.ds((i * SLOTS + s) * CT, CT), :]).then_inc(f["out"], 16)
                for s in range(SLOTS):
                    weights(0, s)
                sp.wait_ge(f["scat"], 16 * 2 * B * (l + 1))
                for s in range(SLOTS):
                    rows(0, s)
                with sp.Fori(1, E // SLOTS) as i:
                    for s in range(SLOTS):
                        store(i - 1, s)
                        weights(i, s)
                        rows(i, s)
                for s in range(SLOTS):
                    store(E // SLOTS - 1, s)

            sp.wait_ge(Z["a"], 1)
            for l in range(2):
                for j in range(ROWS // 128 // CT):
                    sp.dma_start(base_v[l][:, j * CT * D:(j + 1) * CT * D], yk[:, 0:CT, :].rearrange("p c d -> p (c d)")).then_inc(zeroed, 16)
            experts_sp(0)
            for s in range(SLOTS):
                sp.dma_start(ca[s][:, :], t["ctx_1024"][s]).then_inc(C[f"in{s}"], 16)
                sp.dma_start(mk[s][:, :], mask_v[s]).then_inc(C[f"in{s}"], 16)
            with sp.Fori(1, B // SLOTS) as i:
                for s in range(SLOTS):
                    sp.wait_ge(C["cT"], occ1(i - 1, s))
                    sp.wait_ge(C["mb"], occ1(i - 1, s))
                    sp.dma_start(ca[s][:, :], t["ctx_1024"][bass.ds(i * SLOTS + s, 1)].rearrange("a m d -> m (a d)")).then_inc(C[f"in{s}"], 16)
                    sp.dma_start(mk[s][:, :], mask_v[bass.ds(i * SLOTS + s, 1)].rearrange("a q m -> q (a m)")).then_inc(C[f"in{s}"], 16)
            experts_sp(1)
            sp.wait_ge(Z["b"], B // G)
            sp.dma_start(out_v, xs[:, :, :]).then_inc(stored, 16)
            sp.wait_ge(stored, 16)

        @block.gpsimd
        def _(pool):
            pool.memset(ident[:, :], 0.0).then_inc(k_pool, 1)
            pool.memset(ones_bf[:, :], 1.0).then_inc(k_pool, 1)
            pool.memset(minus_half[:, :], -0.5).then_inc(k_pool, 1)
            pool.memset(eps_ln[:, :], EPS_LN).then_inc(k_pool, 1)
            pool.memset(eps_rms[:, :], EPS_RMS).then_inc(k_pool, 1)
            pool.memset(ones_row[:, :], 1.0).then_inc(k_pool, 1)
            for s in range(SLOTS):
                pool.memset(v_s[s][:, :, D:D + 1], 1.0).then_inc(k_pool, 1)
            pool.wait_ge(k_pool, 8)
            pool.affine_select(out=ident[:, :], in_=ident[:, :], compare_op=ALU.not_equal, fill=1.0,
                               base=0, pattern=[[-1, 128]], channel_multiplier=1).then_inc(k_pool, 1)
            pool.affine_select(out=before[:, :], in_=ones_bf[:, :], compare_op=ALU.is_gt, fill=0.0,
                               base=0, pattern=[[1, 128]], channel_multiplier=-1).then_inc(k_pool, 1)
            pool.iota(base_i[:, :, :], pattern=[[CAP0, E], [0, B]], base=0, channel_multiplier=0).then_inc(k_pool, 1)
            pool.wait_ge(k_pool, 11)
            pool.tensor_copy(base[0][:, :, :], base_i[:, :, :]).then_inc(k_pool, 1)
            pool.wait_ge(k_pool, 12)
            pool.iota(base_i[:, :, :], pattern=[[CAP0, E], [CAP1, B]], base=0, channel_multiplier=0).then_inc(k_pool, 1)
            pool.wait_ge(k_pool, 13)
            pool.tensor_copy(base[1][:, :, :], base_i[:, :, :]).then_inc(k_pool, 1)
            pool.memset(chain[:, :, :], 1.0).then_inc(k_pool, 1)
            pool.wait_ge(k_pool, 15)
            pool.memset(chain[:, :, 0:1], 0.0).then_inc(k_pool, 1)
            for e in range(E):
                pool.memset(eight[:, :, e:e + 1], float(E - e)).then_inc(k_pool, 1)
            for s in range(SLOTS):
                pool.memset(va[s][:, :, DK:DK + 1], 1.0).then_inc(k_pool, 1)
            pool.memset(head_sel[:, :, :], 0.0).then_inc(k_pool, 1)
            for a in range(3):
                pool.wait_ge(k_pool, 27 + a)
                pool.affine_select(out=head_sel[:, :, :], in_=head_sel[:, :, :], compare_op=ALU.not_equal, fill=1.0,
                                   base=-H * a, pattern=[[-1, H], [0, M]], channel_multiplier=1).then_inc(k_pool, 1)
            pool.memset(yk[:, :, :], 0.0).then_inc(Z["a"], 1)
            pool.tensor_copy(ident_bf[:, :], ident[:, :]).then_inc(k_pool, 1)

            def power(src, dst, rows, n, s_src, s_mid, mid, s_dst, eps):
                pool.wait_ge(A[s_src], n)
                pool.tensor_tensor(mid[0:rows, :], src, eps[0:rows, :], ALU.add).then_inc(A[s_mid], 1)
                pool.wait_ge(A[s_mid], n)
                pool.tensor_tensor(dst[0:rows, :], mid[0:rows, :], minus_half[0:rows, :], ALU.pow).then_inc(A[s_dst], 1)

            with pool.Fori(0, NG) as i:
                for s in range(SLOTS):
                    n = occ1(i, s)
                    power(pwc[s][0:M, :], rc[s], M, n, "ctx_ms", "ctx_pw", pwc[s], "ctx_rr", eps_rms)
                for s in range(SLOTS):
                    n = occ1(i, s)
                    power(mv[s][:, :, 1], rs[s], 128, n, "x_mv", "x_pw", pw[s], "x_rr", eps_ln)
                for it in range(ITERS):
                    for s in range(SLOTS):
                        n = occ(i, it, s)
                        power(cs[s][:, :], rs[s], 128, n, "i_ms", "i_pw", pw[s], "i_rr", eps_rms)
                    for s in range(SLOTS):
                        n = occ(i, it, s)
                        pool.wait_ge(k_pool, K_POOL)
                        pool.wait_ge(A["i_tz"], n)
                        pool.tensor_scalar(tz[s][:, :], tz[s][:, :], 0.5, 0.5, ALU.mult, ALU.add).then_inc(A["i_z2"], 1)
                        pool.wait_ge(A["i_n"], n)
                        pool.tensor_tensor(uu[s][:, :], sT[s][:, :], nn[s][:, :], ALU.subtract).then_inc(A["i_d"], 1)
                        pool.wait_ge(A["i_z2"], n)
                        pool.wait_ge(A["i_d"], n)
                        pool.tensor_tensor(uu[s][:, :], uu[s][:, :], tz[s][:, :], ALU.mult).then_inc(A["i_v"], 1)
                        pool.wait_ge(A["i_v"], n)
                        pool.wait_ge(A["i_z"], n)
                        pool.tensor_tensor(sT[s][:, :], uu[s][:, :], nn[s][:, :], ALU.add).then_inc(A["i_s"], 1)
                for s in range(SLOTS):
                    n = occ1(i, s)
                    power(mv[s][:, :, 1], rs[s], 128, n, "f_mv", "f_pw", pw[s], "f_rr", eps_ln)
                for s in range(SLOTS):
                    n = occ1(i, s)
                    pool.wait_ge(A["f_x"], n)
                    pool.tensor_copy(xs[:, bass.ds((i * SLOTS + s) * G, G), :], x_s[s][:, :, :])
                    pool.wait_ge(A["f_ln"], n)
                    pool.tensor_copy(hs[:, bass.ds((i * SLOTS + s) * G, G), :], tok[s][:, :, :]).then_inc(A["f_keep"], 1)

            def dispatch(l):
                f = F
                pool.wait_ge(f["slot"], l + 1)
                if l:
                    pool.wait_ge(C["keep"], B)
                else:
                    pool.wait_ge(A["f_keep"], B // G)
                pool.wait_ge(zeroed, 16 * 2 * (ROWS // 128 // CT))
                for b in range(B):
                    for k in range(2):
                        pool.indirect_dma_start(out=rows_d[l], out_offset=bass.IndirectOffsetOnAxis(ap=slot_i[:, k, b:b + 1], axis=0),
                                                in_=hs[:, b, :], in_offset=None, bounds_check=ROWS - 1,
                                                oob_is_err=False).then_inc(f["scat"], 16)

            def collect(l):
                f = F
                pool.wait_ge(f["out"], 16 * E * (l + 1))
                for b in range(B):
                    for k in range(2):
                        pool.indirect_dma_start(out=yk[:, 2 * b + k, :], out_offset=None, in_=res_d[l],
                                                in_offset=bass.IndirectOffsetOnAxis(ap=slot_i[:, k, b:b + 1], axis=0),
                                                bounds_check=ROWS - 1, oob_is_err=False).then_inc(f["gath"], 16)

            def power1(s, n, s_src, s_mid, s_dst):
                pool.wait_ge(C[s_src], n)
                pool.tensor_tensor(pwa[s][:, :], mva[s][:, 1:2], eps_ln[:, 0:1], ALU.add).then_inc(C[s_mid], 1)
                pool.wait_ge(C[s_mid], n)
                pool.tensor_tensor(rsa[s][:, :], pwa[s][:, :], minus_half[:, 0:1], ALU.pow).then_inc(C[s_dst], 1)

            dispatch(0)
            collect(0)
            with pool.Fori(0, B // SLOTS) as i:
                for s in range(SLOTS):
                    power1(s, occ1(i, s), "mv", "pw", "rr")
                for s in range(SLOTS):
                    power1(s, occ1(i, s), "mv2", "pw2", "rr2")
                for s in range(SLOTS):
                    n = occ1(i, s)
                    pool.wait_ge(C["ln2"], n)
                    pool.tensor_copy(xs[:, bass.ds(i * SLOTS + s, 1), :], xa[s][:, :].unsqueeze(1))
                    pool.tensor_copy(hs[:, bass.ds(i * SLOTS + s, 1), :], ha[s][:, :].unsqueeze(1)).then_inc(C["keep"], 1)
            dispatch(1)
            collect(1)

        @block.scalar
        def _(act):
            act.wait_ge(w_in, 16 * NWD)
            act.wait_ge(setup_T, 1)
            for j in range(4):
                act.activation(wT[:, j, :], bank[0][:, j * D:(j + 1) * D], ACT.Identity,
                               **({"scale": win[:, 0:1]} if j == 0 else {}))
            for j in range(4):
                at = 4 + j
                act.activation(wT[:, at, :], bank[1][:, j * D:(j + 1) * D], ACT.Identity,
                               **({"scale": float(DK) ** -0.5} if at == W_QQ else {}))
            act.activation(wT[:, 8:11, :], bank[2][:, 0:3 * D].rearrange("p (j d) -> p j d", j=3), ACT.Identity)
            act.activation(wr[0][:, :], bank[3][:, 0:E], ACT.Identity)
            act.activation(b1T[:, :], bank[3][:, 32:64], ACT.Identity)
            act.activation(mT[:, :], bank[3][:, 128:256], ACT.Identity, scale=win[:, 0:1]).then_inc(setup_ev, 1)

            with act.Fori(0, NG) as i:
                for s in range(SLOTS):
                    n = occ1(i, s)
                    act.wait_ge(A[f"ctx_in{s}"], 16 * (i + 1))
                    for b in range(G):
                        last = act.activation(uu[s][0:M, b * D:(b + 1) * D], c_s[s][:, b, :], ACT.Square, scale=float(D) ** -0.5,
                                              accum_out=pwc[s][0:M, b:b + 1])
                    last.then_inc(A["ctx_ms"], 1)
                    act.wait_ge(A["ctx_T"], n)
                    act.activation(cT[s][:, :, :], bank[4 * s + 3][:, 0:G * M].rearrange("p (b m) -> p b m", b=G),
                                   ACT.Identity).then_inc(A["ctx_Tev"], 1)
                for s in range(SLOTS):
                    n = occ1(i, s)
                    act.wait_ge(A["x_T"], n)
                    act.activation(sT[s][:, :], bank[4 * s][:, :], ACT.Identity).then_inc(A["x_Tev"], 1)
                for it in range(ITERS):
                    for s in range(SLOTS):
                        n = occ(i, it, s)
                        act.wait_ge(A["i_tok"], n)
                        for b in range(G):
                            last = act.activation(uu[s][:, b * D:(b + 1) * D], bank[4 * s][:, b * D:(b + 1) * D], ACT.Square,
                                                  scale=float(D) ** -0.5, accum_out=cs[s][:, b:b + 1])
                        last.then_inc(A["i_ms"], 1)
                    for s in range(SLOTS):
                        n = occ(i, it, s)
                        act.wait_ge(A["i_snT"], n)
                        act.activation(snT[s][:, :], bank[4 * s][:, :], ACT.Identity).then_inc(A["i_snTev"], 1)
                    for s in range(SLOTS):
                        n = occ(i, it, s)
                        act.wait_ge(A["i_nb"], n)
                        for b in range(G):
                            last = act.activation(ex[s][:, b, :], bank[4 * s + 1][0:M, b * S:(b + 1) * S], ACT.Exp,
                                                  bias=nb[s][:, b:b + 1], scale=rc[s][0:M, b:b + 1],
                                                  accum_out=sm[s][:, b:b + 1])
                        last.then_inc(A["i_ex"], 1)
                    for s in range(SLOTS):
                        n = occ(i, it, s)
                        act.wait_ge(A["i_uT"], n)
                        act.activation(upT[s][:, :], bank[4 * s + 2][:, :], ACT.Identity).then_inc(A["i_uTev"], 1)
                    for s in range(SLOTS):
                        n = occ(i, it, s)
                        act.wait_ge(A["i_r"], n)
                        act.activation(tr[s][:, :], bank[4 * s][:, :], ACT.Tanh, bias=gb2[:, 0:1], scale=0.5).then_inc(A["i_tr"], 1)
                        act.wait_ge(A["i_z"], n)
                        act.activation(tz[s][:, :], bank[4 * s + 1][:, :], ACT.Tanh, bias=gb2[:, 1:2], scale=0.5).then_inc(A["i_tz"], 1)
                    for s in range(SLOTS):
                        n = occ(i, it, s)
                        act.wait_ge(A["i_q2"], n)
                        act.activation(nn[s][:, :], qn[s][:, :], ACT.Tanh, bias=gbi[:, 2:3]).then_inc(A["i_n"], 1)
                for s in range(SLOTS):
                    n = occ1(i, s)
                    act.wait_ge(A["f_T2"], n)
                    act.activation(snT[s][:, :], bank[4 * s + 1][:, :], ACT.Identity).then_inc(A["f_T2ev"], 1)

            def experts_act(l):
                f = F
                act.wait_ge(f["d"], l + 1)
                act.activation(ge[:, :, :], gt[:, :, :], ACT.Exp).then_inc(f["ex"], 1)
                with act.Fori(0, E // SLOTS) as i:
                    for s in range(SLOTS):
                        n = occ1(i, s) + l * E
                        act.wait_ge(f["T"], n)
                        act.activation(xeT[s][:, 0:512], bank[0][:, :], ACT.Identity)
                        act.activation(xeT[s][:, 512:CAP0], bank[1][:, 0:D], ACT.Identity).then_inc(f["Tev"], 1)
                        for c in range(HC):
                            act.wait_ge(f["h"], n * HC - (HC - 1 - c))
                            bias = {"bias": b1T[:, bass.ds((i * SLOTS + s) * HC + c, 1)]} if l else {}
                            act.activation(hT[s][:, c, CAP0 // 2:CAP0], bank[3 + 2 * (c % 2)][:, 0:CAP0 // 2],
                                           ACT.Relu, **bias).then_inc(f["hevA"], 1)
                        act.wait_ge(f["y"], n)
                        act.activation(ye[:, bass.ds((i * SLOTS + s) * CT, HC), :],
                                       bank[6][:, :].rearrange("p (c d) -> p c d", c=HC), ACT.Identity).then_inc(f["yevA"], 1)

            experts_act(0)
            with act.Fori(0, B // SLOTS) as i:
                for s in range(SLOTS):
                    n = occ1(i, s)
                    mi = bank[6 + s]
                    act.wait_ge(C["cT"], n)
                    act.activation(caT[s][:, :], mi[:, 0:M], ACT.Identity).then_inc(C["cTev"], 1)
                for s in range(SLOTS):
                    n = occ1(i, s)
                    mi = bank[6 + s]
                    act.wait_ge(C["k"], n)
                    for j in range(HG):
                        last = act.activation(kb[s][:, j, :], mi[:, 0:M], ACT.Identity, scale=band[:, j:j + 1])
                    last.then_inc(C["kev"], 1)
                for s in range(SLOTS):
                    n = occ1(i, s)
                    mi = bank[6 + s]
                    act.wait_ge(C["mbT"], n)
                    act.activation(mbT[s][:, :], mi[0:M, :].bitcast(BF16)[:, 0:S], ACT.Identity).then_inc(C["mbTev"], 1)
                for s in range(SLOTS):
                    n = occ1(i, s)
                    act.wait_ge(C["T"], n)
                    act.activation(haT[s][:, :], bank[6 + s][:, 0:S], ACT.Identity).then_inc(C["Tev"], 1)
                for s in range(SLOTS):
                    n = occ1(i, s)
                    act.wait_ge(C["q"], n)
                    act.activation(qT[s][:, :], bank[6 + s][:, 0:S], ACT.Identity).then_inc(C["qev"], 1)
                for s in range(SLOTS):
                    n = occ1(i, s)
                    act.wait_ge(C["nT"], n)
                    act.activation(nmT[s][:, :], bank[6 + s][0:3 * H, :].bitcast(BF16)[:, 0:S], ACT.Identity).then_inc(C["nTev"], 1)
                for s in range(SLOTS):
                    for hf in range(2):
                        act.wait_ge(C["p"], occ1(i, s) * 2 - 1 + hf)
                        for j in range(2):
                            last = act.activation(pT[s][:, (2 * hf + j) * 512:(2 * hf + j + 1) * 512], bank[4 + j][0:M, :], ACT.Exp)
                        last.then_inc(C["ex"], 1)
                for s in range(SLOTS):
                    n = occ1(i, s)
                    act.wait_ge(C["oT"], n)
                    act.activation(oT[s][:, :], bank[6 + s][:, 0:S], ACT.Identity).then_inc(C["oTev"], 1)
                for s in range(SLOTS):
                    n = occ1(i, s)
                    act.wait_ge(C["T2"], n)
                    act.activation(haT[s][:, :], bank[6 + s][:, 0:S], ACT.Identity).then_inc(C["T2ev"], 1)
            experts_act(1)

        @block.tensor
        def _(pe):
            pe.wait_ge(w_in, 16 * NWD)
            pe.wait_ge(k_pool, K_POOL)
            for j in range(11):
                pe.transpose(bank[j // 4][:, (j % 4) * D:(j % 4 + 1) * D], raw[:, j, :], ident[:, :])
            pe.transpose(bank[3][:, 0:E], small[:, :], ident[0:E, 0:E])
            pe.transpose(bank[3][:, 32:64], b1raw[:, :], ident[0:32, 0:32])
            pe.matmul(bank[3][:, 128:256], wqk[:, 1, :], wqk[:, 0, :], start=True, stop=True).then_inc(setup_T, 1)
            pe.wait_ge(setup_ev, 1)
            with pe.Fori(0, NG) as i:
                for s in range(SLOTS):
                    n = occ1(i, s)
                    b0, b1, b2, b3 = bank[4 * s:4 * s + 4]
                    pe.wait_ge(A[f"ctx_in{s}"], 16 * (i + 1))
                    for b in range(G):
                        last = pe.transpose(b3[:, b * M:(b + 1) * M], c_s[s][:, b, :], ident[0:M, 0:M])
                    last.then_inc(A["ctx_T"], 1)
                for s in range(SLOTS):
                    n = occ1(i, s)
                    b0, b1, b2, b3 = bank[4 * s:4 * s + 4]
                    pe.wait_ge(A["x_ln"], n)
                    for b in range(G):
                        last = pe.transpose(b0[:, b * S:(b + 1) * S], tok[s][:, b, :], ident[:, :])
                    last.then_inc(A["x_T"], 1)
                    pe.wait_ge(A["ctx_Tev"], n)
                    pe.matmul(b2[:, 0:G * M], mT[:, :], cT[s][:, :, :].rearrange("p b m -> p (b m)"),
                              start=True, stop=True).then_inc(A["ctx_G"], 1)
                    for b in range(G):
                        last = pe.matmul(b3[0:M, b * D:(b + 1) * D], cT[s][:, b, :], wT[:, W_V, :], start=True, stop=True)
                    last.then_inc(A["ctx_V"], 1)
                for it in range(ITERS):
                    for s in range(SLOTS):
                        n = occ(i, it, s)
                        b0, b1, b2, b3 = bank[4 * s:4 * s + 4]
                        if it == 0:
                            pe.wait_ge(A["x_Tev"], occ1(i, s))
                            pe.wait_ge(A["ctx_Vev"], occ1(i, s))
                            pe.wait_ge(A["ctx_Gev"], occ1(i, s))
                        else:
                            pe.wait_ge(A["i_s"], n - SLOTS)
                        for b in range(G):
                            last = pe.transpose(b0[:, b * D:(b + 1) * D], sT[s][:, b * S:(b + 1) * S], ident[:, :])
                        last.then_inc(A["i_tok"], 1)
                        pe.matmul(b3[:, :], wT[:, W_HH + 2, :], sT[s][:, :], start=True, stop=True).then_inc(A["i_hn"], 1)
                    for s in range(SLOTS):
                        n = occ(i, it, s)
                        b0 = bank[4 * s]
                        pe.wait_ge(A["i_sn"], n)
                        for b in range(G):
                            last = pe.transpose(b0[:, b * S:(b + 1) * S], tok[s][:, b, :], ident[:, :])
                        last.then_inc(A["i_snT"], 1)
                    for s in range(SLOTS):
                        n = occ(i, it, s)
                        b0, b1, b2, b3 = bank[4 * s:4 * s + 4]
                        pe.wait_ge(A["i_snTev"], n)
                        for b in range(G):
                            last = pe.matmul(b1[0:M, b * S:(b + 1) * S], g_s[s][:, b, :], snT[s][:, b * S:(b + 1) * S],
                                             start=True, stop=True)
                        last.then_inc(A["i_sc"], 1)
                        pe.matmul(b0[:, :], wT[:, W_HH, :], sT[s][:, :], start=True, stop=False)
                    for s in range(SLOTS):
                        n = occ(i, it, s)
                        b0, b1, b2, b3 = bank[4 * s:4 * s + 4]
                        pe.wait_ge(A["i_vr"], n)
                        for b in range(G):
                            pe.matmul(b2[:, b * D:(b + 1) * D], ex[s][:, b, :], vr_s[s][:, b, 0:D], start=True, stop=True)
                            last = pe.matmul(b1[:, b:b + 1], ex[s][:, b, :], vr_s[s][:, b, D:D + 1], start=True, stop=True)
                        last.then_inc(A["i_u"], 1)
                    for s in range(SLOTS):
                        n = occ(i, it, s)
                        b0, b1, b2, b3 = bank[4 * s:4 * s + 4]
                        pe.wait_ge(A["i_cs"], n)
                        pe.matmul(b1[:, :], wT[:, W_HH + 1, :], sT[s][:, :], start=True, stop=False)
                        pe.wait_ge(A["i_ut"], n)
                        for b in range(G):
                            last = pe.transpose(b2[:, b * S:(b + 1) * S], tok[s][:, b, :], ident[:, :])
                        last.then_inc(A["i_uT"], 1)
                    for s in range(SLOTS):
                        n = occ(i, it, s)
                        b0, b1, b2, b3 = bank[4 * s:4 * s + 4]
                        pe.wait_ge(A["i_uTev"], n)
                        pe.matmul(b0[:, :], wT[:, W_IH, :], upT[s][:, :], start=False, stop=True).then_inc(A["i_r"], 1)
                        pe.matmul(b2[:, :], wT[:, W_IH + 2, :], upT[s][:, :], start=True, stop=True).then_inc(A["i_xn"], 1)
                        pe.matmul(b1[:, :], wT[:, W_IH + 1, :], upT[s][:, :], start=False, stop=True).then_inc(A["i_z"], 1)
                for s in range(SLOTS):
                    n = occ1(i, s)
                    b0, b1, b2, b3 = bank[4 * s:4 * s + 4]
                    pe.wait_ge(A["i_s"], occ(i, ITERS - 1, s))
                    for b in range(G):
                        last = pe.transpose(b0[:, b * D:(b + 1) * D], sT[s][:, b * S:(b + 1) * S], ident[:, :])
                    last.then_inc(A["f_T"], 1)
                for s in range(SLOTS):
                    n = occ1(i, s)
                    b0, b1, b2, b3 = bank[4 * s:4 * s + 4]
                    pe.wait_ge(A["f_ln"], n)
                    for b in range(G):
                        last = pe.transpose(b1[:, b * S:(b + 1) * S], tok[s][:, b, :], ident[:, :])
                    last.then_inc(A["f_T2"], 1)
                for s in range(SLOTS):
                    n = occ1(i, s)
                    b0, b1, b2, b3 = bank[4 * s:4 * s + 4]
                    pe.wait_ge(A["f_T2ev"], n)
                    for b in range(G):
                        last = pe.matmul(b2[:, b * E:(b + 1) * E], snT[s][:, b * S:(b + 1) * S], wr[0][:, :], start=True, stop=True)
                    last.then_inc(A["f_lg"], 1)

            def experts_pe(l):
                f = F
                pe.wait_ge(f["pos"], l + 1)
                pe.matmul(bank[0][:, 0:E * B], before[:, :], gmb[:, :, :].rearrange("p e b -> p (e b)"), start=True, stop=True)
                pe.matmul(bank[1][:, 0:E * B], ones_bf[:, :], gmb[:, :, :].rearrange("p e b -> p (e b)"), start=True,
                          stop=True).then_inc(f["posr"], 1)
                pe.wait_ge(f["tot"], l + 1)
                with pe.Fori(0, E // SLOTS) as i:
                    for s in range(SLOTS):
                        n = occ1(i, s) + l * E
                        pe.wait_ge(f[f"in{s}"], 16 * (i + 1) + l * (16 * E // SLOTS))
                        for c in range(CT):
                            last = pe.transpose(bank[c // 4][:, (c % 4) * D:(c % 4 + 1) * D], xe[s][:, c, :], ident[:, :])
                        last.then_inc(f["T"], 1)
                        pe.wait_ge(f["Tev"], n)
                        pe.wait_ge(f[f"w{s}"], 32 * (i + 1) + l * (32 * E // SLOTS))
                        for c in range(HC):
                            if c >= 2:
                                pe.wait_ge(f["hevD"], n * HC - (HC - 1 - (c - 2)))
                                pe.wait_ge(f["hevA"], n * HC - (HC - 1 - (c - 2)))
                            for j in range(2):
                                last = pe.matmul(bank[2 + 2 * (c % 2) + j][:, 0:CAP0 // 2], w1[s][:, c * 128:(c + 1) * 128],
                                                 xeT[s][:, j * (CAP0 // 2):(j + 1) * (CAP0 // 2)], start=True, stop=True)
                            last.then_inc(f["h"], 1)
                        pe.wait_ge(f["hevD"], n * HC)
                        pe.wait_ge(f["hevA"], n * HC)
                        for r in range(CT):
                            o = bank[6 + r // 4][:, (r % 4) * D:(r % 4 + 1) * D]
                            if l:
                                pe.matmul(o, ones_row[:, :], b2r[:, bass.ds((i * SLOTS + s) * D, D)], start=True, stop=False)
                            for c in range(HC):
                                last = pe.matmul(o, hT[s][:, c, r * 128:(r + 1) * 128], w2[s][:, c, :],
                                                 start=(c == 0 and not l), stop=(c == HC - 1))
                        last.then_inc(f["y"], 1)

            experts_pe(0)
            with pe.Fori(0, B // SLOTS) as i:
                for s in range(SLOTS):
                    pe.wait_ge(C[f"in{s}"], 32 * (i + 1))
                    pe.transpose(bank[6 + s][:, 0:M], ca[s][:, :], ident[0:M, 0:M]).then_inc(C["cT"], 1)
                for s in range(SLOTS):
                    n = occ1(i, s)
                    mi = bank[6 + s]
                    pe.wait_ge(C["cTev"], n)
                    pe.matmul(mi[:, 0:M], wT[:, W_KK, :], caT[s][:, :], start=True, stop=True).then_inc(C["k"], 1)
                for s in range(SLOTS):
                    n = occ1(i, s)
                    mi = bank[6 + s]
                    pe.wait_ge(C["kev"], n)
                    pe.matmul(mi[0:M, 0:D], caT[s][:, :], wT[:, W_VV, :], start=True, stop=True).then_inc(C["v"], 1)
                for s in range(SLOTS):
                    n = occ1(i, s)
                    mi = bank[6 + s]
                    pe.wait_ge(C["vev"], n)
                    pe.wait_ge(C["mb"], n)
                    pe.transpose(mi[0:M, :].bitcast(BF16)[:, 0:S], mb[s][:, :], ident_bf[:, :]).then_inc(C["mbT"], 1)
                for s in range(SLOTS):
                    n = occ1(i, s)
                    pe.wait_ge(C["mbTev"], n)
                    pe.wait_ge(C["ln"], n)
                    pe.transpose(bank[6 + s][:, 0:S], ha[s][:, :], ident[:, :]).then_inc(C["T"], 1)
                for s in range(SLOTS):
                    pe.wait_ge(C["Tev"], occ1(i, s))
                    pe.matmul(bank[6 + s][:, 0:S], wT[:, W_QQ, :], haT[s][:, :], start=True, stop=True).then_inc(C["q"], 1)
                for s in range(SLOTS):
                    n = occ1(i, s)
                    pe.wait_ge(C["qev"], n)
                    if s:
                        pe.wait_ge(C["mx"], n - 1)
                    for g in range(4):
                        pe.matmul(bank[g][:, 0:HG * M], qT[s][32 * g:32 * g + 32, :],
                                  kb[s][32 * g:32 * g + 32, :, :].rearrange("p j m -> p (j m)"), start=True, stop=False)
                    for g in range(4):
                        last = pe.matmul(bank[g][:, 0:HG * M], ident_bf[:, :],
                                         mb[s][:, :].unsqueeze(1).to_broadcast([128, HG, M]), start=False, stop=True)
                    last.then_inc(C["s"], 1)
                for s in range(SLOTS):
                    n = occ1(i, s)
                    pe.to_reg(n)
                    pe.wait_ge(k_pool, K_POOL)
                    pe.wait_ge(C["lo"], n)
                    pe.transpose(bank[6 + s][0:3 * H, :].bitcast(BF16)[:, 0:S], nmp[s][:, :, :].rearrange("p a h -> p (a h)"),
                                 ident_bf[:, :]).then_inc(C["nT"], 1)
                for s in range(SLOTS):
                    n = occ1(i, s)
                    pe.wait_ge(C["nTev"], n)
                    for hf in range(2):
                        if s or hf:
                            pe.wait_ge(C["ex"], n * 2 - 2 + hf)
                        for j in range(2):
                            g = 2 * hf + j
                            pe.matmul(bank[4 + j][0:M, :], ident_bf[0:M, 0:M],
                                      mbT[s][:, :].unsqueeze(1).to_broadcast([M, HG, S]), start=True, stop=False,
                                      skip_group_check=True)
                        for j in range(2):
                            g = 2 * hf + j
                            for h in range(HG):
                                pe.matmul(bank[4 + j][0:M, h * S:(h + 1) * S], head_sel[:, HG * g + h, :], nmT[s][:, :],
                                          start=False, stop=False, skip_group_check=True)
                        for h in range(HG):
                            for j in range(2):
                                g = 2 * hf + j
                                last = pe.matmul(bank[4 + j][0:M, h * S:(h + 1) * S], kb[s][32 * g:32 * g + 32, h, :],
                                                 qT[s][32 * g:32 * g + 32, :], start=False, stop=True, skip_group_check=True)
                        last.then_inc(C["p"], 1)
                for s in range(SLOTS):
                    n = occ1(i, s)
                    mi = bank[6 + s]
                    pe.wait_ge(C["ex"], n * 2)
                    for h in range(H):
                        last = pe.matmul(mi[:, h * (DK + 1):(h + 1) * (DK + 1)], pT[s][:, h * S:(h + 1) * S], va[s][:, h, :],
                                         start=True, stop=True)
                    last.then_inc(C["pv"], 1)
                for s in range(SLOTS):
                    pe.wait_ge(C["o"], occ1(i, s))
                    pe.transpose(bank[6 + s][:, 0:S], oa[s][:, :], ident[:, :]).then_inc(C["oT"], 1)
                for s in range(SLOTS):
                    pe.wait_ge(C["oTev"], occ1(i, s))
                    pe.matmul(bank[6 + s][:, 0:D], oT[s][:, :], wT[:, W_OO, :], start=True, stop=True).then_inc(C["w"], 1)
                for s in range(SLOTS):
                    pe.wait_ge(C["ln2"], occ1(i, s))
                    pe.transpose(bank[6 + s][:, 0:S], ha[s][:, :], ident[:, :]).then_inc(C["T2"], 1)
                for s in range(SLOTS):
                    pe.wait_ge(C["T2ev"], occ1(i, s))
                    pe.matmul(bank[6 + s][:, 0:E], haT[s][:, :], wr[1][:, :], start=True, stop=True).then_inc(C["lg"], 1)
                for s in range(SLOTS):
                    pe.wait_ge(C["lgev"], occ1(i, s))
            experts_pe(1)

        @block.vector
        def _(dve):
            dve.wait_ge(w_in, 16 * NWD)
            dve.tensor_tensor(gb2[:, :], gbi[:, 0:2], gbh[:, 0:2], ALU.add).then_inc(setup_m, 1)
            dve.wait_ge(setup_m, 1)
            dve.tensor_scalar(gb2[:, :], gb2[:, :], 0.5, None, ALU.mult).then_inc(setup_m, 1)
            dve.tensor_scalar(wslot[:, :], wslot[:, :], float(D) ** -0.5, None, ALU.mult).then_inc(setup_m, 1)
            dve.wait_ge(setup_m, 3)
            dve.wait_ge(k_pool, K_POOL)
            dve.tensor_reduce(band[:, :], ident[:, :].rearrange("p (c j d) -> p j c d", j=HG, d=DK), AX.XY, ALU.add).then_inc(setup_m, 1)

            def ln(src, s, n, st_n, mv_n, rr_n, ln_n):
                dve.to_reg(n)
                for b in range(G):
                    last = dve.bn_stats(st[s][:, 6 * b:6 * b + 6], src[:, b, :])
                last.then_inc(A[st_n], 1)
                dve.wait_ge(k_pool, K_POOL)
                dve.wait_ge(A[st_n], n)
                for b in range(G):
                    last = dve.bn_aggr(mv[s][:, b, :], st[s][:, 6 * b:6 * b + 6])
                last.then_inc(A[mv_n], 1)

            def ln_out(src, s, n, rr_n, ln_n, mv_n):
                dve.wait_ge(A[mv_n], n)
                dve.wait_ge(A[rr_n], n)
                for b in range(G):
                    last = dve.tensor_scalar(tok[s][:, b, :], src[:, b, :], mv[s][:, b, 0:1], rs[s][:, b:b + 1],
                                             ALU.subtract, ALU.mult)
                last.then_inc(A[ln_n], 1)

            with dve.Fori(0, NG) as i:
                for s in range(SLOTS):
                    n = occ1(i, s)
                    dve.wait_ge(A[f"x_in{s}"], 16 * (i + 1))
                    ln(x_s[s], s, n, "x_st", "x_mv", "x_rr", "x_ln")
                for s in range(SLOTS):
                    n = occ1(i, s)
                    ln_out(x_s[s], s, n, "x_rr", "x_ln", "x_mv")
                for s in range(SLOTS):
                    n = occ1(i, s)
                    b0, b1, b2, b3 = bank[4 * s:4 * s + 4]
                    dve.wait_ge(A["ctx_G"], n)
                    dve.tensor_scalar(g_s[s][:, :, :].rearrange("p b m -> p (b m)"), b2[:, 0:G * M], wslot[:, 0:1], None,
                                      ALU.mult).then_inc(A["ctx_Gev"], 1)
                    dve.wait_ge(A["ctx_rr"], n)
                    dve.wait_ge(A["ctx_V"], n)
                    for b in range(G):
                        last = dve.tensor_scalar(v_s[s][:, b, 0:D], b3[0:M, b * D:(b + 1) * D], rc[s][0:M, b:b + 1], None, ALU.mult)
                    last.then_inc(A["ctx_Vev"], 1)
                for it in range(ITERS):
                    for s in range(SLOTS):
                        n = occ(i, it, s)
                        b0 = bank[4 * s]
                        dve.wait_ge(A["i_rr"], n)
                        for b in range(G):
                            last = dve.tensor_scalar(tok[s][:, b, :], b0[:, b * D:(b + 1) * D], rs[s][:, b:b + 1], None, ALU.mult)
                        last.then_inc(A["i_sn"], 1)
                    for s in range(SLOTS):
                        n = occ(i, it, s)
                        b1 = bank[4 * s + 1]
                        dve.wait_ge(A["i_sc"], n)
                        dve.tensor_reduce(mx[s][:, :], b1[0:M, :].rearrange("p (b k) -> p b k", b=G), AX.X, ALU.max).then_inc(A["i_mx"], 1)
                        dve.wait_ge(A["i_mx"], n)
                        dve.scalar_tensor_tensor(out=nb[s][:, :], in0=mx[s][:, :], scalar=-1.0, in1=rc[s][0:M, :],
                                                 op0=ALU.mult, op1=ALU.mult).then_inc(A["i_nb"], 1)
                    for s in range(SLOTS):
                        n = occ(i, it, s)
                        dve.wait_ge(A["i_ex"], n)
                        dve.reciprocal(rm[s][:, :], sm[s][:, :]).then_inc(A["i_rm"], 1)
                        dve.wait_ge(A["i_rm"], n)
                        if it == 0:
                            dve.wait_ge(A["ctx_Vev"], occ1(i, s))
                        for b in range(G):
                            last = dve.tensor_scalar(vr_s[s][:, b, :], v_s[s][:, b, :], rm[s][:, b:b + 1], None, ALU.mult)
                        last.then_inc(A["i_vr"], 1)
                    for s in range(SLOTS):
                        n = occ(i, it, s)
                        b1, b2 = bank[4 * s + 1], bank[4 * s + 2]
                        dve.wait_ge(A["i_u"], n)
                        dve.tensor_scalar(cs[s][:, :], b1[:, 0:G], EPS_RMS, None, ALU.add).then_inc(A["i_cs"], 1)
                        dve.wait_ge(A["i_cs"], n)
                        dve.reciprocal(ci[s][:, :], cs[s][:, :]).then_inc(A["i_ci"], 1)
                        dve.wait_ge(A["i_ci"], n)
                        for b in range(G):
                            last = dve.tensor_scalar(tok[s][:, b, :], b2[:, b * D:(b + 1) * D], ci[s][:, b:b + 1], None, ALU.mult)
                        last.then_inc(A["i_ut"], 1)
                    for s in range(SLOTS):
                        n = occ(i, it, s)
                        b2, b3 = bank[4 * s + 2], bank[4 * s + 3]
                        dve.wait_ge(A["i_tr"], n)
                        dve.tensor_scalar(tr[s][:, :], tr[s][:, :], 0.5, 0.5, ALU.mult, ALU.add).then_inc(A["i_r2"], 1)
                        dve.wait_ge(A["i_r2"], n)
                        dve.wait_ge(A["i_hn"], n)
                        dve.scalar_tensor_tensor(out=qn[s][:, :], in0=b3[:, :], scalar=gbh[:, 2:3], in1=tr[s][:, :],
                                                 op0=ALU.add, op1=ALU.mult).then_inc(A["i_q"], 1)
                        dve.wait_ge(A["i_q"], n)
                        dve.wait_ge(A["i_xn"], n)
                        dve.tensor_tensor(qn[s][:, :], b2[:, :], qn[s][:, :], ALU.add).then_inc(A["i_q2"], 1)
                for s in range(SLOTS):
                    n = occ1(i, s)
                    dve.wait_ge(A["f_T"], n)
                    dve.tensor_tensor(x_s[s][:, :, :], bank[4 * s][:, :].rearrange("p (b d) -> p b d", b=G),
                                      x_s[s][:, :, :], ALU.add).then_inc(A["f_x"], 1)
                    dve.wait_ge(A["f_x"], n)
                    ln(x_s[s], s, n, "f_st", "f_mv", "f_rr", "f_ln")
                for s in range(SLOTS):
                    ln_out(x_s[s], s, occ1(i, s), "f_rr", "f_ln", "f_mv")
                for s in range(SLOTS):
                    n = occ1(i, s)
                    dve.wait_ge(A["f_lg"], n)
                    dve.tensor_tensor(lg[:, bass.ds((i * SLOTS + s) * G, G), :],
                                      bank[4 * s + 2][:, 0:G * E].rearrange("p (b e) -> p b e", b=G),
                                      br[0][:, :].unsqueeze(1).to_broadcast([128, G, E]), ALU.add).then_inc(A["f_lgev"], 1)

            def route(l, logits_n):
                f = F
                cap = float(CAP0 if l == 0 else CAP1)
                steps = route_steps

                def step(ins):
                    steps[0] += 1
                    ins.then_inc(f["dd"], 1)
                    dve.wait_ge(f["dd"], steps[0])

                def wide(a):
                    return a[:, :].unsqueeze(2).to_broadcast([128, B, E])

                def by_batch(a):
                    return a[:, :, :].rearrange("p e b -> p b e")
                dve.wait_ge((A["f_lgev"] if l == 0 else C["lgev"]), logits_n)
                step(dve.tensor_reduce(gx[:, :], lg[:, :, :], AX.X, ALU.max))
                dve.tensor_tensor(gt[:, :, :], lg[:, :, :], wide(gx), ALU.subtract).then_inc(f["d"], 1)
                for k in range(2):
                    step(dve.tensor_tensor(gw[:, :, :], lg[:, :, :], wide(gx), ALU.is_equal))
                    step(dve.tensor_tensor(gw[:, :, :], gw[:, :, :], eight[:, :, :], ALU.mult))
                    step(dve.tensor_reduce(g1[:, :], gw[:, :, :], AX.X, ALU.max))
                    step(dve.tensor_tensor(by_batch(gm[k]), gw[:, :, :], wide(g1), ALU.is_equal))
                    if k == 0:
                        step(dve.scalar_tensor_tensor(out=lg[:, :, :], in0=by_batch(gm[0]), scalar=-BIG, in1=lg[:, :, :],
                                                      op0=ALU.mult, op1=ALU.add))
                        step(dve.tensor_reduce(gx[:, :], lg[:, :, :], AX.X, ALU.max))
                dve.wait_ge(f["ex"], l + 1)
                step(dve.tensor_reduce(gx[:, :], ge[:, :, :], AX.X, ALU.add))
                step(dve.reciprocal(g1[:, :], gx[:, :]))
                step(dve.tensor_tensor(ge[:, :, :], ge[:, :, :], wide(g1), ALU.mult))
                if l == 0:
                    step(dve.scalar_tensor_tensor(out=by_batch(gv), in0=ge[:, :, :], scalar=0.0, in1=by_batch(gm[1]),
                                                  op0=ALU.is_gt, op1=ALU.mult))
                    step(dve.tensor_tensor(gmb[:, :, :], gm[0][:, :, :], gv[:, :, :], ALU.add))
                else:
                    step(dve.tensor_tensor(gmb[:, :, :], gm[0][:, :, :], gm[1][:, :, :], ALU.add))
                dve.tensor_copy(gx[:, :], g1[:, :]).then_inc(f["pos"], 1)
                dve.wait_ge(f["posr"], l + 1)
                pos = bank[0][:, 0:E * B].rearrange("p (e b) -> p e b", e=E)
                tot = bank[1][:, 0:E * B].rearrange("p (e b) -> p e b", e=E)
                if l == 0:
                    step(dve.tensor_copy(gv[:, :, :], tot))
                    step(dve.tensor_tensor_scan(gp[:, :, :].rearrange("p e b -> p (e b)"), chain[:, :, :].rearrange("p e b -> p (e b)"),
                                                gv[:, :, :].rearrange("p e b -> p (e b)"), 0.0, ALU.mult, ALU.add))
                    step(dve.tensor_tensor(gp[:, :, :], gp[:, :, :], gv[:, :, :], ALU.subtract))
                    step(dve.tensor_tensor(gp[:, :, :], pos, gp[:, :, :], ALU.add))
                else:
                    step(dve.tensor_copy(gp[:, :, :], pos))
                dve.tensor_scalar(gv[:, :, :], gp[:, :, :], cap, float(2 * ROWS), ALU.is_ge, ALU.mult).then_inc(f["tot"], 1)
                step(dve.tensor_tensor(gp[:, :, :], gp[:, :, :], base[l][:, :, :], ALU.add))
                step(dve.tensor_tensor(gp[:, :, :], gp[:, :, :], gv[:, :, :], ALU.add))
                for k in range(2):
                    step(dve.tensor_tensor(gv[:, :, :], gp[:, :, :], gm[k][:, :, :], ALU.mult))
                    step(dve.tensor_reduce(sl[k][:, :], by_batch(gv), AX.X, ALU.add))
                    step(dve.tensor_tensor(gw[:, :, :], ge[:, :, :], by_batch(gm[k]), ALU.mult))
                    step(dve.tensor_reduce(g1[:, :], gw[:, :, :], AX.X, ALU.add))
                    if l == 0:
                        step(dve.tensor_scalar(gx[:, :], g1[:, :], 0.0, float(2 * ROWS), ALU.is_le, ALU.mult))
                        step(dve.tensor_tensor(sl[k][:, :], sl[k][:, :], gx[:, :], ALU.add))
                    step(dve.tensor_copy(slot_i[:, k, :], sl[k][:, :]))
                    step(dve.scalar_tensor_tensor(out=gate[:, k, :], in0=sl[k][:, :], scalar=float(ROWS), in1=g1[:, :],
                                                  op0=ALU.is_lt, op1=ALU.mult))
                dve.tensor_copy(g1[:, :], gx[:, :]).then_inc(f["slot"], 1)

            def experts_dve(l):
                f = F
                with dve.Fori(0, E // SLOTS) as i:
                    for s in range(SLOTS):
                        n = occ1(i, s) + l * E
                        for c in range(HC):
                            dve.wait_ge(f["h"], n * HC - (HC - 1 - c))
                            if l:
                                last = dve.tensor_scalar(hT[s][:, c, 0:CAP0 // 2], bank[2 + 2 * (c % 2)][:, 0:CAP0 // 2],
                                                         b1T[:, bass.ds((i * SLOTS + s) * HC + c, 1)], 0.0, ALU.add, ALU.max)
                            else:
                                last = dve.tensor_scalar(hT[s][:, c, 0:CAP0 // 2], bank[2 + 2 * (c % 2)][:, 0:CAP0 // 2],
                                                         0.0, None, ALU.max)
                            last.then_inc(f["hevD"], 1)
                        dve.wait_ge(f["y"], n)
                        dve.tensor_copy(ye[:, bass.ds((i * SLOTS + s) * CT + HC, 1), :],
                                        bank[7][:, 0:D].unsqueeze(1)).then_inc(f["yevD"], 1)

            def scaled(k, b, x):
                return dict(in0=yk[:, bass.ds(2 * b + k, 1), :].rearrange("p a d -> p (a d)"),
                            scalar=gate[:, k, bass.ds(b, 1)], in1=x, op0=ALU.mult, op1=ALU.add)

            route(0, B // G)
            experts_dve(0)
            dve.wait_ge(F["gath"], 16 * 2 * B)
            with dve.Fori(0, B // SLOTS) as i:
                def ln1(s, st_n, mv_n, x_n):
                    n = occ1(i, s)
                    dve.to_reg(n)
                    dve.wait_ge(C[x_n], n)
                    dve.bn_stats(sta[s][:, :], xa[s][:, :]).then_inc(C[st_n], 1)
                    dve.wait_ge(k_pool, K_POOL)
                    dve.wait_ge(C[st_n], n)
                    dve.bn_aggr(mva[s][:, :], sta[s][:, :]).then_inc(C[mv_n], 1)

                def ln1_out(s, rr_n, ln_n, mv_n):
                    n = occ1(i, s)
                    dve.wait_ge(C[rr_n], n)
                    dve.wait_ge(C[mv_n], n)
                    dve.tensor_scalar(ha[s][:, :], xa[s][:, :], mva[s][:, 0:1], rsa[s][:, :], ALU.subtract, ALU.mult).then_inc(C[ln_n], 1)
                for s in range(SLOTS):
                    n = occ1(i, s)
                    b = i * SLOTS + s
                    dve.scalar_tensor_tensor(out=xa[s][:, :], **scaled(0, b, xs[:, bass.ds(b, 1), :].rearrange("p a d -> p (a d)"))).then_inc(C["x1"], 1)
                    dve.wait_ge(C["x1"], n)
                    dve.scalar_tensor_tensor(out=xa[s][:, :], **scaled(1, b, xa[s][:, :])).then_inc(C["x2"], 1)
                    ln1(s, "st", "mv", "x2")
                    dve.wait_ge(C[f"in{s}"], 32 * (i + 1))
                    dve.tensor_scalar(mb[s][:, :], mk[s][:, :], 0.0, -BIG, ALU.is_equal, ALU.mult).then_inc(C["mb"], 1)
                for s in range(SLOTS):
                    ln1_out(s, "rr", "ln", "mv")
                for s in range(SLOTS):
                    n = occ1(i, s)
                    dve.wait_ge(C["v"], n)
                    dve.tensor_copy(va[s][:, :, 0:DK], bank[6 + s][0:M, 0:D].rearrange("p (h d) -> p h d", h=H)).then_inc(C["vev"], 1)
                for s in range(SLOTS):
                    n = occ1(i, s)
                    dve.wait_ge(C["s"], n)
                    for g in range(4):
                        last = dve.tensor_reduce(mxa[s][:, HG * g:HG * g + HG], bank[g][:, 0:HG * M].rearrange("p (h m) -> p h m", h=HG),
                                                 AX.X, ALU.max)
                    last.then_inc(C["mx"], 1)
                    dve.wait_ge(C["mx"], n)
                    dve.tensor_scalar(nm[s][:, :], mxa[s][:, :], -BIG / 10, -1.0, ALU.max, ALU.mult).then_inc(C["nm"], 1)
                    dve.wait_ge(C["nm"], n)
                    dve.tensor_copy(nmp[s][:, 0, :], nm[s][:, :]).then_inc(C["hi"], 1)
                    dve.wait_ge(C["hi"], n)
                    dve.tensor_tensor(nr[s][:, :], nm[s][:, :], nmp[s][:, 0, :], ALU.subtract).then_inc(C["r1"], 1)
                    dve.wait_ge(C["r1"], n)
                    dve.tensor_copy(nmp[s][:, 1, :], nr[s][:, :]).then_inc(C["mid"], 1)
                    dve.wait_ge(C["mid"], n)
                    dve.tensor_tensor(nmp[s][:, 2, :], nr[s][:, :], nmp[s][:, 1, :], ALU.subtract).then_inc(C["lo"], 1)
                for s in range(SLOTS):
                    n = occ1(i, s)
                    o = bank[6 + s][:, 0:H * (DK + 1)].rearrange("p (h d) -> p h d", h=H)
                    dve.wait_ge(C["pv"], n)
                    dve.tensor_scalar(den[s][:, :].unsqueeze(2), o[:, :, DK:DK + 1], 1.0e-30, None, ALU.max).then_inc(C["den"], 1)
                    dve.wait_ge(C["den"], n)
                    dve.reciprocal(rden[s][:, :], den[s][:, :]).then_inc(C["rd"], 1)
                    dve.wait_ge(C["rd"], n)
                    dve.tensor_tensor(oa[s][:, :].rearrange("p (h d) -> p h d", h=H), o[:, :, 0:DK],
                                      rden[s][:, :].unsqueeze(2).to_broadcast([128, H, DK]), ALU.mult).then_inc(C["o"], 1)
                for s in range(SLOTS):
                    n = occ1(i, s)
                    dve.wait_ge(C["w"], n)
                    dve.tensor_tensor(xa[s][:, :], bank[6 + s][:, 0:D], xa[s][:, :], ALU.add).then_inc(C["x3"], 1)
                    ln1(s, "st2", "mv2", "x3")
                for s in range(SLOTS):
                    ln1_out(s, "rr2", "ln2", "mv2")
                for s in range(SLOTS):
                    n = occ1(i, s)
                    dve.wait_ge(C["lg"], n)
                    dve.wait_ge(C["keep"], n)
                    dve.tensor_tensor(lg[:, bass.ds(i * SLOTS + s, 1), :], bank[6 + s][:, 0:E].unsqueeze(1),
                                      br[1][:, :].unsqueeze(1), ALU.add).then_inc(C["lgev"], 1)
            route(1, B)
            experts_dve(1)
            dve.wait_ge(F["gath"], 2 * 16 * 2 * B)
            with dve.Fori(0, B // G) as i:
                for k in range(2):
                    for j in range(G):
                        b = i * G + j
                        x = xs[:, bass.ds(b, 1), :].rearrange("p a d -> p (a d)")
                        last = dve.scalar_tensor_tensor(out=x, **scaled(k, b, x))
                    if k == 0:
                        last.then_inc(setup_done, 1)
                        dve.wait_ge(setup_done, i + 1)
                last.then_inc(Z["b"], 1)


_INS = ['x', 'ctx_1024', 'mask_Bx1xSxS2_ik0', 'L0_xattn_Wq', 'L0_xattn_Wk', 'L0_xattn_Wv', 'L0_xattn_gru_wih',
        'L0_xattn_gru_whh', 'L0_xattn_gru_bih', 'L0_xattn_gru_bhh', 'L0_xattn_slot_norm_w',
        'L0_xattn_input_norm_w', 'L0_ffn_W_router', 'L0_ffn_b_router', 'L0_ffn_experts_inter',
        'L0_ffn_experts_out', 'L1_xattn_W_Q', 'L1_xattn_W_K', 'L1_xattn_W_V', 'L1_xattn_W_O', 'L1_ffn_Wr',
        'L1_ffn_br', 'L1_ffn_W1', 'L1_ffn_b1', 'L1_ffn_W2', 'L1_ffn_b2']


def kernel(**inputs):
    import numpy as _np
    import concourse.bacc as _bacc
    from concourse import mybir as _mybir
    from concourse.bass_utils import run_bass_kernel_spmd as _run

    nc = _bacc.Bacc("TRN2", target_bir_lowering=False, num_devices=1)
    arrays, args = {}, {}
    for name in _INS:
        a = _np.ascontiguousarray(inputs[name])
        arrays[f"in_{name}_dram"] = a
        args[name] = nc.dram_tensor(f"in_{name}_dram", a.shape, _mybir.dt.from_np(a.dtype), kind="ExternalInput").ap()
    out = nc.dram_tensor("out_0_dram", (B, S, D), F32, kind="ExternalOutput").ap()
    build(nc, args, out)
    r = _run(nc, [arrays], core_ids=[0])
    return r.results[0]["out_0_dram"]
```

```python
from contextlib import ExitStack

import concourse.bass as bass
from concourse import mybir

F32 = mybir.dt.float32
BF16 = mybir.dt.bfloat16
I32 = mybir.dt.int32
ALU = mybir.AluOpType
ACT = mybir.ActivationFunctionType
AX = mybir.AxisListType.X

B, S, D = 32, 128, 128
M = 120
G = 4
SLOTS = 2
NG = B // G // SLOTS
ITERS = 3
E, HID = 8, 512
HC = HID // 128
CAP0 = 640
CAP1 = 20
ROWS = E * CAP0
CT = CAP0 // 128
H, DK = 16, 8
HG = 4
BIG = 1.0e30
EPS_LN, EPS_RMS = 1e-5, 1e-6
STOP = 9


def build(nc, t, out):
    ctx = ExitStack()
    with ctx:
        def sb(name, shape, dt=F32, of=ctx):
            return of.enter_context(nc.sbuf_tensor(name, shape, dt))

        def sem(name):
            return ctx.enter_context(nc.semaphore(name))

        def sems(names):
            return {n: sem("s_" + n) for n in names.split()}

        rows_d = [nc.dram_tensor(f"rows{l}", [ROWS, D], F32, kind="Internal").ap() for l in range(2)]
        res_d = [nc.dram_tensor(f"res{l}", [ROWS, D], F32, kind="Internal").ap() for l in range(2)]

        bank = [ctx.enter_context(nc.psum_tensor(f"bank{i}", [128, 512], F32)) for i in range(8)]
        bank4 = None

        ident = sb("ident", [128, 128])
        ident_bf = sb("ident_bf", [128, 128], BF16)
        ones_bf = sb("ones_bf", [128, 128], BF16)
        before = sb("before", [128, 128], BF16)
        ones_row = sb("ones_row", [1, 128])
        band = sb("band", [128, HG])
        iota_e = sb("iota_e", [128, E])
        minus_half = sb("minus_half", [128, G])
        eps_ln = sb("eps_ln", [128, G])
        eps_rms = sb("eps_rms", [128, G])
        raw = sb("raw", [128, 11, D])
        wqk = sb("wqk", [128, 2, D])
        small = sb("small", [E, D])
        b1raw = sb("b1raw", [32, 128])
        wT = sb("wT", [128, 11, D])
        mT = sb("mT", [128, D])
        wr = [sb(f"wr{l}", [128, E]) for l in range(2)]
        br = [sb(f"br{l}", [128, E]) for l in range(2)]
        b1T = sb("b1T", [128, E * HC])
        b2r = sb("b2r", [1, E * D])
        win = sb("win", [128, 1])
        wslot = sb("wslot", [128, 1])
        gbi = sb("gbi", [128, 3])
        gbh = sb("gbh", [128, 3])
        gb2 = sb("gb2", [128, 2])

        xs = sb("xs", [128, B, D])
        hs = sb("hs", [128, B, D])
        ye = sb("ye", [128, E * CT, D])
        yg = [sb(f"yg{s}", [128, 2, D]) for s in range(SLOTS)]
        pick = [sb(f"pick{s}", [128, 2], I32) for s in range(SLOTS)]
        lg = sb("lg", [128, B, E])
        gate = sb("gate", [128, 2, B])
        slot_i = sb("slot_i", [128, 2, B], I32)

        def per(name, shape, dt=F32, of=ctx):
            return [sb(f"{name}{s}", shape, dt, of) for s in range(SLOTS)]

        gt = sb("gt", [128, B, E])
        ge = sb("ge", [128, B, E])
        gw = sb("gw", [128, B, E])
        gm = [sb(f"gm{k}", [128, E, B]) for k in range(2)]
        gmb = sb("gmb", [128, E, B], BF16)
        gv = sb("gv", [128, E, B])
        gp = sb("gp", [128, E, B])
        gx = sb("gx", [128, B])
        g1 = sb("g1", [128, B])
        eight = sb("eight", [128, B, E])
        chain = sb("chain", [128, E, B])
        base = [sb(f"base{l}", [128, E, B]) for l in range(2)]
        base_i = sb("base_i", [128, E, B], I32)
        sl = [sb(f"sl{k}", [128, B]) for k in range(2)]

        xe = per("xe", [128, CT, D])
        xeT = per("xeT", [128, CAP0])
        w1 = per("w1", [128, HID])
        w2 = per("w2", [128, HC, D])
        hT = per("hT", [128, HC, CAP0])

        va = per("va", [M, H, DK + 1])
        early = ExitStack()
        x_s = per("x_s", [128, G, D], of=early)
        c_s = per("c_s", [M, G, D], of=early)
        cT = per("cT", [128, G, M], of=early)
        g_s = per("g_s", [128, G, M], of=early)
        v_s = per("v_s", [M, G, D + 1], of=early)
        vr_s = per("vr_s", [M, G, D + 1], of=early)
        st = per("st", [128, G * 6], of=early)
        mv = per("mv", [128, G, 2], of=early)
        pw = per("pw", [128, G], of=early)
        rs = per("rs", [128, G], of=early)
        pwc = per("pwc", [128, G], of=early)
        rc = per("rc", [128, G], of=early)
        mx = per("mx", [M, G], of=early)
        nb = per("nb", [M, G], of=early)
        sm = per("sm", [M, G], of=early)
        rm = per("rm", [M, G], of=early)
        cs = per("cs", [128, G], of=early)
        ci = per("ci", [128, G], of=early)
        sT = per("sT", [128, G * S], of=early)
        tok = per("tok", [128, G, D], of=early)
        snT = per("snT", [128, G * S], of=early)
        ex = per("ex", [M, G, S], of=early)
        upT = per("upT", [128, G * S], of=early)
        tr = per("tr", [128, G * S], of=early)
        tz = per("tz", [128, G * S], of=early)
        qn = per("qn", [128, G * S], of=early)
        nn = per("nn", [128, G * S], of=early)
        uu = per("uu", [128, G * S], of=early)

        early.close()

        ca = per("ca", [M, D])
        mk = per("mk", [128, M], I32)
        mb = per("mb", [128, M], BF16)
        caT = per("caT", [128, M])
        kb = per("kb", [128, HG, M])
        sta = per("sta", [128, 6])
        mva = per("mva", [128, 2])
        pwa = per("pwa", [128, 1])
        rsa = per("rsa", [128, 1])
        ha = per("ha", [128, D])
        haT = per("haT", [128, S])
        qT = per("qT", [128, S])
        mxa = per("mxa", [128, H])
        nm = per("nm", [128, H])
        pr = per("pr", [128, H, M])
        pT = per("pT", [M, H * S])
        den = per("den", [128, H])
        rden = per("rden", [128, H])
        oa = per("oa", [128, D])
        oT = per("oT", [128, S])
        stb = per("stb", [128, 6])
        mvb = per("mvb", [128, 2])
        pwb = per("pwb", [128, 1])
        rsb = per("rsb", [128, 1])
        hb = per("hb", [128, D])
        hbT = per("hbT", [128, S])

        w_in = sem("w_in")
        k_pool = sem("k_pool")
        setup_T = sem("setup_T")
        setup_ev = sem("setup_ev")
        setup_m = sem("setup_m")
        setup_done = sem("setup_done")
        zeroed = sem("zeroed")
        stored = sem("stored")
        F = {k: sem(f"f_{k}") for k in
             ("d dd ex pos posr tot slot scat w0 w1 in0 in1 T Tev h hevD hevA y yevD yevA out").split()}
        route_steps = [0]
        C = {k: sem("c_" + k) for k in
             ("in0 in1 g0 g1 pick x1 x2 st mv pw rr ln T Tev kqv kqev mb s mx nm sub ex pt pev pv den rd o "
              "oT oTev w x3 st2 mv2 pw2 rr2 ln2 keep T2 T2ev lg lgev").split()}
        Z = {k: sem("z_" + k) for k in "a b".split()}
        A = sems("ctx_in0 x_in0 ctx_in1 x_in1 ctx_ms ctx_rr ctx_T ctx_Tev ctx_G ctx_Gev ctx_V ctx_Vev "
                 "x_st x_mv x_rr x_ln x_T x_Tev "
                 "i_tok i_ms i_pw i_rr i_sn i_snT i_snTev i_sc i_mx i_nb i_ex i_rm i_vr i_u i_cs i_ci i_ut "
                 "i_uT i_uTev i_hn i_r i_z i_xn i_tr i_tz i_r2 i_q i_q2 i_n i_z2 i_d i_v i_s "
                 "f_T f_x f_st f_mv f_pw f_rr f_ln f_T2 f_T2ev f_lg f_lgev f_keep x_pw ctx_pw")

        K_POOL = 29
        block = ctx.enter_context(nc.Block())
        W_V, W_IH, W_HH, W_QQ, W_KK, W_VV, W_OO = 0, 1, 4, 7, 8, 9, 10
        x_v = t["x"].rearrange("(g b) s d -> g s b d", b=G)
        c_v = t["ctx_1024"].rearrange("(g b) m d -> g m b d", b=G)
        out_v = out.rearrange("b s d -> s b d")
        base_v = [r.rearrange("(p r) d -> p (r d)", p=128) for r in rows_d]
        res_v = [r.rearrange("(e c p) d -> e p c d", e=E, p=128) for r in res_d]
        rows_v = [r.rearrange("(e c p) d -> e p c d", e=E, p=128) for r in rows_d]
        w1_v = (t["L0_ffn_experts_inter"], t["L1_ffn_W1"])
        w2_v = [w.rearrange("e (c p) d -> e p c d", p=128) for w in (t["L0_ffn_experts_out"], t["L1_ffn_W2"])]
        mask_v = t["mask_Bx1xSxS2_ik0"].rearrange("b a s m -> (b a) s m")
        NWD = 19

        def occ(i, it, s, per_turn=ITERS):
            return i * (per_turn * SLOTS) + it * SLOTS + s + 1

        def occ1(i, s):
            return i * SLOTS + s + 1

        FIRST, LAST = -3, B + 2

        def batch_of(i, s, k):
            return i * SLOTS + s + k, (s + k) % SLOTS, i + (s + k) // SLOTS

        def inside(b):
            return not isinstance(b, int) or 0 <= b < B

        def pipeline(eng, step):
            for b in range(FIRST, 2 * SLOTS):
                step(b // SLOTS, b % SLOTS)
            with eng.Fori(2, (B - 3) // SLOTS) as i:
                for s in range(SLOTS):
                    step(i, s)
            for b in range((B - 3) // SLOTS * SLOTS, LAST + 1):
                step(b // SLOTS, b % SLOTS)

        @block.sync
        def _(sp):
            for k, name in enumerate(("L0_xattn_Wv", "L1_xattn_W_Q", "L1_xattn_W_K", "L1_xattn_W_V", "L1_xattn_W_O")):
                at = (W_V, W_QQ, W_KK, W_VV, W_OO)[k]
                sp.dma_start(raw[:, at, :], t[name]).then_inc(w_in, 16)
            sp.dma_start(raw[:, W_IH:W_IH + 3, :], t["L0_xattn_gru_wih"].rearrange("(c p) d -> p c d", p=128)).then_inc(w_in, 16)
            sp.dma_start(raw[:, W_HH:W_HH + 3, :], t["L0_xattn_gru_whh"].rearrange("(c p) d -> p c d", p=128)).then_inc(w_in, 16)
            sp.dma_start(wqk[:, 0, :], t["L0_xattn_Wq"]).then_inc(w_in, 16)
            sp.dma_start(wqk[:, 1, :], t["L0_xattn_Wk"]).then_inc(w_in, 16)
            sp.dma_start(small[:, :], t["L0_ffn_W_router"]).then_inc(w_in, 16)
            sp.dma_start(wr[1][:, :], t["L1_ffn_Wr"]).then_inc(w_in, 16)
            sp.dma_start(br[0][:, :], t["L0_ffn_b_router"].partition_broadcast(128)).then_inc(w_in, 16)
            sp.dma_start(br[1][:, :], t["L1_ffn_br"].partition_broadcast(128)).then_inc(w_in, 16)
            sp.dma_start(b1raw[:, :], t["L1_ffn_b1"].rearrange("e (c p) -> (e c) p", p=128)).then_inc(w_in, 16)
            sp.dma_start(b2r[:, :], t["L1_ffn_b2"].rearrange("(a e) d -> a (e d)", a=1)).then_inc(w_in, 16)
            with nc.allow_non_contiguous_dma(reason="columns of 128 and 384 floats"):
                sp.dma_start(win[:, :], t["L0_xattn_input_norm_w"].rearrange("(p a) -> p a", a=1)).then_inc(w_in, 16)
                sp.dma_start(wslot[:, :], t["L0_xattn_slot_norm_w"].rearrange("(p a) -> p a", a=1)).then_inc(w_in, 16)
                sp.dma_start(gbi[:, :], t["L0_xattn_gru_bih"].rearrange("(c p) -> p c", p=128)).then_inc(w_in, 16)
                sp.dma_start(gbh[:, :], t["L0_xattn_gru_bhh"].rearrange("(c p) -> p c", p=128)).then_inc(w_in, 16)
            for s in range(SLOTS):
                sp.dma_start(c_s[s][:, :, :], c_v[s]).then_inc(A[f"ctx_in{s}"], 16)
                sp.dma_start(x_s[s][:, :, :], x_v[s]).then_inc(A[f"x_in{s}"], 16)
            with sp.Fori(1, NG) as i:
                for s in range(SLOTS):
                    sp.wait_ge(A["f_lgev"], occ1(i - 1, s))
                    sp.wait_ge(A["f_keep"], occ1(i - 1, s))
                    sp.dma_start(c_s[s][:, :, :], c_v[bass.ds(i * SLOTS + s, 1)].rearrange("a m b d -> m (a b) d")).then_inc(A[f"ctx_in{s}"], 16)
                    sp.dma_start(x_s[s][:, :, :], x_v[bass.ds(i * SLOTS + s, 1)].rearrange("a m b d -> m (a b) d")).then_inc(A[f"x_in{s}"], 16)

            def experts_sp(l):
                f = F

                def weights(i, s):
                    sp.dma_start(w1[s][:, :], w1_v[l][bass.ds(i * SLOTS + s, 1)].rearrange("a p n -> p (a n)")).then_inc(f[f"w{s}"], 16)
                    sp.dma_start(w2[s][:, :, :], w2_v[l][bass.ds(i * SLOTS + s, 1)].rearrange("a p c d -> p (a c) d")).then_inc(f[f"w{s}"], 16)

                def rows(i, s):
                    sp.dma_start(xe[s][:, :, :], rows_v[l][bass.ds(i * SLOTS + s, 1)].rearrange("a p c d -> p (a c) d")).then_inc(f[f"in{s}"], 16)

                def store(i, s):
                    sp.wait_ge(f["yevA"], occ1(i, s) + l * E)
                    sp.wait_ge(f["yevD"], occ1(i, s) + l * E)
                    sp.dma_start(res_v[l][bass.ds(i * SLOTS + s, 1)].rearrange("a p c d -> p (a c) d"),
                                 ye[:, bass.ds((i * SLOTS + s) * CT, CT), :]).then_inc(f["out"], 16)
                for s in range(SLOTS):
                    weights(0, s)
                sp.wait_ge(f["scat"], 16 * 2 * B * (l + 1))
                for s in range(SLOTS):
                    rows(0, s)
                with sp.Fori(1, E // SLOTS) as i:
                    for s in range(SLOTS):
                        store(i - 1, s)
                        weights(i, s)
                        rows(i, s)
                for s in range(SLOTS):
                    store(E // SLOTS - 1, s)

            sp.wait_ge(Z["a"], 1)
            for l in range(2):
                for j in range(ROWS // 128 // CT):
                    sp.dma_start(base_v[l][:, j * CT * D:(j + 1) * CT * D], ye[:, 0:CT, :].rearrange("p c d -> p (c d)")).then_inc(zeroed, 16)
            experts_sp(0)
            for s in range(SLOTS):
                sp.dma_start(ca[s][:, :], t["ctx_1024"][s]).then_inc(C[f"in{s}"], 16)
                sp.dma_start(mk[s][:, :], mask_v[s]).then_inc(C[f"in{s}"], 16)

            def step(i, s):
                b, v, turn = batch_of(i, s, 3)
                if inside(b) and (not isinstance(b, int) or b >= SLOTS):
                    sp.wait_ge(C["T"], b - 1)
                    sp.wait_ge(C["mb"], b - 1)
                    sp.dma_start(ca[v][:, :], t["ctx_1024"][bass.ds(b, 1)].rearrange("a m d -> m (a d)")).then_inc(C[f"in{v}"], 16)
                    sp.dma_start(mk[v][:, :], mask_v[bass.ds(b, 1)].rearrange("a q m -> q (a m)")).then_inc(C[f"in{v}"], 16)
            pipeline(sp, step)
            experts_sp(1)
            with sp.Fori(0, B // G) as i:
                sp.wait_ge(Z["b"], (i + 1) * G)
                sp.dma_start(out_v[:, bass.ds(i * G, G), :], xs[:, bass.ds(i * G, G), :]).then_inc(stored, 16)
            sp.wait_ge(stored, 16 * (B // G))

        @block.gpsimd
        def _(pool):
            pool.memset(ident[:, :], 0.0).then_inc(k_pool, 1)
            pool.memset(ones_bf[:, :], 1.0).then_inc(k_pool, 1)
            pool.memset(minus_half[:, :], -0.5).then_inc(k_pool, 1)
            pool.memset(eps_ln[:, :], EPS_LN).then_inc(k_pool, 1)
            pool.memset(eps_rms[:, :], EPS_RMS).then_inc(k_pool, 1)
            pool.memset(ones_row[:, :], 1.0).then_inc(k_pool, 1)
            for s in range(SLOTS):
                pool.memset(v_s[s][:, :, D:D + 1], 1.0).then_inc(k_pool, 1)
            pool.wait_ge(k_pool, 8)
            pool.affine_select(out=ident[:, :], in_=ident[:, :], compare_op=ALU.not_equal, fill=1.0,
                               base=0, pattern=[[-1, 128]], channel_multiplier=1).then_inc(k_pool, 1)
            pool.affine_select(out=before[:, :], in_=ones_bf[:, :], compare_op=ALU.is_gt, fill=0.0,
                               base=0, pattern=[[1, 128]], channel_multiplier=-1).then_inc(k_pool, 1)
            pool.iota(base_i[:, :, :], pattern=[[CAP0, E], [0, B]], base=0, channel_multiplier=0).then_inc(k_pool, 1)
            pool.wait_ge(k_pool, 11)
            pool.tensor_copy(base[0][:, :, :], base_i[:, :, :]).then_inc(k_pool, 1)
            pool.wait_ge(k_pool, 12)
            pool.iota(base_i[:, :, :], pattern=[[CAP0, E], [CAP1, B]], base=0, channel_multiplier=0).then_inc(k_pool, 1)
            pool.wait_ge(k_pool, 13)
            pool.tensor_copy(base[1][:, :, :], base_i[:, :, :]).then_inc(k_pool, 1)
            pool.memset(chain[:, :, :], 1.0).then_inc(k_pool, 1)
            pool.wait_ge(k_pool, 15)
            pool.memset(chain[:, :, 0:1], 0.0).then_inc(k_pool, 1)
            for e in range(E):
                pool.memset(eight[:, :, e:e + 1], float(E - e)).then_inc(k_pool, 1)
            for s in range(SLOTS):
                pool.memset(va[s][:, :, DK:DK + 1], 1.0).then_inc(k_pool, 1)
            for s in range(SLOTS):
                pool.memset(yg[s][:, :, :], 0.0).then_inc(k_pool, 1)
            pool.memset(ye[:, :, :], 0.0).then_inc(Z["a"], 1)
            pool.tensor_copy(ident_bf[:, :], ident[:, :]).then_inc(k_pool, 1)

            def power(src, dst, rows, n, s_src, s_mid, mid, s_dst, eps):
                pool.wait_ge(A[s_src], n)
                pool.tensor_tensor(mid[0:rows, :], src, eps[0:rows, :], ALU.add).then_inc(A[s_mid], 1)
                pool.wait_ge(A[s_mid], n)
                pool.tensor_tensor(dst[0:rows, :], mid[0:rows, :], minus_half[0:rows, :], ALU.pow).then_inc(A[s_dst], 1)

            with pool.Fori(0, NG) as i:
                for s in range(SLOTS):
                    n = occ1(i, s)
                    power(pwc[s][0:M, :], rc[s], M, n, "ctx_ms", "ctx_pw", pwc[s], "ctx_rr", eps_rms)
                for s in range(SLOTS):
                    n = occ1(i, s)
                    power(mv[s][:, :, 1], rs[s], 128, n, "x_mv", "x_pw", pw[s], "x_rr", eps_ln)
                for it in range(ITERS):
                    for s in range(SLOTS):
                        n = occ(i, it, s)
                        power(cs[s][:, :], rs[s], 128, n, "i_ms", "i_pw", pw[s], "i_rr", eps_rms)
                    for s in range(SLOTS):
                        n = occ(i, it, s)
                        pool.wait_ge(k_pool, K_POOL)
                        pool.wait_ge(A["i_tz"], n)
                        pool.tensor_scalar(tz[s][:, :], tz[s][:, :], 0.5, 0.5, ALU.mult, ALU.add).then_inc(A["i_z2"], 1)
                        pool.wait_ge(A["i_n"], n)
                        pool.tensor_tensor(uu[s][:, :], sT[s][:, :], nn[s][:, :], ALU.subtract).then_inc(A["i_d"], 1)
                        pool.wait_ge(A["i_z2"], n)
                        pool.wait_ge(A["i_d"], n)
                        pool.tensor_tensor(uu[s][:, :], uu[s][:, :], tz[s][:, :], ALU.mult).then_inc(A["i_v"], 1)
                        pool.wait_ge(A["i_v"], n)
                        pool.wait_ge(A["i_z"], n)
                        pool.tensor_tensor(sT[s][:, :], uu[s][:, :], nn[s][:, :], ALU.add).then_inc(A["i_s"], 1)
                for s in range(SLOTS):
                    n = occ1(i, s)
                    power(mv[s][:, :, 1], rs[s], 128, n, "f_mv", "f_pw", pw[s], "f_rr", eps_ln)
                for s in range(SLOTS):
                    n = occ1(i, s)
                    pool.wait_ge(A["f_x"], n)
                    pool.tensor_copy(xs[:, bass.ds((i * SLOTS + s) * G, G), :], x_s[s][:, :, :])
                    pool.wait_ge(A["f_ln"], n)
                    pool.tensor_copy(hs[:, bass.ds((i * SLOTS + s) * G, G), :], tok[s][:, :, :]).then_inc(A["f_keep"], 1)

            def dispatch(l):
                f = F
                pool.wait_ge(f["slot"], l + 1)
                if l:
                    pool.wait_ge(C["keep"], B)
                else:
                    pool.wait_ge(A["f_keep"], B // G)
                pool.wait_ge(zeroed, 16 * 2 * (ROWS // 128 // CT))
                for b in range(B):
                    for k in range(2):
                        pool.indirect_dma_start(out=rows_d[l], out_offset=bass.IndirectOffsetOnAxis(ap=slot_i[:, k, b:b + 1], axis=0),
                                                in_=hs[:, b, :], in_offset=None, bounds_check=ROWS - 1,
                                                oob_is_err=False).then_inc(f["scat"], 16)

            def fetch(l, b, v):
                pool.tensor_copy(pick[v][:, :].unsqueeze(2), slot_i[:, :, bass.ds(b, 1)]).then_inc(C["pick"], 1)
                pool.to_reg(l * B + b + 1)
                pool.wait_ge(k_pool, K_POOL)
                pool.wait_ge(C["pick"], l * B + b + 1)
                for k in range(2):
                    pool.indirect_dma_start(out=yg[v][:, k, :], out_offset=None, in_=res_d[l],
                                            in_offset=bass.IndirectOffsetOnAxis(ap=pick[v][:, k:k + 1], axis=0),
                                            bounds_check=ROWS - 1, oob_is_err=False).then_inc(C[f"g{v}"], 16)

            def power1(n, src, mid, dst, s_src, s_mid, s_dst):
                pool.wait_ge(C[s_src], n)
                pool.tensor_tensor(mid[:, :], src[:, 1:2], eps_ln[:, 0:1], ALU.add).then_inc(C[s_mid], 1)
                pool.wait_ge(C[s_mid], n)
                pool.tensor_tensor(dst[:, :], mid[:, :], minus_half[:, 0:1], ALU.pow).then_inc(C[s_dst], 1)

            def step(i, s):
                b, v, turn = batch_of(i, s, 3)
                if inside(b):
                    pool.to_reg(b)
                    if not isinstance(b, int) or b >= SLOTS:
                        pool.wait_ge(C["x2"], b - 1)
                        pool.wait_ge(C[f"g{v}"], 32 * turn)
                    fetch(0, b, v)
                b, v, turn = batch_of(i, s, 2)
                if inside(b):
                    power1(b + 1, mva[v], pwa[v], rsa[v], "mv", "pw", "rr")
                b, v, turn = batch_of(i, s, -2)
                if inside(b):
                    power1(b + 1, mvb[v], pwb[v], rsb[v], "mv2", "pw2", "rr2")
                    pool.wait_ge(C["ln2"], b + 1)
                    pool.tensor_copy(hs[:, bass.ds(b, 1), :], hb[v][:, :].unsqueeze(1)).then_inc(C["keep"], 1)

            dispatch(0)
            pool.wait_ge(F["out"], 16 * E)
            pipeline(pool, step)
            dispatch(1)
            pool.wait_ge(F["out"], 16 * E * 2)
            for s in range(SLOTS):
                fetch(1, s, s)
            with pool.Fori(1, B // SLOTS) as i:
                for s in range(SLOTS):
                    pool.wait_ge(Z["b"], occ1(i - 1, s))
                    pool.wait_ge(C[f"g{s}"], 32 * (B // SLOTS + i))
                    fetch(1, i * SLOTS + s, s)

        @block.scalar
        def _(act):
            act.wait_ge(w_in, 16 * NWD)
            act.wait_ge(setup_T, 1)
            for j in range(4):
                act.activation(wT[:, j, :], bank[0][:, j * D:(j + 1) * D], ACT.Identity,
                               **({"scale": win[:, 0:1]} if j == 0 else {}))
            for j in range(4):
                at = 4 + j
                act.activation(wT[:, at, :], bank[1][:, j * D:(j + 1) * D], ACT.Identity,
                               **({"scale": float(DK) ** -0.5} if at == W_QQ else {}))
            act.activation(wT[:, 8:11, :], bank[2][:, 0:3 * D].rearrange("p (j d) -> p j d", j=3), ACT.Identity)
            act.activation(wr[0][:, :], bank[3][:, 0:E], ACT.Identity)
            act.activation(b1T[:, :], bank[3][:, 32:64], ACT.Identity)
            act.activation(mT[:, :], bank[3][:, 128:256], ACT.Identity, scale=win[:, 0:1]).then_inc(setup_ev, 1)

            with act.Fori(0, NG) as i:
                for s in range(SLOTS):
                    n = occ1(i, s)
                    act.wait_ge(A[f"ctx_in{s}"], 16 * (i + 1))
                    for b in range(G):
                        last = act.activation(uu[s][0:M, b * D:(b + 1) * D], c_s[s][:, b, :], ACT.Square, scale=float(D) ** -0.5,
                                              accum_out=pwc[s][0:M, b:b + 1])
                    last.then_inc(A["ctx_ms"], 1)
                    act.wait_ge(A["ctx_T"], n)
                    act.activation(cT[s][:, :, :], bank[4 * s + 3][:, 0:G * M].rearrange("p (b m) -> p b m", b=G),
                                   ACT.Identity).then_inc(A["ctx_Tev"], 1)
                for s in range(SLOTS):
                    n = occ1(i, s)
                    act.wait_ge(A["x_T"], n)
                    act.activation(sT[s][:, :], bank[4 * s][:, :], ACT.Identity).then_inc(A["x_Tev"], 1)
                for it in range(ITERS):
                    for s in range(SLOTS):
                        n = occ(i, it, s)
                        act.wait_ge(A["i_tok"], n)
                        for b in range(G):
                            last = act.activation(uu[s][:, b * D:(b + 1) * D], bank[4 * s][:, b * D:(b + 1) * D], ACT.Square,
                                                  scale=float(D) ** -0.5, accum_out=cs[s][:, b:b + 1])
                        last.then_inc(A["i_ms"], 1)
                    for s in range(SLOTS):
                        n = occ(i, it, s)
                        act.wait_ge(A["i_snT"], n)
                        act.activation(snT[s][:, :], bank[4 * s][:, :], ACT.Identity).then_inc(A["i_snTev"], 1)
                    for s in range(SLOTS):
                        n = occ(i, it, s)
                        act.wait_ge(A["i_nb"], n)
                        for b in range(G):
                            last = act.activation(ex[s][:, b, :], bank[4 * s + 1][0:M, b * S:(b + 1) * S], ACT.Exp,
                                                  bias=nb[s][:, b:b + 1], scale=rc[s][0:M, b:b + 1],
                                                  accum_out=sm[s][:, b:b + 1])
                        last.then_inc(A["i_ex"], 1)
                    for s in range(SLOTS):
                        n = occ(i, it, s)
                        act.wait_ge(A["i_uT"], n)
                        act.activation(upT[s][:, :], bank[4 * s + 2][:, :], ACT.Identity).then_inc(A["i_uTev"], 1)
                    for s in range(SLOTS):
                        n = occ(i, it, s)
                        act.wait_ge(A["i_r"], n)
                        act.activation(tr[s][:, :], bank[4 * s][:, :], ACT.Tanh, bias=gb2[:, 0:1], scale=0.5).then_inc(A["i_tr"], 1)
                        act.wait_ge(A["i_z"], n)
                        act.activation(tz[s][:, :], bank[4 * s + 1][:, :], ACT.Tanh, bias=gb2[:, 1:2], scale=0.5).then_inc(A["i_tz"], 1)
                    for s in range(SLOTS):
                        n = occ(i, it, s)
                        act.wait_ge(A["i_q2"], n)
                        act.activation(nn[s][:, :], qn[s][:, :], ACT.Tanh, bias=gbi[:, 2:3]).then_inc(A["i_n"], 1)
                for s in range(SLOTS):
                    n = occ1(i, s)
                    act.wait_ge(A["f_T2"], n)
                    act.activation(snT[s][:, :], bank[4 * s + 1][:, :], ACT.Identity).then_inc(A["f_T2ev"], 1)

            def experts_act(l):
                f = F
                act.wait_ge(f["d"], l + 1)
                act.activation(ge[:, :, :], gt[:, :, :], ACT.Exp).then_inc(f["ex"], 1)
                with act.Fori(0, E // SLOTS) as i:
                    for s in range(SLOTS):
                        n = occ1(i, s) + l * E
                        act.wait_ge(f["T"], n)
                        act.activation(xeT[s][:, 0:512], bank[0][:, :], ACT.Identity)
                        act.activation(xeT[s][:, 512:CAP0], bank[1][:, 0:D], ACT.Identity).then_inc(f["Tev"], 1)
                        for c in range(HC):
                            act.wait_ge(f["h"], n * HC - (HC - 1 - c))
                            bias = {"bias": b1T[:, bass.ds((i * SLOTS + s) * HC + c, 1)]} if l else {}
                            act.activation(hT[s][:, c, CAP0 // 2:CAP0], bank[3 + 2 * (c % 2)][:, 0:CAP0 // 2],
                                           ACT.Relu, **bias).then_inc(f["hevA"], 1)
                        act.wait_ge(f["y"], n)
                        act.activation(ye[:, bass.ds((i * SLOTS + s) * CT, HC), :],
                                       bank[6][:, :].rearrange("p (c d) -> p c d", c=HC), ACT.Identity).then_inc(f["yevA"], 1)

            experts_act(0)

            def exponentials(i, s, g):
                b, v, turn = batch_of(i, s, 0)
                if inside(b):
                    act.wait_ge(C["sub"], b * 4 + g + 1)
                    act.activation(pr[v][:, HG * g:HG * g + HG, :], pr[v][:, HG * g:HG * g + HG, :], ACT.Exp).then_inc(C["ex"], 1)

            def keep_pT(i, s, g):
                b, v, turn = batch_of(i, s, -1)
                if inside(b):
                    act.wait_ge(C["pt"], b * 4 + g + 1)
                    act.activation(pT[v][:, g * 512:(g + 1) * 512], bank[4 + g % 2][0:M, :], ACT.Identity).then_inc(C["pev"], 1)

            def step(i, s):
                exponentials(i, s, 0)
                keep_pT(i, s, 0)
                b, v, turn = batch_of(i, s, 1)
                if inside(b):
                    act.wait_ge(C["T"], b + 1)
                    act.activation(caT[v][:, :], bank[6][:, 0:M], ACT.Identity)
                    act.activation(haT[v][:, :], bank[6][:, D:2 * D], ACT.Identity).then_inc(C["Tev"], 1)
                exponentials(i, s, 1)
                keep_pT(i, s, 1)
                b0, v0, turn0 = batch_of(i, s, 0)
                if inside(b) or inside(b0):
                    act.wait_ge(C["kqv"], b + 1)
                if inside(b):
                    act.activation(qT[v][:, :], bank[6][:, D:2 * D], ACT.Identity)
                    for j in range(HG):
                        last = act.activation(kb[v][:, j, :], bank[6][:, 0:M], ACT.Identity, scale=band[:, j:j + 1])
                if inside(b0):
                    last = act.activation(va[v0][:, :, 0:DK], bank[6][0:M, 2 * D:3 * D].rearrange("p (h d) -> p h d", h=H), ACT.Identity)
                if inside(b) or inside(b0):
                    last.then_inc(C["kqev"], 1)
                exponentials(i, s, 2)
                b, v, turn = batch_of(i, s, -2)
                if inside(b):
                    act.wait_ge(C["oT"], b + 1)
                    act.activation(oT[v][:, :], bank[6][:, 0:S], ACT.Identity).then_inc(C["oTev"], 1)
                keep_pT(i, s, 2)
                exponentials(i, s, 3)
                keep_pT(i, s, 3)
                if inside(b):
                    act.wait_ge(C["T2"], b + 1)
                    act.activation(hbT[v][:, :], bank[6][:, 0:S], ACT.Identity).then_inc(C["T2ev"], 1)
            pipeline(act, step)
            experts_act(1)

        @block.tensor
        def _(pe):
            pe.wait_ge(w_in, 16 * NWD)
            pe.wait_ge(k_pool, K_POOL)
            for j in range(11):
                pe.transpose(bank[j // 4][:, (j % 4) * D:(j % 4 + 1) * D], raw[:, j, :], ident[:, :])
            pe.transpose(bank[3][:, 0:E], small[:, :], ident[0:E, 0:E])
            pe.transpose(bank[3][:, 32:64], b1raw[:, :], ident[0:32, 0:32])
            pe.matmul(bank[3][:, 128:256], wqk[:, 1, :], wqk[:, 0, :], start=True, stop=True).then_inc(setup_T, 1)
            pe.wait_ge(setup_ev, 1)
            with pe.Fori(0, NG) as i:
                for s in range(SLOTS):
                    n = occ1(i, s)
                    b0, b1, b2, b3 = bank[4 * s:4 * s + 4]
                    pe.wait_ge(A[f"ctx_in{s}"], 16 * (i + 1))
                    for b in range(G):
                        last = pe.transpose(b3[:, b * M:(b + 1) * M], c_s[s][:, b, :], ident[0:M, 0:M])
                    last.then_inc(A["ctx_T"], 1)
                for s in range(SLOTS):
                    n = occ1(i, s)
                    b0, b1, b2, b3 = bank[4 * s:4 * s + 4]
                    pe.wait_ge(A["x_ln"], n)
                    for b in range(G):
                        last = pe.transpose(b0[:, b * S:(b + 1) * S], tok[s][:, b, :], ident[:, :])
                    last.then_inc(A["x_T"], 1)
                    pe.wait_ge(A["ctx_Tev"], n)
                    pe.matmul(b2[:, 0:G * M], mT[:, :], cT[s][:, :, :].rearrange("p b m -> p (b m)"),
                              start=True, stop=True).then_inc(A["ctx_G"], 1)
                    for b in range(G):
                        last = pe.matmul(b3[0:M, b * D:(b + 1) * D], cT[s][:, b, :], wT[:, W_V, :], start=True, stop=True)
                    last.then_inc(A["ctx_V"], 1)
                for it in range(ITERS):
                    for s in range(SLOTS):
                        n = occ(i, it, s)
                        b0, b1, b2, b3 = bank[4 * s:4 * s + 4]
                        if it == 0:
                            pe.wait_ge(A["x_Tev"], occ1(i, s))
                            pe.wait_ge(A["ctx_Vev"], occ1(i, s))
                            pe.wait_ge(A["ctx_Gev"], occ1(i, s))
                        else:
                            pe.wait_ge(A["i_s"], n - SLOTS)
                        for b in range(G):
                            last = pe.transpose(b0[:, b * D:(b + 1) * D], sT[s][:, b * S:(b + 1) * S], ident[:, :])
                        last.then_inc(A["i_tok"], 1)
                        pe.matmul(b3[:, :], wT[:, W_HH + 2, :], sT[s][:, :], start=True, stop=True).then_inc(A["i_hn"], 1)
                    for s in range(SLOTS):
                        n = occ(i, it, s)
                        b0 = bank[4 * s]
                        pe.wait_ge(A["i_sn"], n)
                        for b in range(G):
                            last = pe.transpose(b0[:, b * S:(b + 1) * S], tok[s][:, b, :], ident[:, :])
                        last.then_inc(A["i_snT"], 1)
                    for s in range(SLOTS):
                        n = occ(i, it, s)
                        b0, b1, b2, b3 = bank[4 * s:4 * s + 4]
                        pe.wait_ge(A["i_snTev"], n)
                        for b in range(G):
                            last = pe.matmul(b1[0:M, b * S:(b + 1) * S], g_s[s][:, b, :], snT[s][:, b * S:(b + 1) * S],
                                             start=True, stop=True)
                        last.then_inc(A["i_sc"], 1)
                        pe.matmul(b0[:, :], wT[:, W_HH, :], sT[s][:, :], start=True, stop=False)
                    for s in range(SLOTS):
                        n = occ(i, it, s)
                        b0, b1, b2, b3 = bank[4 * s:4 * s + 4]
                        pe.wait_ge(A["i_vr"], n)
                        for b in range(G):
                            pe.matmul(b2[:, b * D:(b + 1) * D], ex[s][:, b, :], vr_s[s][:, b, 0:D], start=True, stop=True)
                            last = pe.matmul(b1[:, b:b + 1], ex[s][:, b, :], vr_s[s][:, b, D:D + 1], start=True, stop=True)
                        last.then_inc(A["i_u"], 1)
                    for s in range(SLOTS):
                        n = occ(i, it, s)
                        b0, b1, b2, b3 = bank[4 * s:4 * s + 4]
                        pe.wait_ge(A["i_cs"], n)
                        pe.matmul(b1[:, :], wT[:, W_HH + 1, :], sT[s][:, :], start=True, stop=False)
                        pe.wait_ge(A["i_ut"], n)
                        for b in range(G):
                            last = pe.transpose(b2[:, b * S:(b + 1) * S], tok[s][:, b, :], ident[:, :])
                        last.then_inc(A["i_uT"], 1)
                    for s in range(SLOTS):
                        n = occ(i, it, s)
                        b0, b1, b2, b3 = bank[4 * s:4 * s + 4]
                        pe.wait_ge(A["i_uTev"], n)
                        pe.matmul(b0[:, :], wT[:, W_IH, :], upT[s][:, :], start=False, stop=True).then_inc(A["i_r"], 1)
                        pe.matmul(b2[:, :], wT[:, W_IH + 2, :], upT[s][:, :], start=True, stop=True).then_inc(A["i_xn"], 1)
                        pe.matmul(b1[:, :], wT[:, W_IH + 1, :], upT[s][:, :], start=False, stop=True).then_inc(A["i_z"], 1)
                for s in range(SLOTS):
                    n = occ1(i, s)
                    b0, b1, b2, b3 = bank[4 * s:4 * s + 4]
                    pe.wait_ge(A["i_s"], occ(i, ITERS - 1, s))
                    for b in range(G):
                        last = pe.transpose(b0[:, b * D:(b + 1) * D], sT[s][:, b * S:(b + 1) * S], ident[:, :])
                    last.then_inc(A["f_T"], 1)
                for s in range(SLOTS):
                    n = occ1(i, s)
                    b0, b1, b2, b3 = bank[4 * s:4 * s + 4]
                    pe.wait_ge(A["f_ln"], n)
                    for b in range(G):
                        last = pe.transpose(b1[:, b * S:(b + 1) * S], tok[s][:, b, :], ident[:, :])
                    last.then_inc(A["f_T2"], 1)
                for s in range(SLOTS):
                    n = occ1(i, s)
                    b0, b1, b2, b3 = bank[4 * s:4 * s + 4]
                    pe.wait_ge(A["f_T2ev"], n)
                    for b in range(G):
                        last = pe.matmul(b2[:, b * E:(b + 1) * E], snT[s][:, b * S:(b + 1) * S], wr[0][:, :], start=True, stop=True)
                    last.then_inc(A["f_lg"], 1)

            def experts_pe(l):
                f = F
                pe.wait_ge(f["pos"], l + 1)
                pe.matmul(bank[0][:, 0:E * B], before[:, :], gmb[:, :, :].rearrange("p e b -> p (e b)"), start=True, stop=True)
                pe.matmul(bank[1][:, 0:E * B], ones_bf[:, :], gmb[:, :, :].rearrange("p e b -> p (e b)"), start=True,
                          stop=True).then_inc(f["posr"], 1)
                pe.wait_ge(f["tot"], l + 1)
                with pe.Fori(0, E // SLOTS) as i:
                    for s in range(SLOTS):
                        n = occ1(i, s) + l * E
                        pe.wait_ge(f[f"in{s}"], 16 * (i + 1) + l * (16 * E // SLOTS))
                        for c in range(CT):
                            last = pe.transpose(bank[c // 4][:, (c % 4) * D:(c % 4 + 1) * D], xe[s][:, c, :], ident[:, :])
                        last.then_inc(f["T"], 1)
                        pe.wait_ge(f["Tev"], n)
                        pe.wait_ge(f[f"w{s}"], 32 * (i + 1) + l * (32 * E // SLOTS))
                        for c in range(HC):
                            if c >= 2:
                                pe.wait_ge(f["hevD"], n * HC - (HC - 1 - (c - 2)))
                                pe.wait_ge(f["hevA"], n * HC - (HC - 1 - (c - 2)))
                            for j in range(2):
                                last = pe.matmul(bank[2 + 2 * (c % 2) + j][:, 0:CAP0 // 2], w1[s][:, c * 128:(c + 1) * 128],
                                                 xeT[s][:, j * (CAP0 // 2):(j + 1) * (CAP0 // 2)], start=True, stop=True)
                            last.then_inc(f["h"], 1)
                        pe.wait_ge(f["hevD"], n * HC)
                        pe.wait_ge(f["hevA"], n * HC)
                        for r in range(CT):
                            o = bank[6 + r // 4][:, (r % 4) * D:(r % 4 + 1) * D]
                            if l:
                                pe.matmul(o, ones_row[:, :], b2r[:, bass.ds((i * SLOTS + s) * D, D)], start=True, stop=False)
                            for c in range(HC):
                                last = pe.matmul(o, hT[s][:, c, r * 128:(r + 1) * 128], w2[s][:, c, :],
                                                 start=(c == 0 and not l), stop=(c == HC - 1))
                        last.then_inc(f["y"], 1)

            experts_pe(0)

            def scores(i, s, g):
                b, v, turn = batch_of(i, s, 0)
                if inside(b):
                    if g == 0:
                        pe.wait_ge(C["kqev"], b + 1)
                        pe.wait_ge(C["mb"], b + 1)
                    if not isinstance(b, int) or b:
                        pe.wait_ge(C["sub"], b * 4 + g - 3)
                    pe.matmul(bank[g][:, 0:HG * M], qT[v][32 * g:32 * g + 32, :],
                              kb[v][32 * g:32 * g + 32, :, :].rearrange("p j m -> p (j m)"), start=True, stop=False)
                    pe.matmul(bank[g][:, 0:HG * M], ident_bf[:, :], mb[v][:, :].unsqueeze(1).to_broadcast([128, HG, M]),
                              start=False, stop=True).then_inc(C["s"], 1)

            def turned(i, s, g):
                b, v, turn = batch_of(i, s, -1)
                if inside(b):
                    pe.wait_ge(C["ex"], b * 4 + g + 1)
                    for h in range(HG):
                        last = pe.transpose(bank[4 + g % 2][0:M, h * S:(h + 1) * S], pr[v][:, HG * g + h, :], ident[:, :])
                    last.then_inc(C["pt"], 1)

            def products(i, s, k, g):
                b, v, turn = batch_of(i, s, k)
                if inside(b):
                    pe.wait_ge(C["pev"], b * 4 + g + 1)
                    for h in range(HG * g, HG * g + HG):
                        last = pe.matmul(bank[7][:, h * (DK + 1):(h + 1) * (DK + 1)], pT[v][:, h * S:(h + 1) * S], va[v][:, h, :],
                                         start=True, stop=True)
                    if g == 3:
                        last.then_inc(C["pv"], 1)

            def step(i, s):
                scores(i, s, 0)
                b, v, turn = batch_of(i, s, -3)
                if inside(b):
                    pe.wait_ge(C["T2ev"], b + 1)
                    pe.matmul(bank[6][:, 0:E], hbT[v][:, :], wr[1][:, :], start=True, stop=True).then_inc(C["lg"], 1)
                products(i, s, -2, 3)
                turned(i, s, 0)
                b1, v1, turn1 = batch_of(i, s, 1)
                if inside(b1):
                    if inside(b):
                        pe.wait_ge(C["lgev"], b + 1)
                    pe.wait_ge(C[f"in{v1}"], 32 * (turn1 + 1))
                    pe.wait_ge(C["ln"], b1 + 1)
                    pe.transpose(bank[6][:, 0:M], ca[v1][:, :], ident[0:M, 0:M])
                    pe.transpose(bank[6][:, D:2 * D], ha[v1][:, :], ident[:, :]).then_inc(C["T"], 1)
                scores(i, s, 1)
                turned(i, s, 1)
                b0, v0, turn0 = batch_of(i, s, 0)
                if inside(b1):
                    pe.wait_ge(C["Tev"], b1 + 1)
                    pe.matmul(bank[6][:, 0:M], wT[:, W_KK, :], caT[v1][:, :], start=True, stop=True)
                    last = pe.matmul(bank[6][:, D:2 * D], wT[:, W_QQ, :], haT[v1][:, :], start=True, stop=True)
                if inside(b0):
                    if not inside(b1):
                        pe.wait_ge(C["lgev"], b + 1)
                    last = pe.matmul(bank[6][0:M, 2 * D:3 * D], caT[v0][:, :], wT[:, W_VV, :], start=True, stop=True)
                if inside(b1) or inside(b0):
                    last.then_inc(C["kqv"], 1)
                scores(i, s, 2)
                b, v, turn = batch_of(i, s, -2)
                if inside(b):
                    if inside(b1) or inside(b0):
                        pe.wait_ge(C["kqev"], b1 + 1)
                    elif b:
                        pe.wait_ge(C["lgev"], b)
                    pe.wait_ge(C["o"], b + 1)
                    pe.transpose(bank[6][:, 0:S], oa[v][:, :], ident[:, :]).then_inc(C["oT"], 1)
                products(i, s, -1, 0)
                products(i, s, -1, 1)
                if inside(b):
                    pe.wait_ge(C["oTev"], b + 1)
                    pe.matmul(bank[6][:, 0:D], oT[v][:, :], wT[:, W_OO, :], start=True, stop=True).then_inc(C["w"], 1)
                turned(i, s, 2)
                scores(i, s, 3)
                turned(i, s, 3)
                products(i, s, -1, 2)
                if inside(b):
                    pe.wait_ge(C["ln2"], b + 1)
                    pe.transpose(bank[6][:, 0:S], hb[v][:, :], ident[:, :]).then_inc(C["T2"], 1)
            pipeline(pe, step)
            experts_pe(1)

        @block.vector
        def _(dve):
            dve.wait_ge(w_in, 16 * NWD)
            dve.tensor_tensor(gb2[:, :], gbi[:, 0:2], gbh[:, 0:2], ALU.add).then_inc(setup_m, 1)
            dve.wait_ge(setup_m, 1)
            dve.tensor_scalar(gb2[:, :], gb2[:, :], 0.5, None, ALU.mult).then_inc(setup_m, 1)
            dve.tensor_scalar(wslot[:, :], wslot[:, :], float(D) ** -0.5, None, ALU.mult).then_inc(setup_m, 1)
            dve.wait_ge(setup_m, 3)
            dve.wait_ge(k_pool, K_POOL)
            dve.tensor_reduce(band[:, :], ident[:, :].rearrange("p (c j d) -> p j c d", j=HG, d=DK), AX.XY, ALU.add).then_inc(setup_m, 1)

            def ln(src, s, n, st_n, mv_n, rr_n, ln_n):
                dve.to_reg(n)
                for b in range(G):
                    last = dve.bn_stats(st[s][:, 6 * b:6 * b + 6], src[:, b, :])
                last.then_inc(A[st_n], 1)
                dve.wait_ge(k_pool, K_POOL)
                dve.wait_ge(A[st_n], n)
                for b in range(G):
                    last = dve.bn_aggr(mv[s][:, b, :], st[s][:, 6 * b:6 * b + 6])
                last.then_inc(A[mv_n], 1)

            def ln_out(src, s, n, rr_n, ln_n, mv_n):
                dve.wait_ge(A[mv_n], n)
                dve.wait_ge(A[rr_n], n)
                for b in range(G):
                    last = dve.tensor_scalar(tok[s][:, b, :], src[:, b, :], mv[s][:, b, 0:1], rs[s][:, b:b + 1],
                                             ALU.subtract, ALU.mult)
                last.then_inc(A[ln_n], 1)

            with dve.Fori(0, NG) as i:
                for s in range(SLOTS):
                    n = occ1(i, s)
                    dve.wait_ge(A[f"x_in{s}"], 16 * (i + 1))
                    ln(x_s[s], s, n, "x_st", "x_mv", "x_rr", "x_ln")
                for s in range(SLOTS):
                    n = occ1(i, s)
                    ln_out(x_s[s], s, n, "x_rr", "x_ln", "x_mv")
                for s in range(SLOTS):
                    n = occ1(i, s)
                    b0, b1, b2, b3 = bank[4 * s:4 * s + 4]
                    dve.wait_ge(A["ctx_G"], n)
                    dve.tensor_scalar(g_s[s][:, :, :].rearrange("p b m -> p (b m)"), b2[:, 0:G * M], wslot[:, 0:1], None,
                                      ALU.mult).then_inc(A["ctx_Gev"], 1)
                    dve.wait_ge(A["ctx_rr"], n)
                    dve.wait_ge(A["ctx_V"], n)
                    for b in range(G):
                        last = dve.tensor_scalar(v_s[s][:, b, 0:D], b3[0:M, b * D:(b + 1) * D], rc[s][0:M, b:b + 1], None, ALU.mult)
                    last.then_inc(A["ctx_Vev"], 1)
                for it in range(ITERS):
                    for s in range(SLOTS):
                        n = occ(i, it, s)
                        b0 = bank[4 * s]
                        dve.wait_ge(A["i_rr"], n)
                        for b in range(G):
                            last = dve.tensor_scalar(tok[s][:, b, :], b0[:, b * D:(b + 1) * D], rs[s][:, b:b + 1], None, ALU.mult)
                        last.then_inc(A["i_sn"], 1)
                    for s in range(SLOTS):
                        n = occ(i, it, s)
                        b1 = bank[4 * s + 1]
                        dve.wait_ge(A["i_sc"], n)
                        dve.tensor_reduce(mx[s][:, :], b1[0:M, :].rearrange("p (b k) -> p b k", b=G), AX.X, ALU.max).then_inc(A["i_mx"], 1)
                        dve.wait_ge(A["i_mx"], n)
                        dve.scalar_tensor_tensor(out=nb[s][:, :], in0=mx[s][:, :], scalar=-1.0, in1=rc[s][0:M, :],
                                                 op0=ALU.mult, op1=ALU.mult).then_inc(A["i_nb"], 1)
                    for s in range(SLOTS):
                        n = occ(i, it, s)
                        dve.wait_ge(A["i_ex"], n)
                        dve.reciprocal(rm[s][:, :], sm[s][:, :]).then_inc(A["i_rm"], 1)
                        dve.wait_ge(A["i_rm"], n)
                        if it == 0:
                            dve.wait_ge(A["ctx_Vev"], occ1(i, s))
                        for b in range(G):
                            last = dve.tensor_scalar(vr_s[s][:, b, :], v_s[s][:, b, :], rm[s][:, b:b + 1], None, ALU.mult)
                        last.then_inc(A["i_vr"], 1)
                    for s in range(SLOTS):
                        n = occ(i, it, s)
                        b1, b2 = bank[4 * s + 1], bank[4 * s + 2]
                        dve.wait_ge(A["i_u"], n)
                        dve.tensor_scalar(cs[s][:, :], b1[:, 0:G], EPS_RMS, None, ALU.add).then_inc(A["i_cs"], 1)
                        dve.wait_ge(A["i_cs"], n)
                        dve.reciprocal(ci[s][:, :], cs[s][:, :]).then_inc(A["i_ci"], 1)
                        dve.wait_ge(A["i_ci"], n)
                        for b in range(G):
                            last = dve.tensor_scalar(tok[s][:, b, :], b2[:, b * D:(b + 1) * D], ci[s][:, b:b + 1], None, ALU.mult)
                        last.then_inc(A["i_ut"], 1)
                    for s in range(SLOTS):
                        n = occ(i, it, s)
                        b2, b3 = bank[4 * s + 2], bank[4 * s + 3]
                        dve.wait_ge(A["i_tr"], n)
                        dve.tensor_scalar(tr[s][:, :], tr[s][:, :], 0.5, 0.5, ALU.mult, ALU.add).then_inc(A["i_r2"], 1)
                        dve.wait_ge(A["i_r2"], n)
                        dve.wait_ge(A["i_hn"], n)
                        dve.scalar_tensor_tensor(out=qn[s][:, :], in0=b3[:, :], scalar=gbh[:, 2:3], in1=tr[s][:, :],
                                                 op0=ALU.add, op1=ALU.mult).then_inc(A["i_q"], 1)
                        dve.wait_ge(A["i_q"], n)
                        dve.wait_ge(A["i_xn"], n)
                        dve.tensor_tensor(qn[s][:, :], b2[:, :], qn[s][:, :], ALU.add).then_inc(A["i_q2"], 1)
                for s in range(SLOTS):
                    n = occ1(i, s)
                    dve.wait_ge(A["f_T"], n)
                    dve.tensor_tensor(x_s[s][:, :, :], bank[4 * s][:, :].rearrange("p (b d) -> p b d", b=G),
                                      x_s[s][:, :, :], ALU.add).then_inc(A["f_x"], 1)
                    dve.wait_ge(A["f_x"], n)
                    ln(x_s[s], s, n, "f_st", "f_mv", "f_rr", "f_ln")
                for s in range(SLOTS):
                    ln_out(x_s[s], s, occ1(i, s), "f_rr", "f_ln", "f_mv")
                for s in range(SLOTS):
                    n = occ1(i, s)
                    dve.wait_ge(A["f_lg"], n)
                    dve.tensor_tensor(lg[:, bass.ds((i * SLOTS + s) * G, G), :],
                                      bank[4 * s + 2][:, 0:G * E].rearrange("p (b e) -> p b e", b=G),
                                      br[0][:, :].unsqueeze(1).to_broadcast([128, G, E]), ALU.add).then_inc(A["f_lgev"], 1)

            def route(l, logits_n):
                f = F
                cap = float(CAP0 if l == 0 else CAP1)
                steps = route_steps

                def step(ins):
                    steps[0] += 1
                    ins.then_inc(f["dd"], 1)
                    dve.wait_ge(f["dd"], steps[0])

                def wide(a):
                    return a[:, :].unsqueeze(2).to_broadcast([128, B, E])

                def by_batch(a):
                    return a[:, :, :].rearrange("p e b -> p b e")
                dve.wait_ge((A["f_lgev"] if l == 0 else C["lgev"]), logits_n)
                step(dve.tensor_reduce(gx[:, :], lg[:, :, :], AX.X, ALU.max))
                dve.tensor_tensor(gt[:, :, :], lg[:, :, :], wide(gx), ALU.subtract).then_inc(f["d"], 1)
                for k in range(2):
                    step(dve.tensor_tensor(gw[:, :, :], lg[:, :, :], wide(gx), ALU.is_equal))
                    step(dve.tensor_tensor(gw[:, :, :], gw[:, :, :], eight[:, :, :], ALU.mult))
                    step(dve.tensor_reduce(g1[:, :], gw[:, :, :], AX.X, ALU.max))
                    step(dve.tensor_tensor(by_batch(gm[k]), gw[:, :, :], wide(g1), ALU.is_equal))
                    if k == 0:
                        step(dve.scalar_tensor_tensor(out=lg[:, :, :], in0=by_batch(gm[0]), scalar=-BIG, in1=lg[:, :, :],
                                                      op0=ALU.mult, op1=ALU.add))
                        step(dve.tensor_reduce(gx[:, :], lg[:, :, :], AX.X, ALU.max))
                dve.wait_ge(f["ex"], l + 1)
                step(dve.tensor_reduce(gx[:, :], ge[:, :, :], AX.X, ALU.add))
                step(dve.reciprocal(g1[:, :], gx[:, :]))
                step(dve.tensor_tensor(ge[:, :, :], ge[:, :, :], wide(g1), ALU.mult))
                if l == 0:
                    step(dve.scalar_tensor_tensor(out=by_batch(gv), in0=ge[:, :, :], scalar=0.0, in1=by_batch(gm[1]),
                                                  op0=ALU.is_gt, op1=ALU.mult))
                    step(dve.tensor_tensor(gmb[:, :, :], gm[0][:, :, :], gv[:, :, :], ALU.add))
                else:
                    step(dve.tensor_tensor(gmb[:, :, :], gm[0][:, :, :], gm[1][:, :, :], ALU.add))
                dve.tensor_copy(gx[:, :], g1[:, :]).then_inc(f["pos"], 1)
                dve.wait_ge(f["posr"], l + 1)
                pos = bank[0][:, 0:E * B].rearrange("p (e b) -> p e b", e=E)
                tot = bank[1][:, 0:E * B].rearrange("p (e b) -> p e b", e=E)
                if l == 0:
                    step(dve.tensor_copy(gv[:, :, :], tot))
                    step(dve.tensor_tensor_scan(gp[:, :, :].rearrange("p e b -> p (e b)"), chain[:, :, :].rearrange("p e b -> p (e b)"),
                                                gv[:, :, :].rearrange("p e b -> p (e b)"), 0.0, ALU.mult, ALU.add))
                    step(dve.tensor_tensor(gp[:, :, :], gp[:, :, :], gv[:, :, :], ALU.subtract))
                    step(dve.tensor_tensor(gp[:, :, :], pos, gp[:, :, :], ALU.add))
                else:
                    step(dve.tensor_copy(gp[:, :, :], pos))
                dve.tensor_scalar(gv[:, :, :], gp[:, :, :], cap, float(2 * ROWS), ALU.is_ge, ALU.mult).then_inc(f["tot"], 1)
                step(dve.tensor_tensor(gp[:, :, :], gp[:, :, :], base[l][:, :, :], ALU.add))
                step(dve.tensor_tensor(gp[:, :, :], gp[:, :, :], gv[:, :, :], ALU.add))
                for k in range(2):
                    step(dve.tensor_tensor(gv[:, :, :], gp[:, :, :], gm[k][:, :, :], ALU.mult))
                    step(dve.tensor_reduce(sl[k][:, :], by_batch(gv), AX.X, ALU.add))
                    step(dve.tensor_tensor(gw[:, :, :], ge[:, :, :], by_batch(gm[k]), ALU.mult))
                    step(dve.tensor_reduce(g1[:, :], gw[:, :, :], AX.X, ALU.add))
                    if l == 0:
                        step(dve.tensor_scalar(gx[:, :], g1[:, :], 0.0, float(2 * ROWS), ALU.is_le, ALU.mult))
                        step(dve.tensor_tensor(sl[k][:, :], sl[k][:, :], gx[:, :], ALU.add))
                    step(dve.tensor_copy(slot_i[:, k, :], sl[k][:, :]))
                    step(dve.scalar_tensor_tensor(out=gate[:, k, :], in0=sl[k][:, :], scalar=float(ROWS), in1=g1[:, :],
                                                  op0=ALU.is_lt, op1=ALU.mult))
                dve.tensor_copy(g1[:, :], gx[:, :]).then_inc(f["slot"], 1)

            def experts_dve(l):
                f = F
                with dve.Fori(0, E // SLOTS) as i:
                    for s in range(SLOTS):
                        n = occ1(i, s) + l * E
                        for c in range(HC):
                            dve.wait_ge(f["h"], n * HC - (HC - 1 - c))
                            if l:
                                last = dve.tensor_scalar(hT[s][:, c, 0:CAP0 // 2], bank[2 + 2 * (c % 2)][:, 0:CAP0 // 2],
                                                         b1T[:, bass.ds((i * SLOTS + s) * HC + c, 1)], 0.0, ALU.add, ALU.max)
                            else:
                                last = dve.tensor_scalar(hT[s][:, c, 0:CAP0 // 2], bank[2 + 2 * (c % 2)][:, 0:CAP0 // 2],
                                                         0.0, None, ALU.max)
                            last.then_inc(f["hevD"], 1)
                        dve.wait_ge(f["y"], n)
                        dve.tensor_copy(ye[:, bass.ds((i * SLOTS + s) * CT + HC, 1), :],
                                        bank[7][:, 0:D].unsqueeze(1)).then_inc(f["yevD"], 1)

            def scaled(k, b, v, x):
                return dict(in0=yg[v][:, k, :], scalar=gate[:, k, bass.ds(b, 1)], in1=x, op0=ALU.mult, op1=ALU.add)

            def kept(b):
                return xs[:, bass.ds(b, 1), :].rearrange("p a d -> p (a d)")

            def stats(b, st, mv, s_x, s_st, s_mv):
                dve.to_reg(b + 1)
                dve.wait_ge(k_pool, K_POOL)
                dve.wait_ge(C[s_x], b + 1)
                dve.bn_stats(st[:, :], kept(b)).then_inc(C[s_st], 1)
                dve.wait_ge(k_pool, K_POOL)
                dve.wait_ge(C[s_st], b + 1)
                dve.bn_aggr(mv[:, :], st[:, :]).then_inc(C[s_mv], 1)

            def shifted(i, s, g):
                b, v, turn = batch_of(i, s, 0)
                if inside(b):
                    n = b * 4 + g + 1
                    sc = bank[g][:, 0:HG * M].rearrange("p (h m) -> p h m", h=HG)
                    hd = slice(HG * g, HG * g + HG)
                    dve.wait_ge(C["s"], n)
                    dve.tensor_reduce(mxa[v][:, hd], sc, AX.X, ALU.max).then_inc(C["mx"], 1)
                    dve.wait_ge(C["mx"], n)
                    dve.tensor_scalar(nm[v][:, hd], mxa[v][:, hd], -BIG / 10, None, ALU.max).then_inc(C["nm"], 1)
                    dve.wait_ge(C["nm"], n)
                    dve.tensor_tensor(pr[v][:, hd, :], sc, nm[v][:, hd].unsqueeze(2).to_broadcast([128, HG, M]),
                                      ALU.subtract).then_inc(C["sub"], 1)

            def step(i, s):
                shifted(i, s, 0)
                b, v, turn = batch_of(i, s, -3)
                if inside(b):
                    dve.wait_ge(C["lg"], b + 1)
                    dve.tensor_tensor(lg[:, bass.ds(b, 1), :], bank[6][:, 0:E].unsqueeze(1),
                                      br[1][:, :].unsqueeze(1), ALU.add).then_inc(C["lgev"], 1)
                b, v, turn = batch_of(i, s, -2)
                if inside(b):
                    o = bank[7][:, 0:H * (DK + 1)].rearrange("p (h d) -> p h d", h=H)
                    dve.wait_ge(C["pv"], b + 1)
                    dve.tensor_scalar(den[v][:, :].unsqueeze(2), o[:, :, DK:DK + 1], 1.0e-30, None, ALU.max).then_inc(C["den"], 1)
                    dve.wait_ge(C["den"], b + 1)
                    dve.reciprocal(rden[v][:, :], den[v][:, :]).then_inc(C["rd"], 1)
                    dve.wait_ge(C["rd"], b + 1)
                    dve.tensor_tensor(oa[v][:, :].rearrange("p (h d) -> p h d", h=H), o[:, :, 0:DK],
                                      rden[v][:, :].unsqueeze(2).to_broadcast([128, H, DK]), ALU.mult).then_inc(C["o"], 1)
                shifted(i, s, 1)
                b, v, turn = batch_of(i, s, 1)
                if inside(b):
                    dve.wait_ge(C[f"in{v}"], 32 * (turn + 1))
                    dve.tensor_scalar(mb[v][:, :], mk[v][:, :], 0.0, -BIG, ALU.is_equal, ALU.mult).then_inc(C["mb"], 1)
                b, v, turn = batch_of(i, s, 2)
                if inside(b):
                    dve.wait_ge(C[f"g{v}"], 32 * (turn + 1))
                    dve.scalar_tensor_tensor(out=kept(b), **scaled(0, b, v, kept(b))).then_inc(C["x1"], 1)
                    dve.wait_ge(C["x1"], b + 1)
                    dve.scalar_tensor_tensor(out=kept(b), **scaled(1, b, v, kept(b))).then_inc(C["x2"], 1)
                    stats(b, sta[v], mva[v], "x2", "st", "mv")
                shifted(i, s, 2)
                b, v, turn = batch_of(i, s, -2)
                if inside(b):
                    dve.wait_ge(C["w"], b + 1)
                    dve.tensor_tensor(kept(b), bank[6][:, 0:D], kept(b), ALU.add).then_inc(C["x3"], 1)
                    stats(b, stb[v], mvb[v], "x3", "st2", "mv2")
                shifted(i, s, 3)
                b2, v2, turn2 = batch_of(i, s, 2)
                if inside(b2):
                    dve.wait_ge(C["mv"], b2 + 1)
                    dve.wait_ge(C["rr"], b2 + 1)
                    dve.tensor_scalar(ha[v2][:, :], kept(b2), mva[v2][:, 0:1], rsa[v2][:, :],
                                      ALU.subtract, ALU.mult).then_inc(C["ln"], 1)
                if inside(b):
                    dve.wait_ge(C["mv2"], b + 1)
                    dve.wait_ge(C["rr2"], b + 1)
                    dve.tensor_scalar(hb[v][:, :], kept(b), mvb[v][:, 0:1], rsb[v][:, :],
                                      ALU.subtract, ALU.mult).then_inc(C["ln2"], 1)

            route(0, B // G)
            experts_dve(0)
            pipeline(dve, step)
            route(1, B)
            experts_dve(1)
            with dve.Fori(0, B // SLOTS) as i:
                for s in range(SLOTS):
                    b = i * SLOTS + s
                    dve.wait_ge(C[f"g{s}"], 32 * (B // SLOTS + i + 1))
                    dve.scalar_tensor_tensor(out=kept(b), **scaled(0, b, s, kept(b))).then_inc(C["x1"], 1)
                    dve.wait_ge(C["x1"], B + b + 1)
                    dve.scalar_tensor_tensor(out=kept(b), **scaled(1, b, s, kept(b))).then_inc(Z["b"], 1)


_INS = ['x', 'ctx_1024', 'mask_Bx1xSxS2_ik0', 'L0_xattn_Wq', 'L0_xattn_Wk', 'L0_xattn_Wv', 'L0_xattn_gru_wih',
        'L0_xattn_gru_whh', 'L0_xattn_gru_bih', 'L0_xattn_gru_bhh', 'L0_xattn_slot_norm_w',
        'L0_xattn_input_norm_w', 'L0_ffn_W_router', 'L0_ffn_b_router', 'L0_ffn_experts_inter',
        'L0_ffn_experts_out', 'L1_xattn_W_Q', 'L1_xattn_W_K', 'L1_xattn_W_V', 'L1_xattn_W_O', 'L1_ffn_Wr',
        'L1_ffn_br', 'L1_ffn_W1', 'L1_ffn_b1', 'L1_ffn_W2', 'L1_ffn_b2']


def kernel(**inputs):
    import numpy as _np
    import concourse.bacc as _bacc
    from concourse import mybir as _mybir
    from concourse.bass_utils import run_bass_kernel_spmd as _run

    nc = _bacc.Bacc("TRN2", target_bir_lowering=False, num_devices=1)
    arrays, args = {}, {}
    for name in _INS:
        a = _np.ascontiguousarray(inputs[name])
        arrays[f"in_{name}_dram"] = a
        args[name] = nc.dram_tensor(f"in_{name}_dram", a.shape, _mybir.dt.from_np(a.dtype), kind="ExternalInput").ap()
    out = nc.dram_tensor("out_0_dram", (B, S, D), F32, kind="ExternalOutput").ap()
    build(nc, args, out)
    r = _run(nc, [arrays], core_ids=[0])
    return r.results[0]["out_0_dram"]
```

```python
from contextlib import ExitStack

import concourse.bass as bass
from concourse import mybir

F32 = mybir.dt.float32
BF16 = mybir.dt.bfloat16
I32 = mybir.dt.int32
ALU = mybir.AluOpType
ACT = mybir.ActivationFunctionType
AX = mybir.AxisListType.X

B, S, D = 32, 128, 128
M = 120
G = 4
SLOTS = 2
NG = B // G // SLOTS
ITERS = 3
E, HID = 8, 512
HC = HID // 128
CAP0 = 640
CAP1 = 20
ROWS = E * CAP0
ROWS1 = E * CAP1
HR = ROWS1 // 2
CT = CAP0 // 128
H, DK = 16, 8
HG = 4
BIG = 1.0e30
EPS_LN, EPS_RMS = 1e-5, 1e-6


def build(nc, t, out):
    ctx = ExitStack()
    with ctx:
        def sb(name, shape, dt=F32, of=ctx):
            return of.enter_context(nc.sbuf_tensor(name, shape, dt))

        def sem(name):
            return ctx.enter_context(nc.semaphore(name))

        def sems(names):
            return {n: sem("s_" + n) for n in names.split()}

        rows_d = nc.dram_tensor("rows", [ROWS, D], F32, kind="Internal").ap()
        res_d = [nc.dram_tensor(f"res{l}", [ROWS, D], F32, kind="Internal").ap() for l in range(2)]

        bank = [ctx.enter_context(nc.psum_tensor(f"bank{i}", [128, 512], F32)) for i in range(8)]

        ident = sb("ident", [128, 128])
        ident_bf = sb("ident_bf", [128, 128], BF16)
        ones_bf = sb("ones_bf", [128, 128], BF16)
        before = sb("before", [128, 128], BF16)
        band = sb("band", [128, HG])
        iota_row = sb("iota_row", [128, ROWS1])
        minus_half = sb("minus_half", [128, G])
        eps_ln = sb("eps_ln", [128, G])
        eps_rms = sb("eps_rms", [128, G])
        raw = sb("raw", [128, 11, D])
        wqk = sb("wqk", [128, 2, D])
        small = sb("small", [E, D])
        b1raw = sb("b1raw", [32, 128])
        wT = sb("wT", [128, 11, D])
        mT = sb("mT", [128, D])
        wr = [sb(f"wr{l}", [128, E]) for l in range(2)]
        br = [sb(f"br{l}", [128, E]) for l in range(2)]
        b1T = sb("b1T", [128, E * HC])
        win = sb("win", [128, 1])
        wslot = sb("wslot", [128, 1])
        gbi = sb("gbi", [128, 3])
        gbh = sb("gbh", [128, 3])
        gb2 = sb("gb2", [128, 2])
        gbn = sb("gbn", [128, 1])

        xs = sb("xs", [128, B, D])
        hs = sb("hs", [128, B, D])
        ye = sb("ye", [128, E * CT, D])
        yg = [sb(f"yg{s}", [128, 2, D]) for s in range(SLOTS)]
        pick = [sb(f"pick{s}", [128, 2], I32) for s in range(SLOTS)]
        lg = sb("lg", [128, B, E])
        gate = sb("gate", [128, 2, B])
        slot_i = sb("slot_i", [128, 2, B], I32)

        def per(name, shape, dt=F32, of=ctx):
            return [sb(f"{name}{s}", shape, dt, of) for s in range(SLOTS)]

        gt = sb("gt", [128, B, E])
        ge = sb("ge", [128, B, E])
        gw = sb("gw", [128, B, E])
        gm = [sb(f"gm{k}", [128, E, B]) for k in range(2)]
        gmb = sb("gmb", [128, E, B], BF16)
        gv = sb("gv", [128, E, B])
        gp = sb("gp", [128, E, B])
        gx = sb("gx", [128, B])
        g1 = sb("g1", [128, B])
        eight = sb("eight", [128, B, E])
        chain = sb("chain", [128, E, B])
        base = [sb(f"base{l}", [128, E, B]) for l in range(2)]
        base_i = sb("base_i", [128, E, B], I32)
        sl = [sb(f"sl{k}", [128, B]) for k in range(2)]

        xe = per("xe", [128, CT, D])
        xeT = per("xeT", [128, CAP0])
        w1 = per("w1", [128, HID])
        w2 = per("w2", [128, HC, D])
        hT = per("hT", [128, HC, CAP0])

        zone = ExitStack()
        va = per("va", [M, H, D], of=zone)
        early = ExitStack()
        c_s = per("c_s", [M, G, D], of=early)
        cT = per("cT", [128, G, M], of=early)
        g_s = per("g_s", [128, G, M], of=early)
        v_s = per("v_s", [M, G, D + 1], of=early)
        vr_s = per("vr_s", [M, G, D + 1], of=early)
        st = per("st", [128, G * 6], of=early)
        mv = per("mv", [128, G, 2], of=early)
        pw = per("pw", [128, G], of=early)
        rs = per("rs", [128, G], of=early)
        pwc = per("pwc", [128, G], of=early)
        rc = per("rc", [128, G], of=early)
        mx = per("mx", [M, G], of=early)
        nb = per("nb", [M, G], of=early)
        sm = per("sm", [M, G], of=early)
        rm = per("rm", [M, G], of=early)
        cs = per("cs", [128, G], of=early)
        ci = per("ci", [128, G], of=early)
        xh = per("xh", [128, G, D], of=early)
        lpw = per("lpw", [128, G], of=early)
        lrs = per("lrs", [128, G], of=early)
        sT = per("sT", [128, G * S], of=early)
        tok = per("tok", [128, G, D], of=early)
        snT = per("snT", [128, G * S], of=early)
        ex = per("ex", [M, G, S], of=early)
        upT = per("upT", [128, G * S], of=early)
        tr = per("tr", [128, G * S], of=early)
        tz = per("tz", [128, G * S], of=early)
        qn = per("qn", [128, G * S], of=early)
        nn = per("nn", [128, G * S], of=early)
        uu = per("uu", [128, G * S], of=early)
        hh = [hT[s][:, 0, 0:G * S] for s in range(SLOTS)]

        early.close()

        mid = ExitStack()
        ca = per("ca", [M, D], of=mid)
        mk = per("mk", [128, M], I32, of=mid)
        mb = per("mb", [128, M], BF16, of=mid)
        caT = per("caT", [128, M], of=mid)
        kT = per("kT", [128, M], of=mid)
        kb = per("kb", [128, HG, M], of=mid)
        sta = per("sta", [128, 6], of=mid)
        mva = per("mva", [128, 2], of=mid)
        pwa = per("pwa", [128, 1], of=mid)
        rsa = per("rsa", [128, 1], of=mid)
        ha = per("ha", [128, D], of=mid)
        haT = per("haT", [128, S], of=mid)
        qT = per("qT", [128, S], of=mid)
        mxa = per("mxa", [128, H], of=mid)
        nm = per("nm", [128, H], of=mid)
        pr = per("pr", [128, H, M], of=mid)
        pT = per("pT", [M, H * S], of=mid)
        den = per("den", [128, H], of=mid)
        dg = per("dg", [128, H], of=mid)
        rden = per("rden", [128, H], of=mid)
        oT = per("oT", [128, S], of=mid)
        stb = per("stb", [128, 6], of=mid)
        mvb = per("mvb", [128, 2], of=mid)
        pwb = per("pwb", [128, 1], of=mid)
        rsb = per("rsb", [128, 1], of=mid)
        hb = per("hb", [128, D], of=mid)
        hbT = per("hbT", [128, S], of=mid)

        mid.close()
        zone.close()

        b2b = sb("b2b", [128, E, D])
        xe1T = sb("xe1T", [128, E, B, CAP1])
        yb = sb("yb", [HR, 2, B, D])
        hg = per("hg", [128, G, D])
        sel = per("sel", [128, G, ROWS1])
        cm = sel
        cn = per("cn", [128, G, ROWS1])
        cmT = per("cmT", [HR, 2, G, S])

        w_in = sem("w_in")
        k_pool = sem("k_pool")
        setup_T = sem("setup_T")
        setup_ev = sem("setup_ev")
        setup_m = sem("setup_m")
        setup_done = sem("setup_done")
        zeroed = sem("zeroed")
        stored = sem("stored")
        F = {k: sem(f"f_{k}") for k in
             ("d dd ex pos posr tot slot scat w0 w1 in0 in1 T Tev h hevD hevA y yevD yevA out").split()}
        route_steps = [0]
        C = {k: sem("c_" + k) for k in
             ("in0 in1 g0 g1 pick x1 x2 st mv pw rr ln T Tev kqv kqev kb mb s mx nm ex den rd norm pt pev pv "
              "oTev w x3 st2 mv2 pw2 rr2 ln2 keep T2 T2ev lg lgev").split()}
        L = sems("b2 sel0 sel hg disp dev st yb cm c ct ctev y")
        Z = {k: sem("z_" + k) for k in "a b".split()}
        A = sems("ctx_in0 x_in0 ctx_in1 x_in1 ctx_ms ctx_rr ctx_T ctx_Tev ctx_G ctx_Gev ctx_V ctx_Vev "
                 "x_st x_mv x_rr x_ln x_T x_Tev "
                 "i_tok i_ms i_pw i_rr i_sn i_snT i_snTev i_sc i_mx i_nb i_ex i_rm i_vr i_u i_cs i_ci i_ut "
                 "i_uT i_uTev i_hn i_r i_z i_xn i_tr i_tz i_hh i_q i_q2 i_n i_z2 i_a i_p i_s "
                 "f_T f_x f_st f_mv f_pw f_rr f_ln f_T2 f_T2ev f_lg f_lgev f_keep x_pw ctx_pw")

        K_POOL = 31
        block = ctx.enter_context(nc.Block())
        W_V, W_IH, W_HH, W_QQ, W_KK, W_VV, W_OO = 0, 1, 4, 7, 8, 9, 10
        x_v = t["x"].rearrange("(g b) s d -> g s b d", b=G)
        c_v = t["ctx_1024"].rearrange("(g b) m d -> g m b d", b=G)
        out_v = out.rearrange("b s d -> s b d")
        base_v = rows_d.rearrange("(p r) d -> p (r d)", p=128)
        res_v = [r.rearrange("(e c p) d -> e p c d", e=E, p=128) for r in res_d]
        rows_v = rows_d.rearrange("(e c p) d -> e p c d", e=E, p=128)
        back_v = res_d[1].rearrange("(e b r) d -> e r b d", e=E, r=CAP1)
        w1_v = (t["L0_ffn_experts_inter"], t["L1_ffn_W1"])
        w2_v = [w.rearrange("e (c p) d -> e p c d", p=128) for w in (t["L0_ffn_experts_out"], t["L1_ffn_W2"])]
        mask_v = t["mask_Bx1xSxS2_ik0"].rearrange("b a s m -> (b a) s m")
        ROUTED = B - G * SLOTS
        NWD = 18

        def occ(i, it, s, per_turn=ITERS):
            return i * (per_turn * SLOTS) + it * SLOTS + s + 1

        def occ1(i, s):
            return i * SLOTS + s + 1


        def blocks(a):
            w = a[:, :, :].rearrange("p h d -> p (h d)")
            return bass.AP(tensor=w.tensor, offset=w.offset, ap=[list(w.ap[0]), [D + DK, H], [1, DK]])


        def batch_of(i, s, k):
            return i * SLOTS + s + k, (s + k) % SLOTS, i + (s + k) // SLOTS

        def inside(b):
            return not isinstance(b, int) or 0 <= b < B

        def group_inside(g):
            return not isinstance(g, int) or 0 <= g < B // G

        def pipeline(eng, step, first=-3, low=2 * SLOTS, high=B - 2 * SLOTS, last=B + 2):
            for b in range(first, low):
                step(b // SLOTS, b % SLOTS)
            with eng.Fori(low // SLOTS, high // SLOTS) as i:
                for s in range(SLOTS):
                    step(i, s)
            for b in range(high, last + 1):
                step(b // SLOTS, b % SLOTS)

        @block.sync
        def _(sp):
            for k, name in enumerate(("L0_xattn_Wv", "L1_xattn_W_Q", "L1_xattn_W_K", "L1_xattn_W_V", "L1_xattn_W_O")):
                at = (W_V, W_QQ, W_KK, W_VV, W_OO)[k]
                sp.dma_start(raw[:, at, :], t[name]).then_inc(w_in, 16)
            sp.dma_start(raw[:, W_IH:W_IH + 3, :], t["L0_xattn_gru_wih"].rearrange("(c p) d -> p c d", p=128)).then_inc(w_in, 16)
            sp.dma_start(raw[:, W_HH:W_HH + 3, :], t["L0_xattn_gru_whh"].rearrange("(c p) d -> p c d", p=128)).then_inc(w_in, 16)
            sp.dma_start(wqk[:, 0, :], t["L0_xattn_Wq"]).then_inc(w_in, 16)
            sp.dma_start(wqk[:, 1, :], t["L0_xattn_Wk"]).then_inc(w_in, 16)
            sp.dma_start(small[:, :], t["L0_ffn_W_router"]).then_inc(w_in, 16)
            sp.dma_start(wr[1][:, :], t["L1_ffn_Wr"]).then_inc(w_in, 16)
            sp.dma_start(br[0][:, :], t["L0_ffn_b_router"].partition_broadcast(128)).then_inc(w_in, 16)
            sp.dma_start(br[1][:, :], t["L1_ffn_br"].partition_broadcast(128)).then_inc(w_in, 16)
            sp.dma_start(b1raw[:, :], t["L1_ffn_b1"].rearrange("e (c p) -> (e c) p", p=128)).then_inc(w_in, 16)
            with nc.allow_non_contiguous_dma(reason="columns of 128 and 384 floats"):
                sp.dma_start(win[:, :], t["L0_xattn_input_norm_w"].rearrange("(p a) -> p a", a=1)).then_inc(w_in, 16)
                sp.dma_start(wslot[:, :], t["L0_xattn_slot_norm_w"].rearrange("(p a) -> p a", a=1)).then_inc(w_in, 16)
                sp.dma_start(gbi[:, :], t["L0_xattn_gru_bih"].rearrange("(c p) -> p c", p=128)).then_inc(w_in, 16)
                sp.dma_start(gbh[:, :], t["L0_xattn_gru_bhh"].rearrange("(c p) -> p c", p=128)).then_inc(w_in, 16)
            def group(i, s):
                return bass.ds(i * SLOTS + s, 1)

            def load_c(i, s):
                sp.dma_start(c_s[s][:, :, :], c_v[group(i, s)].rearrange("a m b d -> m (a b) d")).then_inc(A[f"ctx_in{s}"], 16)

            def load_x(i, s):
                sp.dma_start(xs[:, bass.ds((i * SLOTS + s) * G, G), :], x_v[group(i, s)].rearrange("a m b d -> m (a b) d")).then_inc(A[f"x_in{s}"], 16)
            for s in range(SLOTS):
                load_c(0, s)
                load_x(0, s)
            with sp.Fori(1, NG) as i:
                for s in range(SLOTS):
                    sp.wait_ge(A[f"x_in{s}"], 16 * i)
                    load_x(i, s)
            with sp.Fori(1, NG) as i:
                for s in range(SLOTS):
                    sp.wait_ge(A["ctx_T"], occ1(i - 1, s))
                    sp.wait_ge(A["ctx_ms"], occ1(i - 1, s))
                    load_c(i, s)

            def weights(l, e, s):
                e = bass.ds(e, 1)
                sp.dma_start(w1[s][:, :], w1_v[l][e].rearrange("a p n -> p (a n)")).then_inc(F[f"w{s}"], 16)
                sp.dma_start(w2[s][:, :, :], w2_v[l][e].rearrange("a p c d -> p (a c) d")).then_inc(F[f"w{s}"], 16)

            def rows(e, s):
                sp.dma_start(xe[s][:, :, :], rows_v[bass.ds(e, 1)].rearrange("a p c d -> p (a c) d")).then_inc(F[f"in{s}"], 16)

            def store(l, e, done):
                if l == 0:
                    sp.wait_ge(F["yevA"], e + 1)
                sp.wait_ge(F["yevD"], e + 1 + l * E)
                sp.dma_start(res_v[l][bass.ds(e, 1)].rearrange("a p c d -> p (a c) d"),
                             ye[:, bass.ds(e * CT, CT), :]).then_inc(done, 16)

            sp.wait_ge(Z["a"], 1)
            for j in range(ROWS // 128 // CT):
                sp.dma_start(base_v[:, j * CT * D:(j + 1) * CT * D], ye[:, 0:CT, :].rearrange("p c d -> p (c d)")).then_inc(zeroed, 16)
            for s in range(SLOTS):
                weights(0, s, s)
            sp.wait_ge(F["scat"], 16 * 2 * B)
            for s in range(SLOTS):
                rows(s, s)
            with sp.Fori(1, E // SLOTS) as i:
                for s in range(SLOTS):
                    sp.wait_ge(F["T"], (i - 1) * SLOTS + s + 1)
                    rows(i * SLOTS + s, s)
                    store(0, (i - 1) * SLOTS + s, F["out"])
                    weights(0, i * SLOTS + s, s)
            for s in range(SLOTS):
                store(0, E - SLOTS + s, F["out"])
            for s in range(SLOTS):
                sp.dma_start(ca[s][:, :], t["ctx_1024"][s]).then_inc(C[f"in{s}"], 16)
                sp.dma_start(mk[s][:, :], mask_v[s]).then_inc(C[f"in{s}"], 16)

            def step(i, s):
                b, v, turn = batch_of(i, s, 3)
                if inside(b) and (not isinstance(b, int) or b >= SLOTS):
                    sp.wait_ge(C["T"], b - 1)
                    sp.wait_ge(C["mb"], b - 1)
                    sp.dma_start(ca[v][:, :], t["ctx_1024"][bass.ds(b, 1)].rearrange("a m d -> m (a d)")).then_inc(C[f"in{v}"], 16)
                    sp.dma_start(mk[v][:, :], mask_v[bass.ds(b, 1)].rearrange("a q m -> q (a m)")).then_inc(C[f"in{v}"], 16)
            pipeline(sp, step)
            sp.wait_ge(C["lgev"], B)
            sp.dma_start(b2b[:, :, :], t["L1_ffn_b2"].partition_broadcast(128)).then_inc(L["b2"], 16)
            for s in range(SLOTS):
                weights(1, s, s)
            for e in range(E):
                store(1, e, L["st"])
                if e + SLOTS < E:
                    weights(1, e + SLOTS, e % SLOTS)
                sp.wait_ge(L["st"], 16 * (e + 1))
                p = e % 4 * CAP1
                sp.dma_start(yb[p:p + CAP1, e // 4, :, :], back_v[e]).then_inc(L["yb"], 16)
            with sp.Fori(0, B // G) as i:
                sp.wait_ge(Z["b"], i + 1)
                sp.dma_start(out_v[:, bass.ds(i * G, G), :], xs[:, bass.ds(i * G, G), :]).then_inc(stored, 16)
            sp.wait_ge(stored, 16 * (B // G))

        @block.gpsimd
        def _(pool):
            pool.memset(ident[:, :], 0.0).then_inc(k_pool, 1)
            pool.memset(ones_bf[:, :], 1.0).then_inc(k_pool, 1)
            pool.memset(minus_half[:, :], -0.5).then_inc(k_pool, 1)
            pool.memset(eps_ln[:, :], EPS_LN).then_inc(k_pool, 1)
            pool.memset(eps_rms[:, :], EPS_RMS).then_inc(k_pool, 1)
            pool.memset(gv[:, :, :], 0.0).then_inc(k_pool, 1)
            for s in range(SLOTS):
                pool.memset(v_s[s][:, :, D:D + 1], 1.0).then_inc(k_pool, 1)
            pool.wait_ge(k_pool, 8)
            pool.affine_select(out=ident[:, :], in_=ident[:, :], compare_op=ALU.not_equal, fill=1.0,
                               base=0, pattern=[[-1, 128]], channel_multiplier=1).then_inc(k_pool, 1)
            pool.affine_select(out=before[:, :], in_=ones_bf[:, :], compare_op=ALU.is_gt, fill=0.0,
                               base=0, pattern=[[1, 128]], channel_multiplier=-1).then_inc(k_pool, 1)
            pool.iota(base_i[:, :, :], pattern=[[CAP0, E], [0, B]], base=0, channel_multiplier=0).then_inc(k_pool, 1)
            pool.wait_ge(k_pool, 11)
            pool.tensor_copy(base[0][:, :, :], base_i[:, :, :]).then_inc(k_pool, 1)
            pool.wait_ge(k_pool, 12)
            pool.iota(base_i[:, :, :], pattern=[[CAP1, E], [0, B]], base=0, channel_multiplier=0).then_inc(k_pool, 1)
            pool.wait_ge(k_pool, 13)
            pool.tensor_copy(base[1][:, :, :], base_i[:, :, :]).then_inc(k_pool, 1)
            pool.memset(chain[:, :, :], 1.0).then_inc(k_pool, 1)
            pool.wait_ge(k_pool, 15)
            pool.memset(chain[:, :, 0:1], 0.0).then_inc(k_pool, 1)
            for e in range(E):
                pool.memset(eight[:, :, e:e + 1], float(E - e)).then_inc(k_pool, 1)
            for s in range(SLOTS):
                pool.memset(va[s][:, :, :], 0.0).then_inc(k_pool, 1)
            for s in range(SLOTS):
                pool.memset(yg[s][:, :, :], 0.0).then_inc(k_pool, 1)
            pool.wait_ge(k_pool, 28)
            row_i = base_i[:, 0:ROWS1 // B, :].rearrange("p e b -> p (e b)")
            pool.iota(row_i, pattern=[[1, ROWS1]], base=0, channel_multiplier=0).then_inc(k_pool, 1)
            pool.wait_ge(k_pool, 29)
            pool.tensor_copy(iota_row[:, :], row_i).then_inc(k_pool, 1)
            pool.memset(ye[:, :, :], 0.0).then_inc(Z["a"], 1)
            pool.tensor_copy(ident_bf[:, :], ident[:, :]).then_inc(k_pool, 1)

            def power(src, dst, rows, n, s_src, s_mid, mid, s_dst, eps):
                pool.wait_ge(A[s_src], n)
                pool.tensor_tensor(mid[0:rows, :], src, eps[0:rows, :], ALU.add).then_inc(A[s_mid], 1)
                pool.wait_ge(A[s_mid], n)
                pool.tensor_tensor(dst[0:rows, :], mid[0:rows, :], minus_half[0:rows, :], ALU.pow).then_inc(A[s_dst], 1)

            def scatter(lo, hi):
                for b in range(lo, hi):
                    for k in range(2):
                        pool.indirect_dma_start(out=rows_d, out_offset=bass.IndirectOffsetOnAxis(ap=slot_i[:, k, b:b + 1], axis=0),
                                                in_=hs[:, b, :], in_offset=None, bounds_check=ROWS - 1,
                                                oob_is_err=False).then_inc(F["scat"], 16)

            def x_power(i):
                for s in range(SLOTS):
                    power(mv[s][:, :, 1], lrs[s], 128, occ1(i, s), "x_mv", "x_pw", lpw[s], "x_rr", eps_ln)

            def f_power(i):
                for s in range(SLOTS):
                    power(mv[s][:, :, 1], lrs[s], 128, occ1(i, s), "f_mv", "f_pw", lpw[s], "f_rr", eps_ln)

            def ctx_power(i):
                for s in range(SLOTS):
                    power(pwc[s][0:M, :], rc[s], M, occ1(i, s), "ctx_ms", "ctx_pw", pwc[s], "ctx_rr", eps_rms)

            def slot_turn(i, prev=True, nxt=True):
                if prev:
                    f_power(i - 1)
                for it in range(ITERS):
                    for s in range(SLOTS):
                        n = occ(i, it, s)
                        power(cs[s][:, :], rs[s], 128, n, "i_ms", "i_pw", pw[s], "i_rr", eps_rms)
                    if nxt and it == 1:
                        x_power(i + 1)
                    if nxt and it == 2:
                        for s in range(SLOTS):
                            pool.wait_ge(A["i_ex"], occ(i, it, s))
                        ctx_power(i + 1)
                    if not nxt and it > 0:
                        if it == 1:
                            pool.wait_ge(F["slot"], 1)
                            pool.wait_ge(A["f_keep"], ROUTED // G)
                            pool.wait_ge(zeroed, 16 * (ROWS // 128 // CT))
                        scatter((it - 1) * ROUTED // 2, it * ROUTED // 2)
                        continue
                    for s in range(SLOTS):
                        n = occ(i, it, s)
                        pool.wait_ge(k_pool, K_POOL)
                        pool.wait_ge(A["i_tz"], n)
                        pool.tensor_scalar(tz[s][:, :], tz[s][:, :], 0.5, 0.5, ALU.mult, ALU.add).then_inc(A["i_z2"], 1)
                        pool.wait_ge(A["i_z2"], n)
                        pool.tensor_tensor(uu[s][:, :], sT[s][:, :], tz[s][:, :], ALU.mult).then_inc(A["i_a"], 1)

            def fetch(b, v):
                pool.tensor_copy(pick[v][:, :].unsqueeze(2), slot_i[:, :, bass.ds(b, 1)]).then_inc(C["pick"], 1)
                pool.to_reg(b + 1)
                pool.wait_ge(k_pool, K_POOL)
                pool.wait_ge(C["pick"], b + 1)
                for k in range(2):
                    pool.indirect_dma_start(out=yg[v][:, k, :], out_offset=None, in_=res_d[0],
                                            in_offset=bass.IndirectOffsetOnAxis(ap=pick[v][:, k:k + 1], axis=0),
                                            bounds_check=ROWS - 1, oob_is_err=False).then_inc(C[f"g{v}"], 16)

            def power1(n, src, mid, dst, s_src, s_mid, s_dst):
                pool.wait_ge(C[s_src], n)
                pool.tensor_tensor(mid[:, :], src[:, 1:2], eps_ln[:, 0:1], ALU.add).then_inc(C[s_mid], 1)
                pool.wait_ge(C[s_mid], n)
                pool.tensor_tensor(dst[:, :], mid[:, :], minus_half[:, 0:1], ALU.pow).then_inc(C[s_dst], 1)

            def step(i, s):
                b, v, turn = batch_of(i, s, -3)
                if inside(b):
                    pool.wait_ge(C["ln2"], b + 1)
                    pool.tensor_copy(hs[:, bass.ds(b, 1), :], hb[v][:, :].unsqueeze(1)).then_inc(C["keep"], 1)
                b, v, turn = batch_of(i, s, 3)
                if inside(b):
                    pool.to_reg(b)
                    if not isinstance(b, int) or b >= SLOTS:
                        pool.wait_ge(C["x2"], b - 1)
                        pool.wait_ge(C[f"g{v}"], 32 * turn)
                    fetch(b, v)
                b, v, turn = batch_of(i, s, 2)
                if inside(b):
                    power1(b + 1, mva[v], pwa[v], rsa[v], "mv", "pw", "rr")
                b, v, turn = batch_of(i, s, -2)
                if inside(b):
                    power1(b + 1, mvb[v], pwb[v], rsb[v], "mv2", "pw2", "rr2")

            ctx_power(0)
            x_power(0)
            slot_turn(0, prev=False)
            with pool.Fori(1, NG - 1) as i:
                slot_turn(i)
            slot_turn(NG - 1, nxt=False)
            f_power(NG - 1)
            pool.wait_ge(F["slot"], 2)
            pool.wait_ge(A["f_keep"], B // G)
            scatter(ROUTED, B)
            pool.wait_ge(F["out"], 16 * E)
            pipeline(pool, step)

        @block.scalar
        def _(act):
            act.wait_ge(w_in, 16 * NWD)
            act.wait_ge(setup_m, 5)
            act.wait_ge(setup_T, 1)
            for j in range(4):
                act.activation(wT[:, j, :], bank[0][:, j * D:(j + 1) * D], ACT.Identity,
                               **({"scale": win[:, 0:1]} if j == 0 else {}))
            for j in range(4):
                at = 4 + j
                act.activation(wT[:, at, :], bank[1][:, j * D:(j + 1) * D], ACT.Identity,
                               **({"scale": float(DK) ** -0.5} if at == W_QQ else {}))
            act.activation(wT[:, 8:11, :], bank[2][:, 0:3 * D].rearrange("p (j d) -> p j d", j=3), ACT.Identity)
            act.activation(wr[0][:, :], bank[3][:, 0:E], ACT.Identity)
            act.activation(b1T[:, :], bank[3][:, 32:64], ACT.Identity)
            act.activation(mT[:, :], bank[3][:, 128:256], ACT.Identity, scale=win[:, 0:1]).then_inc(setup_ev, 1)

            def ctx_square(i):
                for s in range(SLOTS):
                    act.wait_ge(A[f"ctx_in{s}"], 16 * (i + 1))
                    for b in range(G):
                        last = act.activation(tr[s][0:M, b * D:(b + 1) * D], c_s[s][:, b, :], ACT.Square, scale=float(D) ** -0.5,
                                              accum_out=pwc[s][0:M, b:b + 1])
                    last.then_inc(A["ctx_ms"], 1)

            def ctx_keep(i):
                for s in range(SLOTS):
                    act.wait_ge(A["ctx_T"], occ1(i, s))
                    act.activation(cT[s][:, :, :], bank[4 * s + 3][:, 0:G * M].rearrange("p (b m) -> p b m", b=G),
                                   ACT.Identity).then_inc(A["ctx_Tev"], 1)

            def f_keep(i):
                for s in range(SLOTS):
                    act.wait_ge(A["f_ln"], occ1(i, s))
                    act.activation(hs[:, bass.ds((i * SLOTS + s) * G, G), :], xh[s][:, :, :], ACT.Identity).then_inc(A["f_keep"], 1)

            def f_keepT(i):
                for s in range(SLOTS):
                    act.wait_ge(A["f_T2"], occ1(i, s))
                    act.activation(snT[s][:, :], bank[4 * s + 3][:, :], ACT.Identity).then_inc(A["f_T2ev"], 1)

            def slot_turn(i, prev=True, nxt=True):
                for s in range(SLOTS):
                    n = occ1(i, s)
                    act.wait_ge(A["x_T"], n)
                    act.activation(sT[s][:, :], bank[4 * s + 1][:, :], ACT.Identity).then_inc(A["x_Tev"], 1)
                for it in range(ITERS):
                    for s in range(SLOTS):
                        n = occ(i, it, s)
                        act.wait_ge(A["i_tok"], n)
                        for b in range(G):
                            last = act.activation(uu[s][:, b * D:(b + 1) * D], bank[4 * s][:, b * D:(b + 1) * D], ACT.Square,
                                                  scale=float(D) ** -0.5, accum_out=cs[s][:, b:b + 1])
                        last.then_inc(A["i_ms"], 1)
                    for s in range(SLOTS):
                        n = occ(i, it, s)
                        act.wait_ge(A["i_snT"], n)
                        act.activation(snT[s][:, :], bank[4 * s][:, :], ACT.Identity).then_inc(A["i_snTev"], 1)
                    for s in range(SLOTS):
                        n = occ(i, it, s)
                        act.wait_ge(A["i_hn"], n)
                        act.activation(hh[s][:, :], bank[4 * s + 3][:, :], ACT.Identity, bias=gbn[:, 0:1], scale=0.5).then_inc(A["i_hh"], 1)
                    if prev and it == 0:
                        f_keep(i - 1)
                    if nxt and it == 2:
                        ctx_square(i + 1)
                    for s in range(SLOTS):
                        n = occ(i, it, s)
                        act.wait_ge(A["i_nb"], n)
                        for b in range(G):
                            last = act.activation(ex[s][:, b, :], bank[4 * s + 1][0:M, b * S:(b + 1) * S], ACT.Exp,
                                                  bias=nb[s][:, b:b + 1], scale=rc[s][0:M, b:b + 1],
                                                  accum_out=sm[s][:, b:b + 1])
                        last.then_inc(A["i_ex"], 1)
                    if prev and it == 0:
                        f_keepT(i - 1)
                    if nxt and it == 2:
                        ctx_keep(i + 1)
                    for s in range(SLOTS):
                        n = occ(i, it, s)
                        act.wait_ge(A["i_uT"], n)
                        act.activation(upT[s][:, :], bank[4 * s + 2][:, :], ACT.Identity).then_inc(A["i_uTev"], 1)
                    for s in range(SLOTS):
                        n = occ(i, it, s)
                        act.wait_ge(A["i_r"], n)
                        act.activation(tr[s][:, :], bank[4 * s][:, :], ACT.Tanh, bias=gb2[:, 0:1], scale=0.5).then_inc(A["i_tr"], 1)
                        act.wait_ge(A["i_z"], n)
                        act.activation(tz[s][:, :], bank[4 * s + 1][:, :], ACT.Tanh, bias=gb2[:, 1:2], scale=0.5).then_inc(A["i_tz"], 1)
                        act.wait_ge(A["i_q2"], n)
                        act.activation(nn[s][:, :], qn[s][:, :], ACT.Tanh, bias=gbi[:, 2:3]).then_inc(A["i_n"], 1)
                    if not nxt and it == 0:
                        router_exp(0, 0, ROUTED)

            def router_exp(c, lo, hi):
                act.wait_ge(F["d"], c + 1)
                act.activation(ge[:, lo:hi, :], gt[:, lo:hi, :], ACT.Exp).then_inc(F["ex"], 1)

            ctx_square(0)
            ctx_keep(0)
            slot_turn(0, prev=False)
            with act.Fori(1, NG - 1) as i:
                slot_turn(i)
            slot_turn(NG - 1, nxt=False)
            f_keep(NG - 1)
            f_keepT(NG - 1)

            def rows_T(i, s):
                act.wait_ge(F["T"], occ1(i, s))
                act.activation(xeT[s][:, 0:512], bank[0][:, :], ACT.Identity)
                act.activation(xeT[s][:, 512:CAP0], bank[1][:, 0:D], ACT.Identity).then_inc(F["Tev"], 1)

            def expert(l, i, s, last_one=False):
                f = F
                n = occ1(i, s) + l * E
                for c in range(HC):
                    act.wait_ge(f["h"], n * HC - (HC - 1 - c))
                    bias = {"bias": b1T[:, bass.ds((i * SLOTS + s) * HC + c, 1)]} if l else {}
                    act.activation(hT[s][:, c, CAP0 // 2:CAP0], bank[3 + 2 * (c % 2)][:, 0:CAP0 // 2],
                                   ACT.Relu, **bias).then_inc(f["hevA"], 1)
                if l == 0:
                    if not last_one:
                        rows_T(i + (s + 1) // SLOTS, (s + 1) % SLOTS)
                    act.wait_ge(f["y"], n)
                    act.activation(ye[:, bass.ds((i * SLOTS + s) * CT, HC), :],
                                   bank[6][:, :].rearrange("p (c d) -> p c d", c=HC), ACT.Identity).then_inc(f["yevA"], 1)

            def experts_act(l):
                if l == 0:
                    rows_T(0, 0)
                with act.Fori(0, E // SLOTS - 1) as i:
                    for s in range(SLOTS):
                        expert(l, i, s)
                for s in range(SLOTS):
                    expert(l, E // SLOTS - 1, s, last_one=(s == SLOTS - 1))

            router_exp(1, ROUTED, B)
            experts_act(0)

            def exponentials(i, s, g):
                b, v, turn = batch_of(i, s, 0)
                if inside(b):
                    act.wait_ge(C["nm"], b * 4 + g + 1)
                    for j in range(HG):
                        h = HG * g + j
                        last = act.activation(pr[v][:, h, :], bank[g][:, j * M:(j + 1) * M], ACT.Exp, bias=nm[v][:, h:h + 1],
                                              accum_out=den[v][:, h:h + 1])
                    last.then_inc(C["ex"], 1)

            def keep_pT(i, s, g):
                b, v, turn = batch_of(i, s, -1)
                if inside(b):
                    act.wait_ge(C["pt"], b * 4 + g + 1)
                    act.activation(pT[v][:, g * 512:(g + 1) * 512], bank[4 + g % 2][0:M, :], ACT.Identity).then_inc(C["pev"], 1)

            def step(i, s):
                exponentials(i, s, 0)
                b, v, turn = batch_of(i, s, -2)
                if inside(b):
                    act.wait_ge(C["pv"], b + 1)
                    act.activation(oT[v][:, :], bank[7][:, 0:S], ACT.Identity).then_inc(C["oTev"], 1)
                keep_pT(i, s, 0)
                b, v, turn = batch_of(i, s, -3)
                if inside(b):
                    act.wait_ge(C["T2"], b + 1)
                    act.activation(hbT[v][:, :], bank[6][:, 0:S], ACT.Identity).then_inc(C["T2ev"], 1)
                exponentials(i, s, 1)
                keep_pT(i, s, 1)
                b, v, turn = batch_of(i, s, 1)
                if inside(b):
                    act.wait_ge(C["T"], b + 1)
                    act.activation(caT[v][:, :], bank[6][:, 0:M], ACT.Identity)
                    act.activation(haT[v][:, :], bank[6][:, D:2 * D], ACT.Identity).then_inc(C["Tev"], 1)
                b0, v0, turn0 = batch_of(i, s, 0)
                if inside(b) or inside(b0):
                    act.wait_ge(C["kqv"], b + 1)
                if inside(b):
                    act.activation(kT[v][:, :], bank[6][:, 0:M], ACT.Identity)
                    last = act.activation(qT[v][:, :], bank[6][:, D:2 * D], ACT.Identity)
                if inside(b0):
                    last = act.activation(blocks(va[v0]), bank[6][0:M, 2 * D:3 * D].rearrange("p (h d) -> p h d", h=H), ACT.Identity)
                if inside(b) or inside(b0):
                    last.then_inc(C["kqev"], 1)
                exponentials(i, s, 2)
                keep_pT(i, s, 2)
                exponentials(i, s, 3)
                keep_pT(i, s, 3)
            pipeline(act, step)
            router_exp(2, 0, B)

            act.wait_ge(C["keep"], B)

            def rows_act(i, s):
                g, v, turn = batch_of(i, s, 1)
                if not isinstance(g, int) or g < B // G:
                    act.activation(hg[v][:, :, :], hs[:, bass.ds(g * G, G), :], ACT.Identity).then_inc(L["hg"], 1)
                g, v, turn = batch_of(i, s, 0)
                if not isinstance(g, int) or g >= 0:
                    act.wait_ge(L["disp"], g + 1)
                    for j in range(2):
                        last = act.activation(xe1T[:, :, bass.ds(g * G + 2 * j, 2), :].rearrange("p e b r -> p b e r"),
                                              bank[2 + 2 * v + j][:, 0:2 * ROWS1].rearrange("p (b e r) -> p b e r", b=2, e=E), ACT.Identity)
                    last.then_inc(L["dev"], 1)
            pipeline(act, rows_act, -1, SLOTS, B // G - SLOTS, B // G - 1)
            experts_act(1)

            def step(i, s):
                g, v, turn = batch_of(i, s, 1)
                if group_inside(g):
                    act.wait_ge(L["ct"], g + 1)
                    for k in range(2):
                        last = act.activation(cmT[v][:, k, :, :], bank[2 * v + k][0:HR, :].rearrange("p (b t) -> p b t", b=G), ACT.Identity)
                    last.then_inc(L["ctev"], 1)
            pipeline(act, step, -1, SLOTS, B // G - SLOTS, B // G - 1)

        @block.tensor
        def _(pe):
            pe.wait_ge(w_in, 16 * NWD)
            pe.wait_ge(k_pool, K_POOL)
            for j in range(11):
                pe.transpose(bank[j // 4][:, (j % 4) * D:(j % 4 + 1) * D], raw[:, j, :], ident[:, :])
            pe.transpose(bank[3][:, 0:E], small[:, :], ident[0:E, 0:E])
            pe.transpose(bank[3][:, 32:64], b1raw[:, :], ident[0:32, 0:32])
            pe.matmul(bank[3][:, 128:256], wqk[:, 1, :], wqk[:, 0, :], start=True, stop=True).then_inc(setup_T, 1)
            pe.wait_ge(setup_ev, 1)

            def ctx_turn(i):
                for s in range(SLOTS):
                    pe.wait_ge(A[f"ctx_in{s}"], 16 * (i + 1))
                    for b in range(G):
                        last = pe.transpose(bank[4 * s + 3][:, b * M:(b + 1) * M], c_s[s][:, b, :], ident[0:M, 0:M])
                    last.then_inc(A["ctx_T"], 1)

            def ctx_G(i):
                for s in range(SLOTS):
                    pe.wait_ge(A["ctx_Tev"], occ1(i, s))
                    pe.matmul(bank[4 * s + 3][:, 0:G * M], mT[:, :], cT[s][:, :, :].rearrange("p b m -> p (b m)"),
                              start=True, stop=True).then_inc(A["ctx_G"], 1)

            def ctx_V(i):
                for s in range(SLOTS):
                    pe.wait_ge(A["ctx_Gev"], occ1(i, s))
                    for b in range(G):
                        last = pe.matmul(bank[4 * s + 3][0:M, b * D:(b + 1) * D], cT[s][:, b, :], wT[:, W_V, :], start=True, stop=True)
                    last.then_inc(A["ctx_V"], 1)

            def f_T(i):
                for s in range(SLOTS):
                    pe.wait_ge(A["i_s"], occ(i, ITERS - 1, s))
                    for b in range(G):
                        last = pe.transpose(bank[4 * s][:, b * D:(b + 1) * D], sT[s][:, b * S:(b + 1) * S], ident[:, :])
                    last.then_inc(A["f_T"], 1)

            def f_T2(i, hh_n):
                for s in range(SLOTS):
                    pe.wait_ge(A["f_ln"], occ1(i, s))
                    pe.wait_ge(A["i_hh"], hh_n + s)
                    for b in range(G):
                        last = pe.transpose(bank[4 * s + 3][:, b * S:(b + 1) * S], xh[s][:, b, :], ident[:, :])
                    last.then_inc(A["f_T2"], 1)

            def f_logits(i):
                for s in range(SLOTS):
                    pe.wait_ge(A["f_T2ev"], occ1(i, s))
                    for b in range(G):
                        last = pe.matmul(bank[4 * s + 3][:, b * E:(b + 1) * E], snT[s][:, b * S:(b + 1) * S], wr[0][:, :], start=True, stop=True)
                    last.then_inc(A["f_lg"], 1)

            def slot_turn(i, prev=True, nxt=True):
                if prev:
                    f_T(i - 1)
                for s in range(SLOTS):
                    pe.wait_ge(A["x_ln"], occ1(i, s))
                    for b in range(G):
                        last = pe.transpose(bank[4 * s + 1][:, b * S:(b + 1) * S], xh[s][:, b, :], ident[:, :])
                    last.then_inc(A["x_T"], 1)
                for it in range(ITERS):
                    for s in range(SLOTS):
                        n = occ(i, it, s)
                        b0, b1, b2, b3 = bank[4 * s:4 * s + 4]
                        if it == 0:
                            pe.wait_ge(A["x_Tev"], occ1(i, s))
                            pe.wait_ge(A["ctx_Vev"], occ1(i, s))
                            pe.wait_ge(A["ctx_Gev"], occ1(i, s))
                            if prev:
                                pe.wait_ge(A["f_x"], occ1(i - 1, s))
                        else:
                            pe.wait_ge(A["i_s"], n - SLOTS)
                            if prev and it == 1:
                                pe.wait_ge(A["f_lgev"], occ1(i - 1, s))
                        for b in range(G):
                            last = pe.transpose(b0[:, b * D:(b + 1) * D], sT[s][:, b * S:(b + 1) * S], ident[:, :])
                        last.then_inc(A["i_tok"], 1)
                    for s in range(SLOTS):
                        pe.matmul(bank[4 * s + 3][:, :], wT[:, W_HH + 2, :], sT[s][:, :], start=True, stop=True).then_inc(A["i_hn"], 1)
                    for s in range(SLOTS):
                        n = occ(i, it, s)
                        b0 = bank[4 * s]
                        pe.wait_ge(A["i_sn"], n)
                        for b in range(G):
                            last = pe.transpose(b0[:, b * S:(b + 1) * S], tok[s][:, b, :], ident[:, :])
                        last.then_inc(A["i_snT"], 1)
                    for s in range(SLOTS):
                        n = occ(i, it, s)
                        b0, b1, b2, b3 = bank[4 * s:4 * s + 4]
                        pe.wait_ge(A["i_snTev"], n)
                        for b in range(G):
                            last = pe.matmul(b1[0:M, b * S:(b + 1) * S], g_s[s][:, b, :], snT[s][:, b * S:(b + 1) * S],
                                             start=True, stop=True)
                        last.then_inc(A["i_sc"], 1)
                        pe.matmul(b0[:, :], wT[:, W_HH, :], sT[s][:, :], start=True, stop=False)
                    if nxt and it == 2:
                        for s in range(SLOTS):
                            pe.wait_ge(A["i_hh"], occ(i, it, s))
                        ctx_turn(i + 1)
                    for s in range(SLOTS):
                        n = occ(i, it, s)
                        b0, b1, b2, b3 = bank[4 * s:4 * s + 4]
                        pe.wait_ge(A["i_vr"], n)
                        for b in range(G):
                            o = b2[:, b * (D + 1):(b + 1) * (D + 1)] if b < G - 1 else b1[:, 0:D + 1]
                            last = pe.matmul(o, ex[s][:, b, :], vr_s[s][:, b, :], start=True, stop=True)
                        last.then_inc(A["i_u"], 1)
                    if nxt and it == 2:
                        ctx_G(i + 1)
                    if prev and it == 0:
                        f_T2(i - 1, occ(i, it, 0))
                    for s in range(SLOTS):
                        n = occ(i, it, s)
                        b0, b1, b2, b3 = bank[4 * s:4 * s + 4]
                        pe.wait_ge(A["i_ut"], n)
                        for b in range(G):
                            last = pe.transpose(b2[:, b * S:(b + 1) * S], tok[s][:, b, :], ident[:, :])
                        last.then_inc(A["i_uT"], 1)
                        pe.matmul(b1[:, :], wT[:, W_HH + 1, :], sT[s][:, :], start=True, stop=False)
                    for s in range(SLOTS):
                        n = occ(i, it, s)
                        b0, b1, b2, b3 = bank[4 * s:4 * s + 4]
                        pe.wait_ge(A["i_uTev"], n)
                        pe.matmul(b0[:, :], wT[:, W_IH, :], upT[s][:, :], start=False, stop=True).then_inc(A["i_r"], 1)
                        pe.matmul(b2[:, :], wT[:, W_IH + 2, :], upT[s][:, :], start=True, stop=True).then_inc(A["i_xn"], 1)
                        pe.matmul(b1[:, :], wT[:, W_IH + 1, :], upT[s][:, :], start=False, stop=True).then_inc(A["i_z"], 1)
                    if prev and it == 0:
                        f_logits(i - 1)
                    if nxt and it == 2:
                        ctx_V(i + 1)
                    if not nxt and it == 0:
                        ranks(0, ROUTED)
                        pe.wait_ge(F["tot"], 1)

            def ranks(c, hi):
                pe.wait_ge(F["pos"], c + 1)
                for k, m in enumerate((before, ones_bf)):
                    last = pe.matmul(bank[k][:, 0:E * hi].rearrange("p (e b) -> p e b", e=E), m[:, :], gmb[:, :, 0:hi], start=True, stop=True)
                last.then_inc(F["posr"], 1)

            ctx_turn(0)
            ctx_G(0)
            ctx_V(0)
            slot_turn(0, prev=False)
            with pe.Fori(1, NG - 1) as i:
                slot_turn(i)
            slot_turn(NG - 1, nxt=False)
            f_T(NG - 1)
            f_T2(NG - 1, occ(NG - 1, ITERS - 1, 0))
            f_logits(NG - 1)

            def rows_T(i, s):
                pe.wait_ge(F[f"in{s}"], 16 * (i + 1))
                for c in range(CT):
                    last = pe.transpose(bank[c // 4][:, (c % 4) * D:(c % 4 + 1) * D], xe[s][:, c, :], ident[:, :])
                last.then_inc(F["T"], 1)

            def expert(l, i, s, last_one=False):
                f = F
                n = occ1(i, s) + l * E
                if l == 0:
                    pe.wait_ge(f["Tev"], n)
                pe.wait_ge(f[f"w{s}"], 32 * (i + 1) + l * (32 * E // SLOTS))
                for c in range(HC):
                    if c >= 2:
                        pe.wait_ge(f["hevD"], n * HC - (HC - 1 - (c - 2)))
                        pe.wait_ge(f["hevA"], n * HC - (HC - 1 - (c - 2)))
                    for j in range(2):
                        if l:
                            x = xe1T[:, bass.ds(i * SLOTS + s, 1), j * (B // 2):(j + 1) * (B // 2), :].rearrange("p a b r -> p (a b r)")
                        else:
                            x = xeT[s][:, j * (CAP0 // 2):(j + 1) * (CAP0 // 2)]
                        last = pe.matmul(bank[2 + 2 * (c % 2) + j][:, 0:CAP0 // 2], w1[s][:, c * 128:(c + 1) * 128],
                                         x, start=True, stop=True)
                    last.then_inc(f["h"], 1)
                if l == 0 and not last_one:
                    rows_T(i + (s + 1) // SLOTS, (s + 1) % SLOTS)
                pe.wait_ge(f["hevD"], n * HC - 1)
                pe.wait_ge(f["hevA"], n * HC - 1)
                for r in range(CT):
                    for c in range(HC):
                        if r == 0 and c == HC - 1:
                            pe.wait_ge(f["hevD"], n * HC)
                            pe.wait_ge(f["hevA"], n * HC)
                        last = pe.matmul(bank[6 + r // 4][:, (r % 4) * D:(r % 4 + 1) * D], hT[s][:, c, r * 128:(r + 1) * 128], w2[s][:, c, :],
                                         start=(c == 0), stop=(c == HC - 1))
                last.then_inc(f["y"], 1)

            def experts_pe(l):
                if l == 0:
                    rows_T(0, 0)
                with pe.Fori(0, E // SLOTS - 1) as i:
                    for s in range(SLOTS):
                        expert(l, i, s)
                for s in range(SLOTS):
                    expert(l, E // SLOTS - 1, s, last_one=(s == SLOTS - 1))

            ranks(1, B)
            pe.wait_ge(F["tot"], 2)
            experts_pe(0)

            def scores(i, s, g):
                b, v, turn = batch_of(i, s, 0)
                if inside(b):
                    if g == 0:
                        pe.wait_ge(C["kb"], b + 1)
                        pe.wait_ge(C["mb"], b + 1)
                    if not isinstance(b, int) or b:
                        pe.wait_ge(C["ex"], b * 4 + g - 3)
                    pe.matmul(bank[g][:, 0:HG * M], qT[v][32 * g:32 * g + 32, :],
                              kb[v][32 * g:32 * g + 32, :, :].rearrange("p j m -> p (j m)"), start=True, stop=False)
                    pe.matmul(bank[g][:, 0:HG * M], ident_bf[:, :], mb[v][:, :].unsqueeze(1).to_broadcast([128, HG, M]),
                              start=False, stop=True).then_inc(C["s"], 1)

            def turned(i, s, g):
                b, v, turn = batch_of(i, s, -1)
                if inside(b):
                    pe.wait_ge(C["norm"], b * 4 + g + 1)
                    for h in range(HG):
                        last = pe.transpose(bank[4 + g % 2][0:M, h * S:(h + 1) * S], pr[v][:, HG * g + h, :], ident[:, :])
                    last.then_inc(C["pt"], 1)

            def products(i, s, k, g):
                b, v, turn = batch_of(i, s, k)
                if inside(b):
                    if g == 0 and (not isinstance(b, int) or b):
                        pe.wait_ge(C["oTev"], b)
                    pe.wait_ge(C["pev"], b * 4 + g + 1)
                    for h in range(HG * g, HG * g + HG):
                        last = pe.matmul(bank[7][:, 0:S], va[v][:, h, :], pT[v][:, h * S:(h + 1) * S],
                                         start=(h == 0), stop=(h == H - 1))
                    if g == 3:
                        last.then_inc(C["pv"], 1)

            def step(i, s):
                b0, v0, turn0 = batch_of(i, s, 0)
                b1, v1, turn1 = batch_of(i, s, 1)
                b2, v2, turn2 = batch_of(i, s, -2)
                b3, v3, turn3 = batch_of(i, s, -3)
                scores(i, s, 0)
                products(i, s, -2, 3)
                turned(i, s, 0)
                if inside(b3):
                    pe.wait_ge(C["ln2"], b3 + 1)
                    pe.transpose(bank[6][:, 0:S], hb[v3][:, :], ident[:, :]).then_inc(C["T2"], 1)
                scores(i, s, 1)
                turned(i, s, 1)
                if inside(b3):
                    pe.wait_ge(C["T2ev"], b3 + 1)
                    pe.matmul(bank[6][:, 0:E], hbT[v3][:, :], wr[1][:, :], start=True, stop=True).then_inc(C["lg"], 1)
                products(i, s, -1, 0)
                if inside(b1):
                    if inside(b3):
                        pe.wait_ge(C["lgev"], b3 + 1)
                    pe.wait_ge(C[f"in{v1}"], 32 * (turn1 + 1))
                    pe.wait_ge(C["ln"], b1 + 1)
                    pe.transpose(bank[6][:, 0:M], ca[v1][:, :], ident[0:M, 0:M])
                    pe.transpose(bank[6][:, D:2 * D], ha[v1][:, :], ident[:, :]).then_inc(C["T"], 1)
                scores(i, s, 2)
                turned(i, s, 2)
                if inside(b1):
                    pe.wait_ge(C["Tev"], b1 + 1)
                    pe.matmul(bank[6][:, 0:M], wT[:, W_KK, :], caT[v1][:, :], start=True, stop=True)
                    last = pe.matmul(bank[6][:, D:2 * D], wT[:, W_QQ, :], haT[v1][:, :], start=True, stop=True)
                if inside(b0):
                    if not inside(b1):
                        pe.wait_ge(C["lgev"], b3 + 1)
                    last = pe.matmul(bank[6][0:M, 2 * D:3 * D], caT[v0][:, :], wT[:, W_VV, :], start=True, stop=True)
                if inside(b1) or inside(b0):
                    last.then_inc(C["kqv"], 1)
                products(i, s, -1, 1)
                scores(i, s, 3)
                turned(i, s, 3)
                if inside(b2):
                    if inside(b1) or inside(b0):
                        pe.wait_ge(C["kqev"], b1 + 1)
                    elif inside(b3):
                        pe.wait_ge(C["lgev"], b3 + 1)
                    pe.wait_ge(C["oTev"], b2 + 1)
                    pe.matmul(bank[6][:, 0:D], oT[v2][:, :], wT[:, W_OO, :], start=True, stop=True).then_inc(C["w"], 1)
                products(i, s, -1, 2)
            pipeline(pe, step)
            ranks(2, B)

            def rows_pe(i, s, first=False):
                n = occ1(i, s)
                pe.wait_ge(L["sel"], n)
                pe.wait_ge(L["hg"], n)
                if not first:
                    pe.wait_ge(L["dev"], n - SLOTS)
                for j in range(G):
                    last = pe.matmul(bank[2 + 2 * s + j // 2][:, j % 2 * ROWS1:(j % 2 + 1) * ROWS1], hg[s][:, j, :], sel[s][:, j, :],
                                     start=True, stop=True)
                last.then_inc(L["disp"], 1)
            for s in range(SLOTS):
                rows_pe(0, s, True)
            with pe.Fori(1, NG) as i:
                for s in range(SLOTS):
                    rows_pe(i, s)
            pe.wait_ge(L["dev"], NG * SLOTS)
            experts_pe(1)

            def step(i, s):
                g, v, turn = batch_of(i, s, 1)
                if group_inside(g):
                    pe.wait_ge(L["c"], g + 1)
                    for k in range(2):
                        for j in range(G):
                            last = pe.transpose(bank[2 * v + k][0:HR, j * S:(j + 1) * S], cm[v][:, j, k * HR:(k + 1) * HR], ident[:, :])
                    last.then_inc(L["ct"], 1)
                g, v, turn = batch_of(i, s, 0)
                if group_inside(g):
                    if isinstance(g, int) and g == 0:
                        pe.wait_ge(L["yb"], 16 * E)
                    if not isinstance(g, int) or g >= SLOTS:
                        pe.wait_ge(Z["b"], g - 1)
                    pe.wait_ge(L["ctev"], g + 1)
                    for j in range(G):
                        for k in range(2):
                            last = pe.matmul(bank[4 + v][:, j * D:(j + 1) * D], cmT[v][:, k, j, :],
                                             yb[:, k, bass.ds(g * G + j, 1), :].rearrange("p a d -> p (a d)"),
                                             start=(k == 0), stop=(k == 1))
                    last.then_inc(L["y"], 1)
            pipeline(pe, step, -1, SLOTS, B // G - SLOTS, B // G - 1)

        @block.vector
        def _(dve):
            dve.wait_ge(w_in, 16 * NWD)
            dve.tensor_tensor(gb2[:, :], gbi[:, 0:2], gbh[:, 0:2], ALU.add).then_inc(setup_m, 1)
            dve.wait_ge(setup_m, 1)
            dve.tensor_scalar(gb2[:, :], gb2[:, :], 0.5, None, ALU.mult).then_inc(setup_m, 1)
            dve.tensor_scalar(gbn[:, :], gbh[:, 2:3], 0.5, None, ALU.mult).then_inc(setup_m, 1)
            dve.tensor_scalar(wslot[:, :], wslot[:, :], float(D) ** -0.5, None, ALU.mult).then_inc(setup_m, 1)
            dve.wait_ge(setup_m, 4)
            dve.wait_ge(k_pool, K_POOL)
            dve.tensor_reduce(band[:, :], ident[:, :].rearrange("p (c j d) -> p j c d", j=HG, d=DK), AX.XY, ALU.add).then_inc(setup_m, 1)

            def kept_of(i, s, b):
                return xs[:, bass.ds((i * SLOTS + s) * G + b, 1), :].rearrange("p a d -> p (a d)")

            def ln(i, s, src_n, src_v, st_n, mv_n):
                n = occ1(i, s)
                dve.to_reg(n)
                dve.to_reg(src_v)
                dve.wait_ge(k_pool, K_POOL)
                dve.wait_ge(A[src_n], src_v)
                for b in range(G):
                    last = dve.bn_stats(st[s][:, 6 * b:6 * b + 6], kept_of(i, s, b))
                last.then_inc(A[st_n], 1)
                dve.wait_ge(k_pool, K_POOL)
                dve.wait_ge(A[st_n], n)
                for b in range(G):
                    last = dve.bn_aggr(mv[s][:, b, :], st[s][:, 6 * b:6 * b + 6])
                last.then_inc(A[mv_n], 1)

            def ln_out(i, s, rr_n, ln_n, mv_n):
                n = occ1(i, s)
                dve.wait_ge(A[mv_n], n)
                dve.wait_ge(A[rr_n], n)
                for b in range(G):
                    last = dve.tensor_scalar(xh[s][:, b, :], kept_of(i, s, b), mv[s][:, b, 0:1], lrs[s][:, b:b + 1],
                                             ALU.subtract, ALU.mult)
                last.then_inc(A[ln_n], 1)

            def x_stats(i):
                for s in range(SLOTS):
                    ln(i, s, f"x_in{s}", 16 * (i + 1), "x_st", "x_mv")

            def x_out(i):
                for s in range(SLOTS):
                    ln_out(i, s, "x_rr", "x_ln", "x_mv")

            def ctx_keepG(i):
                for s in range(SLOTS):
                    dve.wait_ge(A["ctx_G"], occ1(i, s))
                    dve.tensor_scalar(g_s[s][:, :, :].rearrange("p b m -> p (b m)"), bank[4 * s + 3][:, 0:G * M], wslot[:, 0:1], None,
                                      ALU.mult).then_inc(A["ctx_Gev"], 1)

            def ctx_keepV(i):
                for s in range(SLOTS):
                    dve.wait_ge(A["ctx_rr"], occ1(i, s))
                    dve.wait_ge(A["ctx_V"], occ1(i, s))
                    for b in range(G):
                        last = dve.tensor_scalar(v_s[s][:, b, 0:D], bank[4 * s + 3][0:M, b * D:(b + 1) * D], rc[s][0:M, b:b + 1], None, ALU.mult)
                    last.then_inc(A["ctx_Vev"], 1)

            def f_add(i):
                for s in range(SLOTS):
                    n = occ1(i, s)
                    dve.wait_ge(A["f_T"], n)
                    x = xs[:, bass.ds((i * SLOTS + s) * G, G), :]
                    dve.tensor_tensor(x, bank[4 * s][:, :].rearrange("p (b d) -> p b d", b=G), x, ALU.add).then_inc(A["f_x"], 1)
                    ln(i, s, "f_x", n, "f_st", "f_mv")

            def f_out(i):
                for s in range(SLOTS):
                    ln_out(i, s, "f_rr", "f_ln", "f_mv")

            def f_keep_logits(i):
                for s in range(SLOTS):
                    dve.wait_ge(A["f_lg"], occ1(i, s))
                    dve.tensor_tensor(lg[:, bass.ds((i * SLOTS + s) * G, G), :],
                                      bank[4 * s + 3][:, 0:G * E].rearrange("p (b e) -> p b e", b=G),
                                      br[0][:, :].unsqueeze(1).to_broadcast([128, G, E]), ALU.add).then_inc(A["f_lgev"], 1)

            def slot_turn(i, prev=True, nxt=True):
                if prev:
                    f_add(i - 1)
                for it in range(ITERS):
                    for s in range(SLOTS):
                        n = occ(i, it, s)
                        b0 = bank[4 * s]
                        dve.wait_ge(A["i_rr"], n)
                        for b in range(G):
                            last = dve.tensor_scalar(tok[s][:, b, :], b0[:, b * D:(b + 1) * D], rs[s][:, b:b + 1], None, ALU.mult)
                        last.then_inc(A["i_sn"], 1)
                    if prev and it == 0:
                        for s in range(SLOTS):
                            dve.wait_ge(A["x_T"], occ1(i, s))
                        f_out(i - 1)
                    if nxt and it == 1:
                        x_stats(i + 1)
                    for s in range(SLOTS):
                        n = occ(i, it, s)
                        b1 = bank[4 * s + 1]
                        dve.wait_ge(A["i_sc"], n)
                        dve.tensor_reduce(mx[s][:, :], b1[0:M, :].rearrange("p (b k) -> p b k", b=G), AX.X, ALU.max).then_inc(A["i_mx"], 1)
                        dve.wait_ge(A["i_mx"], n)
                        dve.scalar_tensor_tensor(out=nb[s][:, :], in0=mx[s][:, :], scalar=-1.0, in1=rc[s][0:M, :],
                                                 op0=ALU.mult, op1=ALU.mult).then_inc(A["i_nb"], 1)
                    for s in range(SLOTS):
                        n = occ(i, it, s)
                        dve.wait_ge(A["i_ex"], n)
                        dve.reciprocal(rm[s][:, :], sm[s][:, :]).then_inc(A["i_rm"], 1)
                        dve.wait_ge(A["i_rm"], n)
                        if it == 0:
                            dve.wait_ge(A["ctx_Vev"], occ1(i, s))
                        for b in range(G):
                            last = dve.tensor_scalar(vr_s[s][:, b, :], v_s[s][:, b, :], rm[s][:, b:b + 1], None, ALU.mult)
                        last.then_inc(A["i_vr"], 1)
                    if nxt and it == 1:
                        for s in range(SLOTS):
                            dve.wait_ge(A["x_T"], occ1(i, s))
                            if prev:
                                dve.wait_ge(A["f_T2"], occ1(i - 1, s))
                                dve.wait_ge(A["f_keep"], occ1(i - 1, s))
                        x_out(i + 1)
                    for s in range(SLOTS):
                        n = occ(i, it, s)
                        b1, b2 = bank[4 * s + 1], bank[4 * s + 2]
                        dve.wait_ge(A["i_u"], n)
                        dve.tensor_scalar(cs[s][:, G - 1:G], b1[:, D:D + 1], EPS_RMS, None, ALU.add)
                        dve.tensor_scalar(cs[s][:, 0:G - 1].unsqueeze(2), b2[:, 0:(G - 1) * (D + 1)].rearrange("p (b c) -> p b c", b=G - 1)[:, :, D:D + 1],
                                          EPS_RMS, None, ALU.add).then_inc(A["i_cs"], 1)
                        dve.wait_ge(A["i_cs"], n)
                        dve.reciprocal(ci[s][:, :], cs[s][:, :]).then_inc(A["i_ci"], 1)
                        dve.wait_ge(A["i_ci"], n)
                        for b in range(G):
                            u = b2[:, b * (D + 1):b * (D + 1) + D] if b < G - 1 else b1[:, 0:D]
                            last = dve.tensor_scalar(tok[s][:, b, :], u, ci[s][:, b:b + 1], None, ALU.mult)
                        last.then_inc(A["i_ut"], 1)
                    if nxt and it == 2:
                        ctx_keepG(i + 1)
                    own_z = not nxt and it > 0

                    def z(s):
                        dve.wait_ge(A["i_tz"], occ(i, it, s))
                        dve.tensor_scalar(tz[s][:, :], tz[s][:, :], 0.5, 0.5, ALU.mult, ALU.add).then_inc(A["i_z2"], 1)

                    def z_by_s(s):
                        dve.wait_ge(A["i_z2"], occ(i, it, s))
                        dve.tensor_tensor(uu[s][:, :], sT[s][:, :], tz[s][:, :], ALU.mult).then_inc(A["i_a"], 1)

                    def new_part(s):
                        dve.wait_ge(A["i_n"], occ(i, it, s))
                        dve.wait_ge(A["i_z2"], occ(i, it, s))
                        dve.scalar_tensor_tensor(out=nn[s][:, :], in0=tz[s][:, :], scalar=-1.0, in1=nn[s][:, :],
                                                 op0=ALU.add, op1=ALU.mult).then_inc(A["i_p"], 1)

                    for s in range(SLOTS):
                        n = occ(i, it, s)
                        b2 = bank[4 * s + 2]
                        dve.wait_ge(A["i_tr"], n)
                        dve.wait_ge(A["i_hh"], n)
                        dve.scalar_tensor_tensor(out=qn[s][:, :], in0=tr[s][:, :], scalar=1.0, in1=hh[s][:, :],
                                                 op0=ALU.add, op1=ALU.mult).then_inc(A["i_q"], 1)
                        dve.wait_ge(A["i_q"], n)
                        dve.wait_ge(A["i_xn"], n)
                        dve.tensor_tensor(qn[s][:, :], b2[:, :], qn[s][:, :], ALU.add).then_inc(A["i_q2"], 1)
                        if s == 0:
                            if own_z:
                                z(s)
                            new_part(s)
                    if prev and it == 0:
                        f_keep_logits(i - 1)
                    for s in range(SLOTS):
                        n = occ(i, it, s)
                        if s > 0:
                            if own_z:
                                z(s)
                                z_by_s(s)
                            new_part(s)
                        if own_z and s == 0:
                            z_by_s(s)
                        dve.wait_ge(A["i_p"], n)
                        dve.wait_ge(A["i_a"], n)
                        dve.wait_ge(A["i_z"], n)
                        dve.tensor_tensor(sT[s][:, :], uu[s][:, :], nn[s][:, :], ALU.subtract).then_inc(A["i_s"], 1)
                    if nxt and it == 2:
                        ctx_keepV(i + 1)
                    if not nxt and it == 0:
                        route(0, 0, 0, ROUTED, ROUTED // G)

            def route(c, l, lo, hi, logits_n):
                f = F
                cap = float(CAP0 if l == 0 else CAP1)
                steps = route_steps
                n = hi - lo

                def step(ins):
                    steps[0] += 1
                    ins.then_inc(f["dd"], 1)
                    dve.wait_ge(f["dd"], steps[0])

                def wide(a):
                    return a[:, lo:hi].unsqueeze(2).to_broadcast([128, n, E])

                def cut(a):
                    return a[:, lo:hi, :]

                def by_batch(a):
                    return a[:, :, lo:hi].rearrange("p e b -> p b e")

                def flat(a):
                    return a[:, :, :].rearrange("p e b -> p (e b)")

                def ex(a, first=lo):
                    return a[:, :, first:hi]
                lgc, gtc, gec, gwc = cut(lg), cut(gt), cut(ge), cut(gw)
                gxc, g1c = gx[:, lo:hi], g1[:, lo:hi]
                dve.wait_ge((A["f_lgev"] if l == 0 else C["lgev"]), logits_n)
                step(dve.tensor_reduce(gxc, lgc, AX.X, ALU.max))
                dve.tensor_tensor(gtc, lgc, wide(gx), ALU.subtract).then_inc(f["d"], 1)
                for k in range(2):
                    step(dve.tensor_tensor(gwc, lgc, wide(gx), ALU.is_equal))
                    step(dve.tensor_tensor(gwc, gwc, cut(eight), ALU.mult))
                    step(dve.tensor_reduce(g1c, gwc, AX.X, ALU.max))
                    step(dve.tensor_tensor(by_batch(gm[k]), gwc, wide(g1), ALU.is_equal))
                    if k == 0:
                        step(dve.scalar_tensor_tensor(out=lgc, in0=by_batch(gm[0]), scalar=-BIG, in1=lgc,
                                                      op0=ALU.mult, op1=ALU.add))
                        step(dve.tensor_reduce(gxc, lgc, AX.X, ALU.max))
                dve.wait_ge(f["ex"], c + 1)
                step(dve.tensor_reduce(gxc, gec, AX.X, ALU.add))
                step(dve.reciprocal(g1c, gxc))
                step(dve.tensor_tensor(gec, gec, wide(g1), ALU.mult))
                if l == 0:
                    step(dve.scalar_tensor_tensor(out=by_batch(gv), in0=gec, scalar=0.0, in1=by_batch(gm[1]),
                                                  op0=ALU.is_gt, op1=ALU.mult))
                    dve.tensor_tensor(ex(gmb), ex(gm[0]), ex(gv), ALU.add).then_inc(f["pos"], 1)
                else:
                    dve.tensor_tensor(ex(gmb), ex(gm[0]), ex(gm[1]), ALU.add).then_inc(f["pos"], 1)
                dve.wait_ge(f["posr"], c + 1)
                pos = bank[0][:, 0:E * hi].rearrange("p (e b) -> p e b", e=E)
                tot = bank[1][:, 0:E * hi].rearrange("p (e b) -> p e b", e=E)
                if l == 0:
                    step(dve.tensor_copy(ex(gv, 0), tot))
                    step(dve.tensor_tensor_scan(flat(gp), flat(chain), flat(gv), 0.0, ALU.mult, ALU.add))
                    step(dve.tensor_tensor(ex(gp), ex(gp), ex(gv), ALU.subtract))
                    step(dve.tensor_tensor(ex(gp), pos[:, :, lo:hi], ex(gp), ALU.add))
                else:
                    step(dve.tensor_copy(ex(gp), pos))
                dve.tensor_scalar(ex(gv), ex(gp), cap, float(2 * ROWS), ALU.is_ge, ALU.mult).then_inc(f["tot"], 1)
                step(dve.tensor_tensor(ex(gp), ex(gp), ex(base[l]), ALU.add))
                step(dve.tensor_tensor(ex(gp), ex(gp), ex(gv), ALU.add))
                for k in range(2):
                    s = sl[k][:, lo:hi]
                    step(dve.tensor_tensor(ex(gv), ex(gp), ex(gm[k]), ALU.mult))
                    step(dve.tensor_reduce(s, by_batch(gv), AX.X, ALU.add))
                    step(dve.tensor_tensor(gwc, gec, by_batch(gm[k]), ALU.mult))
                    step(dve.tensor_reduce(g1c, gwc, AX.X, ALU.add))
                    if l == 0:
                        step(dve.tensor_scalar(gxc, g1c, 0.0, float(2 * ROWS), ALU.is_le, ALU.mult))
                        step(dve.tensor_tensor(s, s, gxc, ALU.add))
                        step(dve.tensor_copy(slot_i[:, k, lo:hi], s))
                    last = dve.scalar_tensor_tensor(out=gate[:, k, lo:hi], in0=s, scalar=float(ROWS), in1=g1c,
                                                    op0=ALU.is_lt, op1=ALU.mult)
                    if k == 0:
                        step(last)
                last.then_inc(f["slot"], 1)

            def experts_dve(l):
                f = F
                with dve.Fori(0, E // SLOTS) as i:
                    for s in range(SLOTS):
                        n = occ1(i, s) + l * E
                        for c in range(HC):
                            dve.wait_ge(f["h"], n * HC - (HC - 1 - c))
                            if l:
                                last = dve.tensor_scalar(hT[s][:, c, 0:CAP0 // 2], bank[2 + 2 * (c % 2)][:, 0:CAP0 // 2],
                                                         b1T[:, bass.ds((i * SLOTS + s) * HC + c, 1)], 0.0, ALU.add, ALU.max)
                            else:
                                last = dve.tensor_scalar(hT[s][:, c, 0:CAP0 // 2], bank[2 + 2 * (c % 2)][:, 0:CAP0 // 2],
                                                         0.0, None, ALU.max)
                            last.then_inc(f["hevD"], 1)
                        dve.wait_ge(f["y"], n)
                        y7 = ye[:, bass.ds((i * SLOTS + s) * CT + HC, 1), :]
                        if l:
                            bias = b2b[:, bass.ds(i * SLOTS + s, 1), :]
                            dve.tensor_tensor(ye[:, bass.ds((i * SLOTS + s) * CT, HC), :], bank[6][:, :].rearrange("p (c d) -> p c d", c=HC),
                                              bias.to_broadcast([128, HC, D]), ALU.add)
                            last = dve.tensor_tensor(y7, bank[7][:, 0:D].unsqueeze(1), bias, ALU.add)
                        else:
                            last = dve.tensor_copy(y7, bank[7][:, 0:D].unsqueeze(1))
                        last.then_inc(f["yevD"], 1)

            def scaled(k, b, v, x):
                return dict(in0=yg[v][:, k, :], scalar=gate[:, k, bass.ds(b, 1)], in1=x, op0=ALU.mult, op1=ALU.add)

            def kept(b):
                return xs[:, bass.ds(b, 1), :].rearrange("p a d -> p (a d)")

            def stats(b, st, mv, s_x, s_st, s_mv):
                dve.to_reg(b + 1)
                dve.wait_ge(k_pool, K_POOL)
                dve.wait_ge(C[s_x], b + 1)
                dve.bn_stats(st[:, :], kept(b)).then_inc(C[s_st], 1)
                dve.wait_ge(k_pool, K_POOL)
                dve.wait_ge(C[s_st], b + 1)
                dve.bn_aggr(mv[:, :], st[:, :]).then_inc(C[s_mv], 1)

            def maxima(i, s, g):
                b, v, turn = batch_of(i, s, 0)
                if inside(b):
                    n = b * 4 + g + 1
                    hd = slice(HG * g, HG * g + HG)
                    dve.wait_ge(C["s"], n)
                    dve.tensor_reduce(mxa[v][:, hd], bank[g][:, 0:HG * M].rearrange("p (h m) -> p h m", h=HG),
                                      AX.X, ALU.max).then_inc(C["mx"], 1)
                    dve.wait_ge(C["mx"], n)
                    dve.tensor_scalar(nm[v][:, hd], mxa[v][:, hd], -BIG / 10, -1.0, ALU.max, ALU.mult).then_inc(C["nm"], 1)

            def normalised(i, s, k, g):
                b, v, turn = batch_of(i, s, k)
                if inside(b):
                    n = b * 4 + g + 1
                    hd = slice(HG * g, HG * g + HG)
                    dve.wait_ge(C["ex"], n)
                    dve.tensor_scalar(dg[v][:, hd], den[v][:, hd], 1.0e-30, None, ALU.max).then_inc(C["den"], 1)
                    dve.wait_ge(C["den"], n)
                    dve.reciprocal(rden[v][:, hd], dg[v][:, hd]).then_inc(C["rd"], 1)
                    dve.wait_ge(C["rd"], n)
                    dve.tensor_tensor(pr[v][:, hd, :], pr[v][:, hd, :], rden[v][:, hd].unsqueeze(2).to_broadcast([128, HG, M]),
                                      ALU.mult).then_inc(C["norm"], 1)

            def step(i, s):
                maxima(i, s, 0)
                b, v, turn = batch_of(i, s, -3)
                if inside(b):
                    dve.wait_ge(C["mv2"], b + 1)
                    dve.wait_ge(C["rr2"], b + 1)
                    dve.tensor_scalar(hb[v][:, :], kept(b), mvb[v][:, 0:1], rsb[v][:, :],
                                      ALU.subtract, ALU.mult).then_inc(C["ln2"], 1)
                normalised(i, s, -1, 3)
                maxima(i, s, 1)
                if inside(b):
                    dve.wait_ge(C["lg"], b + 1)
                    dve.tensor_tensor(lg[:, bass.ds(b, 1), :], bank[6][:, 0:E].unsqueeze(1),
                                      br[1][:, :].unsqueeze(1), ALU.add).then_inc(C["lgev"], 1)
                normalised(i, s, 0, 0)
                b, v, turn = batch_of(i, s, 1)
                if inside(b):
                    dve.wait_ge(C[f"in{v}"], 32 * (turn + 1))
                    dve.tensor_scalar(mb[v][:, :], mk[v][:, :], 0.0, -BIG, ALU.is_equal, ALU.mult).then_inc(C["mb"], 1)
                b2, v2, turn2 = batch_of(i, s, 2)
                if inside(b2):
                    dve.wait_ge(C[f"g{v2}"], 32 * (turn2 + 1))
                    dve.scalar_tensor_tensor(out=kept(b2), **scaled(0, b2, v2, kept(b2))).then_inc(C["x1"], 1)
                    dve.wait_ge(C["x1"], b2 + 1)
                    dve.scalar_tensor_tensor(out=kept(b2), **scaled(1, b2, v2, kept(b2))).then_inc(C["x2"], 1)
                    stats(b2, sta[v2], mva[v2], "x2", "st", "mv")
                maxima(i, s, 2)
                normalised(i, s, 0, 1)
                maxima(i, s, 3)
                if inside(b):
                    dve.wait_ge(C["kqev"], b + 1)
                    dve.tensor_tensor(kb[v][:, :, :], kT[v][:, :].unsqueeze(1).to_broadcast([128, HG, M]),
                                      band[:, :].unsqueeze(2).to_broadcast([128, HG, M]), ALU.mult).then_inc(C["kb"], 1)
                b, v, turn = batch_of(i, s, -2)
                if inside(b):
                    dve.wait_ge(C["w"], b + 1)
                    dve.tensor_tensor(kept(b), bank[6][:, 0:D], kept(b), ALU.add).then_inc(C["x3"], 1)
                    stats(b, stb[v], mvb[v], "x3", "st2", "mv2")
                normalised(i, s, 0, 2)
                if inside(b2):
                    dve.wait_ge(C["mv"], b2 + 1)
                    dve.wait_ge(C["rr"], b2 + 1)
                    dve.tensor_scalar(ha[v2][:, :], kept(b2), mva[v2][:, 0:1], rsa[v2][:, :],
                                      ALU.subtract, ALU.mult).then_inc(C["ln"], 1)

            x_stats(0)
            x_out(0)
            ctx_keepG(0)
            ctx_keepV(0)
            slot_turn(0, prev=False)
            with dve.Fori(1, NG - 1) as i:
                slot_turn(i)
            slot_turn(NG - 1, nxt=False)
            f_add(NG - 1)
            f_out(NG - 1)
            f_keep_logits(NG - 1)
            route(1, 0, ROUTED, B, B // G)
            experts_dve(0)
            pipeline(dve, step)
            route(2, 1, 0, B, B)

            def rows_dve(i, s, first=False):
                n = occ1(i, s)
                if not first:
                    dve.wait_ge(L["disp"], n - SLOTS)
                for j in range(G):
                    col = bass.ds((i * SLOTS + s) * G + j, 1)
                    last = dve.tensor_scalar(sel[s][:, j, :], iota_row[:, :], sl[0][:, col], None, ALU.is_equal)
                last.then_inc(L["sel0"], 1)
                dve.wait_ge(L["sel0"], n)
                for j in range(G):
                    col = bass.ds((i * SLOTS + s) * G + j, 1)
                    last = dve.scalar_tensor_tensor(out=sel[s][:, j, :], in0=iota_row[:, :], scalar=sl[1][:, col],
                                                    in1=sel[s][:, j, :], op0=ALU.is_equal, op1=ALU.add)
                last.then_inc(L["sel"], 1)
            dve.wait_ge(C["keep"], B)
            for s in range(SLOTS):
                rows_dve(0, s, True)
            with dve.Fori(1, NG) as i:
                for s in range(SLOTS):
                    rows_dve(i, s)
            dve.wait_ge(L["b2"], 16)
            experts_dve(1)

            def step(i, s):
                g, v, turn = batch_of(i, s, 2)
                if group_inside(g):
                    if not isinstance(g, int) or g >= SLOTS:
                        dve.wait_ge(L["ct"], g - 1)
                    for k, c in enumerate((cm, cn)):
                        for j in range(G):
                            col = bass.ds(g * G + j, 1)
                            last = dve.tensor_scalar(c[v][:, j, :], iota_row[:, :], sl[k][:, col], gate[:, k, col], ALU.is_equal, ALU.mult)
                    last.then_inc(L["cm"], 1)
                    dve.wait_ge(L["cm"], g + 1)
                    dve.tensor_tensor(cm[v][:, :, :], cm[v][:, :, :], cn[v][:, :, :], ALU.add).then_inc(L["c"], 1)
                g, v, turn = batch_of(i, s, 0)
                if group_inside(g):
                    dve.wait_ge(L["y"], g + 1)
                    x = xs[:, bass.ds(g * G, G), :]
                    dve.tensor_tensor(x, bank[4 + v][:, :].rearrange("p (b d) -> p b d", b=G), x, ALU.add).then_inc(Z["b"], 1)
            pipeline(dve, step, -2, SLOTS, B // G - SLOTS, B // G - 1)


_INS = ['x', 'ctx_1024', 'mask_Bx1xSxS2_ik0', 'L0_xattn_Wq', 'L0_xattn_Wk', 'L0_xattn_Wv', 'L0_xattn_gru_wih',
        'L0_xattn_gru_whh', 'L0_xattn_gru_bih', 'L0_xattn_gru_bhh', 'L0_xattn_slot_norm_w',
        'L0_xattn_input_norm_w', 'L0_ffn_W_router', 'L0_ffn_b_router', 'L0_ffn_experts_inter',
        'L0_ffn_experts_out', 'L1_xattn_W_Q', 'L1_xattn_W_K', 'L1_xattn_W_V', 'L1_xattn_W_O', 'L1_ffn_Wr',
        'L1_ffn_br', 'L1_ffn_W1', 'L1_ffn_b1', 'L1_ffn_W2', 'L1_ffn_b2']


def kernel(**inputs):
    import numpy as _np
    import concourse.bacc as _bacc
    from concourse import mybir as _mybir
    from concourse.bass_utils import run_bass_kernel_spmd as _run

    nc = _bacc.Bacc("TRN2", target_bir_lowering=False, num_devices=1)
    arrays, args = {}, {}
    for name in _INS:
        a = _np.ascontiguousarray(inputs[name])
        arrays[f"in_{name}_dram"] = a
        args[name] = nc.dram_tensor(f"in_{name}_dram", a.shape, _mybir.dt.from_np(a.dtype), kind="ExternalInput").ap()
    out = nc.dram_tensor("out_0_dram", (B, S, D), F32, kind="ExternalOutput").ap()
    build(nc, args, out)
    r = _run(nc, [arrays], core_ids=[0])
    return r.results[0]["out_0_dram"]
```
